# Optimizing a Trainium2 kernel written in Bass

```python
import numpy as np
import jax
import jax.numpy as jnp

def _softmax(x, axis=-1):
    return jax.nn.softmax(x, axis=axis)

def _gelu(x):
    return jax.nn.gelu(x, approximate=True)

def _silu(x):
    return jax.nn.silu(x)

def _sigmoid(x):
    return jax.nn.sigmoid(x)

def _layernorm(x, axis=-1, eps=1e-05):
    m = jnp.mean(x, axis=axis, keepdims=True)
    v = jnp.var(x, axis=axis, keepdims=True)
    return (x - m) / jnp.sqrt(v + eps)

def _scatter_add(tgt, idx, src, axis=0):
    return tgt.at[idx].add(src)

def _segment_sum(src, seg, n):
    return jax.ops.segment_sum(src, seg, n)
kernel_name = 'mk_gps_d1_gnn_r8_cb96ed'

def setup_inputs(seed: int=0):
    np.random.seed(seed)
    _w = jnp.asarray

    def _rec_inputs():
        import jax
        import jax.numpy as jnp
        _gk = jax.random.key(seed)
        x = -0.0003713 + 1 * jax.random.normal(jax.random.fold_in(_gk, 1), (6250, 256), jnp.float32)
        src = jax.random.randint(jax.random.fold_in(_gk, 2), (200000,), 0, 6250, jnp.int32)
        dst = jnp.minimum((6250 * jax.random.uniform(jax.random.fold_in(_gk, 3), (200000,)) ** 2.0).astype(jnp.int32), 49999)
        _o = jnp.argsort(dst, stable=True)
        src = src[_o]
        dst = dst[_o]
        return (x, src, dst)
    x, src, dst = _rec_inputs()

    def _L0_gnn_setup():
        import jax, jax.numpy as jnp
        import numpy as np
        N_NODES = 6250
        N_EDGES = 100000
        IN_DIM = 256
        OUT_DIM = 64
        HEADS = 4
        NEG_SLOPE = 0.2
        key = jax.random.key(seed)
        k1, k2, k3, k4, k5, k6 = jax.random.split(key, 6)
        x = jax.random.normal(k1, (N_NODES, IN_DIM), dtype=jnp.float32)
        edge_index = jax.random.randint(k2, (2, N_EDGES), 0, N_NODES, dtype=jnp.int64)
        scale = 1.0 / np.sqrt(IN_DIM)
        W = jax.random.normal(k3, (IN_DIM, HEADS * OUT_DIM), dtype=jnp.float32) * scale
        att_src = jax.random.normal(k4, (HEADS, OUT_DIM), dtype=jnp.float32) * scale
        att_dst = jax.random.normal(k5, (HEADS, OUT_DIM), dtype=jnp.float32) * scale
        bias = jnp.zeros((HEADS * OUT_DIM,), dtype=jnp.float32)
        return {'x': x, 'edge_index': edge_index, 'W': W, 'att_src': att_src, 'att_dst': att_dst, 'bias': bias}
    _L0_gnn_all = _L0_gnn_setup()
    _L0_gnn_in = {k: v for k, v in _L0_gnn_all.items() if k in ('W', 'att_src', 'att_dst', 'bias')}
    del _L0_gnn_all

    def _L0_mix_setup():
        import jax, jax.numpy as jnp
        import numpy as np
        MIDC = 256
        HEADS = 8
        HEADC = MIDC // HEADS
        EPS = 1e-05

        def _ln(x, gamma, beta):
            mu = jnp.mean(x, axis=-1, keepdims=True)
            var = jnp.var(x, axis=-1, keepdims=True)
            return (x - mu) * jax.lax.rsqrt(var + EPS) * gamma + beta
        key = jax.random.key(seed)
        ks = jax.random.split(key, 8)
        B, HW, C = (8, 512, MIDC)
        s = 1.0 / np.sqrt(C)
        return {'x': jax.random.normal(ks[0], (B, HW, C), jnp.float32), 'w_qkv': jax.random.normal(ks[1], (C, 3 * C), jnp.float32) * s, 'b_qkv': jnp.zeros((3 * C,), jnp.float32), 'kln_g': jnp.ones((HEADC,), jnp.float32), 'kln_b': jnp.zeros((HEADC,), jnp.float32), 'vln_g': jnp.ones((HEADC,), jnp.float32), 'vln_b': jnp.zeros((HEADC,), jnp.float32), 'w1': jax.random.normal(ks[2], (C, C), jnp.float32) * s, 'b1': jnp.zeros((C,), jnp.float32), 'w2': jax.random.normal(ks[3], (C, C), jnp.float32) * s, 'b2': jnp.zeros((C,), jnp.float32)}
    _L0_mix_all = _L0_mix_setup()
    _L0_mix_in = {k: v for k, v in _L0_mix_all.items() if k in ('w_qkv', 'b_qkv', 'kln_g', 'kln_b', 'vln_g', 'vln_b', 'w1', 'b1', 'w2', 'b2')}
    del _L0_mix_all

    def _L0_ffn_setup():
        import jax, jax.numpy as jnp
        import numpy as np
        E = 8
        K = 2
        D = 256
        H = 512
        DOUT = 256
        EPS = 1e-05
        key = jax.random.key(seed)
        ks = jax.random.split(key, 9)
        s = 0.02
        return {'x': jax.random.normal(ks[0], (4, 1024, D), jnp.float32), 'gamma': 1.0 + 0.05 * jax.random.normal(ks[1], (D,), jnp.float32), 'beta': 0.05 * jax.random.normal(ks[2], (D,), jnp.float32), 'Wr': 0.01 * jax.random.normal(ks[3], (D, E), jnp.float32), 'br': jnp.zeros((E,), jnp.float32), 'W1': s * jax.random.normal(ks[4], (E, D, H), jnp.float32), 'b1': s * jax.random.normal(ks[5], (E, H), jnp.float32), 'W2': s * jax.random.normal(ks[6], (E, H, DOUT), jnp.float32), 'b2': s * jax.random.normal(ks[7], (E, DOUT), jnp.float32)}
    _L0_ffn_all = _L0_ffn_setup()
    _L0_ffn_in = {k: v for k, v in _L0_ffn_all.items() if k in ('gamma', 'beta', 'Wr', 'br', 'W1', 'b1', 'W2', 'b2')}
    del _L0_ffn_all
    return {'x': x, 'src': src, 'dst': dst, 'L0_gnn_W': _L0_gnn_in['W'], 'L0_gnn_att_src': _L0_gnn_in['att_src'], 'L0_gnn_att_dst': _L0_gnn_in['att_dst'], 'L0_gnn_bias': _L0_gnn_in['bias'], 'L0_mix_w_qkv': _L0_mix_in['w_qkv'], 'L0_mix_b_qkv': _L0_mix_in['b_qkv'], 'L0_mix_kln_g': _L0_mix_in['kln_g'], 'L0_mix_kln_b': _L0_mix_in['kln_b'], 'L0_mix_vln_g': _L0_mix_in['vln_g'], 'L0_mix_vln_b': _L0_mix_in['vln_b'], 'L0_mix_w1': _L0_mix_in['w1'], 'L0_mix_b1': _L0_mix_in['b1'], 'L0_mix_w2': _L0_mix_in['w2'], 'L0_mix_b2': _L0_mix_in['b2'], 'L0_ffn_gamma': _L0_ffn_in['gamma'], 'L0_ffn_beta': _L0_ffn_in['beta'], 'L0_ffn_Wr': _L0_ffn_in['Wr'], 'L0_ffn_br': _L0_ffn_in['br'], 'L0_ffn_W1': _L0_ffn_in['W1'], 'L0_ffn_b1': _L0_ffn_in['b1'], 'L0_ffn_W2': _L0_ffn_in['W2'], 'L0_ffn_b2': _L0_ffn_in['b2']}

def reference(x, src, dst, L0_gnn_W, L0_gnn_att_src, L0_gnn_att_dst, L0_gnn_bias, L0_mix_w_qkv, L0_mix_b_qkv, L0_mix_kln_g, L0_mix_kln_b, L0_mix_vln_g, L0_mix_vln_b, L0_mix_w1, L0_mix_b1, L0_mix_w2, L0_mix_b2, L0_ffn_gamma, L0_ffn_beta, L0_ffn_Wr, L0_ffn_br, L0_ffn_W1, L0_ffn_b1, L0_ffn_W2, L0_ffn_b2):
    import jax
    import jax.numpy as jnp

    def _L0_gnn_ref(x, edge_index, W, att_src, att_dst, bias):
        import jax, jax.numpy as jnp
        import numpy as np
        N_NODES = 6250
        N_EDGES = 100000
        IN_DIM = 256
        OUT_DIM = 64
        HEADS = 4
        NEG_SLOPE = 0.2
        N = x.shape[0]
        H, C = att_src.shape
        loop = jnp.arange(N, dtype=edge_index.dtype)
        src = jnp.concatenate([edge_index[0], loop])
        dst = jnp.concatenate([edge_index[1], loop])
        h = (x @ W).reshape(N, H, C)
        a_src = jnp.einsum('nhc,hc->nh', h, att_src)
        a_dst = jnp.einsum('nhc,hc->nh', h, att_dst)
        e = jax.nn.leaky_relu(a_src[src] + a_dst[dst], negative_slope=NEG_SLOPE)
        m = jax.ops.segment_max(e, dst, num_segments=N)
        p = jnp.exp(e - m[dst])
        denom = jax.ops.segment_sum(p, dst, num_segments=N)
        alpha = p / (denom[dst] + 1e-16)
        out = jax.ops.segment_sum(alpha[:, :, None] * h[src], dst, num_segments=N)
        out = out.reshape(N, H * C) + bias
        return jax.nn.relu(out)

    def _L0_mix_ref(x, w_qkv, b_qkv, kln_g, kln_b, vln_g, vln_b, w1, b1, w2, b2):
        import jax, jax.numpy as jnp
        import numpy as np
        MIDC = 256
        HEADS = 8
        HEADC = MIDC // HEADS
        EPS = 1e-05

        def _ln(x, gamma, beta):
            mu = jnp.mean(x, axis=-1, keepdims=True)
            var = jnp.var(x, axis=-1, keepdims=True)
            return (x - mu) * jax.lax.rsqrt(var + EPS) * gamma + beta
        B, HW, C = x.shape
        bias = x
        qkv = (x @ w_qkv + b_qkv).reshape(B, HW, HEADS, 3 * HEADC)
        qkv = qkv.transpose(0, 2, 1, 3)
        q, k, v = jnp.split(qkv, 3, axis=-1)
        k = _ln(k, kln_g, kln_b)
        v = _ln(v, vln_g, vln_b)
        kv = jnp.einsum('bhnd,bhne->bhde', k, v) / HW
        out = jnp.einsum('bhnd,bhde->bhne', q, kv)
        out = out.transpose(0, 2, 1, 3).reshape(B, HW, C)
        ret = out + bias
        h = jax.nn.gelu(ret @ w1 + b1, approximate=False)
        return h @ w2 + b2 + bias

    def _L0_ffn_ref(x, gamma, beta, Wr, br, W1, b1, W2, b2):
        import jax, jax.numpy as jnp
        import numpy as np
        E = 8
        K = 2
        D = 256
        H = 512
        DOUT = 256
        EPS = 1e-05
        mu = jnp.mean(x, axis=-1, keepdims=True)
        var = jnp.mean(jnp.square(x - mu), axis=-1, keepdims=True)
        xn = (x - mu) * jax.lax.rsqrt(var + EPS) * gamma + beta
        logits = jnp.einsum('bsd,de->bse', xn, Wr) + br
        top_vals, top_idx = jax.lax.top_k(logits, K)
        w = jax.nn.softmax(top_vals, axis=-1)
        w_full = jnp.einsum('bsk,bske->bse', w, jax.nn.one_hot(top_idx, E, dtype=w.dtype))
        y = jnp.zeros(x.shape[:-1] + (DOUT,), x.dtype)
        for e in range(E):
            h = jax.nn.gelu(jnp.einsum('bsd,dh->bsh', xn, W1[e]) + b1[e], approximate=False)
            y_e = jnp.einsum('bsh,hd->bsd', h, W2[e]) + b2[e]
            y = y + y_e * w_full[..., e, None]
        return y
    edge_index = jnp.stack([src, dst])
    xn = _layernorm(x, axis=-1)
    x = x + _L0_gnn_ref(xn, edge_index, L0_gnn_W, L0_gnn_att_src, L0_gnn_att_dst, L0_gnn_bias) + _L0_mix_ref(xn[None], L0_mix_w_qkv, L0_mix_b_qkv, L0_mix_kln_g, L0_mix_kln_b, L0_mix_vln_g, L0_mix_vln_b, L0_mix_w1, L0_mix_b1, L0_mix_w2, L0_mix_b2)[0]
    x = x + _L0_ffn_ref(_layernorm(x, axis=-1)[None], L0_ffn_gamma, L0_ffn_beta, L0_ffn_Wr, L0_ffn_br, L0_ffn_W1, L0_ffn_b1, L0_ffn_W2, L0_ffn_b2)[0]
    return x

_drawn_inputs = setup_inputs


def setup_inputs(seed=0):
    import zlib

    import numpy as np

    out = dict(_drawn_inputs(seed))
    spreads = {'L0_gnn_bias': (0.0, 0.1),
     'L0_mix_b_qkv': (0.0, 0.1),
     'L0_mix_kln_g': (1.0, 0.6),
     'L0_mix_kln_b': (0.0, 0.436),
     'L0_mix_vln_g': (1.0, 0.582),
     'L0_mix_vln_b': (0.0, 0.392),
     'L0_mix_b1': (0.0, 0.1),
     'L0_mix_b2': (0.0, 0.1),
     'L0_ffn_br': (0.0, 0.304)}
    factors = {'L0_gnn_att_dst': 18.703,
     'L0_ffn_gamma': 8.0,
     'L0_ffn_beta': 8.0,
     'L0_ffn_Wr': 3.158,
     'L0_ffn_b1': 23.308,
     'L0_ffn_b2': 8.0}
    for name, (base, spread) in spreads.items():
        noise = np.random.default_rng([zlib.crc32(name.encode()), seed]).standard_normal(out[name].shape)
        drawn = base * np.exp(spread * noise) if base else spread * noise
        out[name] = jnp.asarray(drawn.astype(out[name].dtype))
    for name, factor in factors.items():
        out[name] = (out[name] * factor).astype(out[name].dtype)
    return out
```

```python
from contextlib import ExitStack

import concourse.bass as bass
from concourse import mybir

P = 128
F32 = mybir.dt.float32
I32 = mybir.dt.int32
U32 = mybir.dt.uint32
ALU = mybir.AluOpType
ACT = mybir.ActivationFunctionType
AX_X = mybir.AxisListType.X

EPS = 1e-5
SLOPE = 0.2
HEADS = 4
MH = 8
GB = 4
SB = GB * P
RING = 4


def gps_layer(nc, x, src, dst, gnn_W, att_src, att_dst, gnn_bias, w_qkv, b_qkv, kln_g, kln_b, vln_g, vln_b,
              w1, b1, w2, b2, gamma, beta, Wr, br, W1, fb1, W2, fb2, out):
    N, D = x.shape
    E = src.shape[0]
    NT = -(-N // P)
    TAIL = N - (NT - 1) * P
    FULL = NT - 1
    NSB = -(-E // SB)
    PAD = (NSB + 1) * SB - E
    NS = -(-(NSB + NT - 1) // RING) * RING
    NCH = -(-NS // P)
    C = D // HEADS
    HW_ = D + 2 * HEADS
    AW = D + HEADS
    KT = D // P
    HC = D // MH
    NE, _, H = W1.shape
    HK = H // P
    assert FULL % 2 == 0 and NSB <= 512 and NS // RING >= 3 and NCH <= NT

    node_table = nc.dram_tensor("node_table", (NT * P, HW_), F32).ap()
    edge_src = nc.dram_tensor("edge_src", ((NSB + 1) * SB,), I32).ap()
    edge_dst = nc.dram_tensor("edge_dst", ((NSB + 1) * SB,), I32).ap()
    step_table = nc.dram_tensor("step_table", (2, NCH * P), I32).ap()
    xnT_dram = nc.dram_tensor("xnT_dram", (NT, P, KT, P), F32).ap()
    base_dram = nc.dram_tensor("base_dram", (NT * P, D), F32).ap()
    mixed_dram = nc.dram_tensor("mixed_dram", (NT * P, D), F32).ap()

    with ExitStack() as ctx:
        def sem(name):
            return ctx.enter_context(nc.semaphore(name))

        def sb(name, shape, dt=F32, c=ctx):
            return c.enter_context(nc.sbuf_tensor(name, shape, dt))

        ident = sb("ident", [P, P])
        node_ids = sb("node_ids", [P, NT])
        iota8 = sb("iota8", [P, NE])
        ones_row = sb("ones_row", [1, P])
        eps_col = sb("eps_col", [P, 1])
        W_ext = sb("W_ext", [P, KT, HW_])
        gnn_bias_b = sb("gnn_bias_b", [P, D])
        wqkv_s = sb("wqkv_s", [P, KT, 3 * D])
        bqkv_b = sb("bqkv_b", [P, 3 * D])
        w1_s = sb("w1_s", [P, KT, D])
        w2_s = sb("w2_s", [P, KT, D])
        b1_b = sb("b1_b", [P, D])
        b2_b = sb("b2_b", [P, D])
        ln_g = sb("ln_g", [P, 2, HC])
        ln_b = sb("ln_b", [P, 2, HC])
        head_mask = sb("head_mask", [P, P])
        weff = sb("weff", [P, KT, D])
        beff = sb("beff", [P, D])
        gam_b = sb("gam_b", [P, D])
        bet_b = sb("bet_b", [P, D])
        wr_s = sb("wr_s", [P, KT, NE])
        br_b = sb("br_b", [P, NE])
        acc = sb("acc", [P, NT, HW_])
        adm = sb("adm", [P, NT, 2 * HEADS])
        smax = sb("smax", [P, HEADS])
        smax_all = sb("smax_all", [P, HEADS])
        steps_row = sb("steps_row", [1, 2, NCH * P], I32)
        xin = sb("xin", [P, 2, D])
        xn = sb("xn", [P, 2, D])
        xnT = sb("xnT", [P, 2, KT, P])
        stats = sb("stats", [P, 2, 6])
        mv = sb("mv", [P, 2, 2])
        std = sb("std", [P, 2, 1])
        rstd = sb("rstd", [P, 2, 1])

        psA = [ctx.enter_context(nc.psum_tensor(f"psA{q}", [P, 512], F32)) for q in range(2)]
        psB = [ctx.enter_context(nc.psum_tensor(f"psB{q}", [P, 512], F32)) for q in range(2)]
        psC = [ctx.enter_context(nc.psum_tensor(f"psC{q}", [P, 512], F32)) for q in range(2)]
        psD = [ctx.enter_context(nc.psum_tensor(f"psD{q}", [P, 512], F32)) for q in range(2)]

        loads_done = sem("loads_done")
        act_gate, dve_gate, pool_gate = sem("act_gate"), sem("dve_gate"), sem("pool_gate")

        LOADS = [
            (W_ext[:, :, 0:D], gnn_W.rearrange("(k p) n -> p k n", p=P)),
            (gnn_bias_b[:], gnn_bias.partition_broadcast(P)),
            (wqkv_s[:], w_qkv.rearrange("(k p) n -> p k n", p=P)),
            (bqkv_b[:], b_qkv.partition_broadcast(P)),
            (w1_s[:], w1.rearrange("(k p) n -> p k n", p=P)),
            (w2_s[:], w2.rearrange("(k p) n -> p k n", p=P)),
            (b1_b[:], b1.partition_broadcast(P)),
            (b2_b[:], b2.partition_broadcast(P)),
            (ln_g[:, 0], kln_g.partition_broadcast(P)),
            (ln_g[:, 1], vln_g.partition_broadcast(P)),
            (ln_b[:, 0], kln_b.partition_broadcast(P)),
            (ln_b[:, 1], vln_b.partition_broadcast(P)),
            (gam_b[:], gamma.partition_broadcast(P)),
            (bet_b[:], beta.partition_broadcast(P)),
            (wr_s[:], Wr.rearrange("(k p) n -> p k n", p=P)),
            (br_b[:], br.partition_broadcast(P)),
        ]


        def each_tile(eng, body):
            for i in range(2):
                body(i, i % 2, P, 0)
            with eng.Fori(1, FULL // 2 - 1) as it:
                for q in range(2):
                    body(it * 2 + q, q, P, it)
            for i in range(FULL - 2, FULL):
                body(i, i % 2, P, i // 2)
            body(FULL, 0, TAIL, FULL // 2)

        def later(i, n):
            return not (isinstance(i, int) and i < n)

        def node_rows(i, rows):
            return bass.ds(i * P, rows)

        with ExitStack() as ph:
            att_b = sb("att_b", [P, 2, D], c=ph)
            att_prod = sb("att_prod", [P, KT, D], c=ph)
            pad_row = sb("pad_row", [1, 2, PAD], I32, c=ph)
            last_dst = sb("last_dst", [1, NSB], I32, c=ph)
            last_tile = sb("last_tile", [1, NSB], I32, c=ph)
            last_step = sb("last_step", [1, NSB], c=ph)
            sb_ids = sb("sb_ids", [1, NSB], c=ph)
            below = sb("below", [P, NSB], c=ph)
            sb_done = sb("sb_done", [P, NCH], c=ph)
            tile_of = sb("tile_of", [P, NCH], c=ph)
            steps_i = sb("steps_i", [P, 2, NCH], I32, c=ph)
            pads_set, edges_in, last_in = sem("pads_set"), sem("edges_in"), sem("last_in")
            consts_set, ident_zero, rows_set = sem("consts_set"), sem("ident_zero"), sem("rows_set")
            att_prod_ready, att_cols_ready = sem("att_prod_ready"), sem("att_cols_ready")
            last_tile_ready, last_step_ready, last_step_spread = sem("last_tile_ready"), sem("last_step_ready"), sem("last_step_spread")
            sb_done_ready, tile_of_ready = sem("sb_done_ready"), sem("tile_of_ready")
            steps_ready, steps_out, steps_in, mask_zero = sem("steps_ready"), sem("steps_out"), sem("steps_in"), sem("mask_zero")
            NLOADS = len(LOADS) + 2

            with nc.Block() as block:
                @block.sync
                def _(sp):
                    sp.dma_start(edge_src[0:E], src).then_inc(edges_in, 16)
                    sp.dma_start(edge_dst[0:E], dst).then_inc(edges_in, 16)
                    sp.wait_ge(pads_set, 2)
                    sp.dma_start(edge_src[E:E + PAD].unsqueeze(0), pad_row[:, 0]).then_inc(edges_in, 16)
                    sp.dma_start(edge_dst[E:E + PAD].unsqueeze(0), pad_row[:, 1]).then_inc(edges_in, 16)
                    sp.wait_ge(edges_in, 64)
                    sp.dma_start(last_dst[:], edge_dst.rearrange("(b e) -> e b", e=SB)[SB - 1:SB, 0:NSB],
                                 allow_slow_non_contiguous=True).then_inc(last_in, 16)
                    sp.wait_ge(steps_ready, 2)
                    for w in range(2):
                        sp.dma_start(step_table[w].rearrange("(c p) -> p c", p=P), steps_i[:, w],
                                     allow_slow_non_contiguous=True).then_inc(steps_out, 16)
                    sp.wait_ge(steps_out, 32)
                    sp.dma_start(steps_row[:], step_table.unsqueeze(0)).then_inc(steps_in, 16)
                    sp.wait_ge(steps_in, 16)

                @block.scalar
                def _(act):
                    for w, a in enumerate((att_src, att_dst)):
                        act.dma_start(att_b[:, w], a.rearrange("h c -> (h c)").partition_broadcast(P)).then_inc(loads_done, 16)
                    for to, frm in LOADS:
                        act.dma_start(to, frm).then_inc(loads_done, 16)
                    act.wait_ge(loads_done, 16 * NLOADS)

                @block.gpsimd
                def _(pool):
                    pool.memset(ident[:], 0.0).then_inc(ident_zero, 1)
                    for ids, step, mult in ((node_ids, P, 1), (sb_ids, 1, 0), (iota8, 1, 0)):
                        pool.iota(ids[:], pattern=[[step, ids.shape[1]]], base=0, channel_multiplier=mult,
                                  allow_small_or_imprecise_dtypes=True).then_inc(consts_set, 1)
                    pool.wait_ge(ident_zero, 1)
                    pool.affine_select(out=ident[:], in_=ident[:], compare_op=ALU.not_equal, fill=1.0, base=0,
                                       pattern=[[-1, P]], channel_multiplier=1).then_inc(consts_set, 1)

                @block.tensor
                def _(pe):
                    pe.wait_ge(rows_set, 1)
                    pe.wait_ge(last_step_ready, 1)
                    pe.matmul(psA[0][:, 0:NSB], ones_row[:], last_step[:], start=True, stop=True).then_inc(last_step_spread, 1)

                @block.vector
                def _(dve):
                    dve.memset(pad_row[:, 0], 0).then_inc(pads_set, 1)
                    dve.memset(pad_row[:, 1], NT * P).then_inc(pads_set, 1)
                    dve.memset(ones_row[:], 1.0).then_inc(rows_set, 1)
                    dve.memset(eps_col[:], EPS)
                    dve.memset(acc[:, NT - 1], 0.0)
                    dve.memset(head_mask[:], 0.0).then_inc(mask_zero, 1)
                    dve.wait_ge(mask_zero, 1)
                    for j in range(P // HC):
                        dve.memset(head_mask[HC * j:HC * (j + 1), HC * j:HC * (j + 1)], 1.0 / N)
                    dve.wait_ge(loads_done, 16 * NLOADS)
                    for w in range(2):
                        if w:
                            dve.wait_ge(att_cols_ready, 1)
                        dve.tensor_tensor(att_prod[:], W_ext[:, :, 0:D], att_b[:, w].unsqueeze(1).broadcast_to([P, KT, D]),
                                          ALU.mult).then_inc(att_prod_ready, 1)
                        dve.wait_ge(att_prod_ready, w + 1)
                        for k in range(KT):
                            last = dve.tensor_reduce(W_ext[:, k, D + HEADS * w:D + HEADS * (w + 1)],
                                                     att_prod[:, k].rearrange("p (h c) -> p h c", h=HEADS), AX_X, ALU.add)
                        last.then_inc(att_cols_ready, 1)
                    dve.wait_ge(last_in, 16)
                    dve.tensor_scalar(last_tile[:], last_dst[:], P.bit_length() - 1, None,
                                      ALU.logical_shift_right).then_inc(last_tile_ready, 1)
                    dve.wait_ge(last_tile_ready, 1)
                    dve.wait_ge(consts_set, 4)
                    dve.scalar_tensor_tensor(out=last_step[:], in0=last_tile[:], scalar=float(NT - 1), in1=sb_ids[:],
                                             op0=ALU.min, op1=ALU.add).then_inc(last_step_ready, 1)
                    dve.wait_ge(last_step_spread, 1)
                    for c in range(NCH):
                        last = dve.tensor_scalar(below[:], psA[0][:, 0:NSB], node_ids[:, c:c + 1], 0.0, ALU.is_lt, ALU.add,
                                                 accum_out=sb_done[:, c:c + 1])
                        last.then_inc(sb_done_ready, 1)
                        dve.wait_ge(sb_done_ready, c + 1)
                    dve.tensor_tensor(tile_of[:], node_ids[:, 0:NCH], sb_done[:], ALU.subtract).then_inc(tile_of_ready, 1)
                    dve.tensor_copy(steps_i[:, 0], sb_done[:]).then_inc(steps_ready, 1)
                    dve.wait_ge(tile_of_ready, 1)
                    dve.tensor_scalar(steps_i[:, 1], tile_of[:], float(NT - 1), None, ALU.min).then_inc(steps_ready, 1)

        with ExitStack() as ph:
            kvx = sb("kvx", [P, 2, MH, 2 * HC], c=ph)
            kvc = sb("kvc", [P, 2, MH, 2 * HC], c=ph)
            kvsq = sb("kvsq", [P, 2, MH, 2 * HC], c=ph)
            kvo = sb("kvo", [P, 2, 2, MH, HC], c=ph)
            kvsum = sb("kvsum", [P, 2, 2 * MH], c=ph)
            kvvar = sb("kvvar", [P, 2, 2 * MH], c=ph)
            kvstd = sb("kvstd", [P, 2, 2 * MH], c=ph)
            kvrstd = sb("kvrstd", [P, 2, 2 * MH], c=ph)
            base = sb("base1", [P, 2, D], c=ph)
            x_in = [sem("x_in0"), sem("x_in1")]
            xnT_out = [sem("xnT_out0"), sem("xnT_out1")]
            base_out = [sem("base_out0"), sem("base_out1")]
            table_out = sem("table_out")
            stats_ready, mv_ready, std_ready, rstd_ready, xn_ready = (sem(n) for n in ("stats_ready", "mv_ready", "std_ready", "rstd_ready", "xn_ready"))
            base_sum, base_ready, turned, xnT_ready = sem("base_sum"), sem("base_ready"), sem("turned"), sem("xnT_ready")
            h_done, h_copied, kv_done, kv_biased = sem("h_done"), sem("h_copied"), sem("kv_done"), sem("kv_biased")
            kv_summed, kv_centred, kv_squared, kv_var_ready = sem("kv_summed"), sem("kv_centred"), sem("kv_squared"), sem("kv_var_ready")
            kv_std_ready, kv_rstd_ready, kv_normed, kv_scaled, kvo_ready, kvo_used = (sem(n) for n in (
                "kv_std_ready", "kv_rstd_ready", "kv_normed", "kv_scaled", "kvo_ready", "kvo_used"))
            with nc.Block() as block:
                @block.sync
                def _(sp):
                    def load_x(i, q, rows):
                        sp.dma_start(xin[0:rows, q], x[node_rows(i, rows)]).then_inc(x_in[q], 16)

                    def tile(i, q, rows, it):
                        sp.wait_ge(h_copied, i + 1)
                        sp.dma_start(node_table[node_rows(i, P)].unsqueeze(1), acc[:, bass.ds(i, 1)]).then_inc(table_out, 16)
                        sp.wait_ge(xnT_ready, i + 1)
                        sp.dma_start(xnT_dram[bass.ds(i, 1), :, :, 0:rows].rearrange("o p k n -> p (o k) n"),
                                     xnT[:, q, :, 0:rows]).then_inc(xnT_out[q], 16)
                        sp.wait_ge(base_ready, i + 1)
                        sp.dma_start(base_dram[node_rows(i, rows)], base[0:rows, q]).then_inc(base_out[q], 16)
                        if isinstance(i, int) and i + 2 > FULL:
                            return
                        load_x(i + 2, q, TAIL if isinstance(i, int) and i + 2 == FULL else P)

                    for i in range(2):
                        load_x(i, i, P)
                    each_tile(sp, tile)
                    sp.wait_ge(table_out, 16 * NT)
                    for q in range(2):
                        sp.wait_ge(xnT_out[q], 16 * (NT // 2 + (1 - q)))
                        sp.wait_ge(base_out[q], 16 * (NT // 2 + (1 - q)))

                @block.vector
                def _(dve):
                    def normalise(i, q, rows, it):
                        dve.wait_ge(x_in[q], it * 16 + 16)
                        dve.bn_stats(stats[0:rows, q], xin[0:rows, q]).then_inc(stats_ready, 1)
                        dve.wait_ge(stats_ready, i + 1)
                        dve.sem_inc(dve_gate, 1)
                        dve.bn_aggr(mv[0:rows, q], stats[0:rows, q]).then_inc(mv_ready, 1)
                        dve.wait_ge(std_ready, i + 1)
                        dve.reciprocal(rstd[0:rows, q], std[0:rows, q]).then_inc(rstd_ready, 1)
                        dve.wait_ge(rstd_ready, i + 1)
                        dve.tensor_scalar(xn[0:rows, q], xin[0:rows, q], mv[0:rows, q, 0:1], rstd[0:rows, q],
                                          ALU.subtract, ALU.mult).then_inc(xn_ready, 1)
                        dve.wait_ge(xn_ready, i + 1)
                        if later(i, 2):
                            dve.wait_ge(base_out[q], it * 16)
                        dve.tensor_tensor(base[0:rows, q], xin[0:rows, q], xn[0:rows, q], ALU.add).then_inc(base_sum, 1)
                        dve.wait_ge(base_sum, i + 1)
                        dve.tensor_tensor(base[0:rows, q], base[0:rows, q], b2_b[0:rows], ALU.add).then_inc(base_ready, 1)

                    def keys_values(i, q, rows):
                        groups = lambda t: t[0:rows, q].rearrange("p h (s c) -> p (h s) c", s=2)
                        spread = lambda t: t[0:rows, q].unsqueeze(2).broadcast_to([rows, 2 * MH, HC])
                        heads = lambda t: t[0:rows].rearrange("p s c -> p (s c)").unsqueeze(1).broadcast_to([rows, MH, 2 * HC])
                        dve.wait_ge(kv_done, i + 1)
                        dve.tensor_tensor(kvx[0:rows, q], psC[q][0:rows, :].rearrange("p (h c) -> p h c", h=MH),
                                          bqkv_b[0:rows].rearrange("p (h c) -> p h c", h=MH)[:, :, HC:3 * HC],
                                          ALU.add).then_inc(kv_biased, 1)
                        dve.wait_ge(kv_biased, i + 1)
                        dve.tensor_reduce(kvsum[0:rows, q], groups(kvx), AX_X, ALU.add).then_inc(kv_summed, 1)
                        dve.wait_ge(kv_summed, i + 1)
                        dve.scalar_tensor_tensor(out=groups(kvc), in0=spread(kvsum), scalar=-1.0 / HC, in1=groups(kvx),
                                                 op0=ALU.mult, op1=ALU.add).then_inc(kv_centred, 1)
                        dve.wait_ge(kv_squared, i + 1)
                        dve.tensor_reduce(kvvar[0:rows, q], groups(kvsq), AX_X, ALU.add).then_inc(kv_var_ready, 1)
                        dve.wait_ge(kv_std_ready, i + 1)
                        dve.reciprocal(kvrstd[0:rows, q], kvstd[0:rows, q]).then_inc(kv_rstd_ready, 1)
                        dve.wait_ge(kv_rstd_ready, i + 1)
                        dve.tensor_tensor(groups(kvx), groups(kvc), spread(kvrstd), ALU.mult).then_inc(kv_normed, 1)
                        dve.wait_ge(kv_normed, i + 1)
                        dve.tensor_tensor(kvc[0:rows, q], kvx[0:rows, q], heads(ln_g), ALU.mult).then_inc(kv_scaled, 1)
                        dve.wait_ge(kv_scaled, i + 1)
                        if later(i, 2):
                            dve.wait_ge(kvo_used, i - 1)
                        dve.tensor_tensor(kvo[0:rows, q].rearrange("p s h c -> p h s c"),
                                          kvc[0:rows, q].rearrange("p h (s c) -> p h s c", s=2),
                                          ln_b[0:rows].unsqueeze(1).broadcast_to([rows, MH, 2, HC]),
                                          ALU.add).then_inc(kvo_ready, 1)

                    def tile(i, q, rows, it):
                        if later(i, 2):
                            dve.wait_ge(turned, i - 1)
                        normalise(i, q, rows, it)
                        dve.wait_ge(h_done, i + 1)
                        dve.tensor_scalar(acc[0:rows, bass.ds(i, 1)], psB[q][0:rows, 0:HW_].unsqueeze(1), 1.0, None,
                                          ALU.mult).then_inc(h_copied, 1)
                        keys_values(i, q, rows)

                    each_tile(dve, tile)

                @block.scalar
                def _(act):
                    def tile(i, q, rows, it):
                        act.wait_ge(mv_ready, i + 1)
                        act.activation(std[0:rows, q], mv[0:rows, q, 1:2], ACT.Sqrt, bias=eps_col[0:rows]).then_inc(std_ready, 1)
                        act.wait_ge(turned, i + 1)
                        if later(i, 2):
                            act.wait_ge(xnT_out[q], it * 16)
                            act.wait_ge(kv_done, i - 1)
                        act.activation(xnT[:, q, :, 0:rows], psA[q][:, 0:KT * P].rearrange("p (k n) -> p k n", k=KT)[:, :, 0:rows],
                                       ACT.Copy).then_inc(xnT_ready, 1)
                        act.wait_ge(kv_centred, i + 1)
                        act.activation(kvsq[0:rows, q], kvc[0:rows, q], ACT.Square).then_inc(kv_squared, 1)
                        act.wait_ge(kv_var_ready, i + 1)
                        act.activation(kvstd[0:rows, q], kvvar[0:rows, q], ACT.Sqrt, bias=eps_col[0:rows],
                                       scale=1.0 / HC).then_inc(kv_std_ready, 1)

                    each_tile(act, tile)

                @block.tensor
                def _(pe):
                    def key_value_product(i, q, rows):
                        pe.wait_ge(kvo_ready, i + 1)
                        for hf in range(KT):
                            k, v = (kvo[0:rows, q, s].rearrange("p h c -> p (h c)")[:, hf * P:(hf + 1) * P] for s in range(2))
                            last = pe.matmul(psD[hf][:, 0:P], k, v, start=not later(i, 1), stop=isinstance(i, int) and i == FULL,
                                             skip_group_check=True)
                        last.then_inc(kvo_used, 1)

                    def tile(i, q, rows, it):
                        pe.wait_ge(xn_ready, i + 1)
                        if later(i, 2):
                            pe.wait_ge(xnT_ready, i - 1)
                        for k in range(KT):
                            last = pe.transpose(psA[q][:, k * P:k * P + rows], xn[0:rows, q, k * P:(k + 1) * P],
                                                ident[0:rows, 0:rows])
                        last.then_inc(turned, 1)
                        pe.wait_ge(xnT_ready, i + 1)
                        if later(i, 2):
                            pe.wait_ge(h_copied, i - 1)
                        for k in range(KT):
                            last = pe.matmul(psB[q][0:rows, 0:HW_], xnT[:, q, k, 0:rows], W_ext[:, k],
                                             start=(k == 0), stop=(k == KT - 1))
                        last.then_inc(h_done, 1)
                        if later(i, 2):
                            pe.wait_ge(kv_biased, i - 1)
                        for k in range(KT):
                            last = pe.matmul(psC[q][0:rows, :], xnT[:, q, k, 0:rows],
                                             wqkv_s[:, k].rearrange("p (h c) -> p h c", h=MH)[:, :, HC:3 * HC],
                                             start=(k == 0), stop=(k == KT - 1))
                        last.then_inc(kv_done, 1)
                        if later(i, 1):
                            key_value_product(i - 1, 1 - q, P)

                    each_tile(pe, tile)
                    key_value_product(FULL, 0, TAIL)

        with ExitStack() as ph:
            wq_c = sb("wq_c", [P, KT, D], c=ph)
            bq_c = sb("bq_c", [1, D], c=ph)
            wqT = sb("wqT", [P, KT, D], c=ph)
            kvm = sb("kvm", [P, KT, P], c=ph)
            bq_col = sb("bq_col", [P, KT], c=ph)
            qkvT = sb("qkvT", [P, KT, D], c=ph)
            bq_kv = sb("bq_kv", [P, KT, P], c=ph)
            za = sb("za", [P, NT, HEADS], c=ph)
            zl = sb("zl", [P, NT, HEADS], c=ph)
            p_self = sb("p_self", [P, NT, HEADS], c=ph)
            wq_ready, wq_turned, wqT_ready, kvm_ready = sem("wq_ready"), sem("wq_turned"), sem("wqT_ready"), sem("kvm_ready")
            bq_turned, bq_col_ready, qkv_done, qkvT_ready = sem("bq_turned"), sem("bq_col_ready"), sem("qkv_done"), sem("qkvT_ready")
            weff_done, beff_done, bq_kv_done, bq_kv_ready, folded = (sem(n) for n in ("weff_done", "beff_done", "bq_kv_done", "bq_kv_ready", "folded"))
            smax_ready, smax_spread, adm_part, self_part, p_self_ready = (sem(n) for n in ("smax_ready", "smax_spread", "adm_part", "self_part", "p_self_ready"))
            with nc.Block() as block:
                @block.gpsimd
                def _(pool):
                    pool.wait_ge(smax_ready, 1)
                    pool.partition_all_reduce(smax_all[:], smax[:], P, bass.bass_isa.ReduceOp.max).then_inc(smax_spread, 1)

                @block.scalar
                def _(act):
                    act.wait_ge(self_part, 3)
                    act.activation(p_self[:], za[:], ACT.Exp).then_inc(p_self_ready, 1)

                @block.tensor
                def _(pe):
                    pe.wait_ge(wq_ready, 2)
                    for hf in range(KT):
                        for k in range(KT):
                            last = pe.transpose(psA[hf][:, k * P:(k + 1) * P], wq_c[:, k, hf * P:(hf + 1) * P], ident[:])
                    last.then_inc(wq_turned, 1)
                    for hf in range(KT):
                        last = pe.matmul(psC[0][:, hf:hf + 1], bq_c[:, hf * P:(hf + 1) * P], ones_row[:, 0:1], start=True, stop=True)
                    last.then_inc(bq_turned, 1)
                    pe.wait_ge(wqT_ready, 2)
                    pe.wait_ge(kvm_ready, 2)
                    for hf in range(KT):
                        last = pe.matmul(psB[hf][:, 0:D], kvm[:, hf], wqT[:, hf], start=True, stop=True)
                    last.then_inc(qkv_done, 1)
                    pe.wait_ge(bq_col_ready, 1)
                    for hf in range(KT):
                        last = pe.matmul(psC[1][:, hf:hf + 1], kvm[:, hf], bq_col[:, hf:hf + 1], start=True, stop=True)
                    last.then_inc(bq_kv_done, 1)
                    pe.wait_ge(qkvT_ready, 2)
                    for c in range(KT):
                        for hf in range(KT):
                            last = pe.matmul(psA[c][:, 0:D], qkvT[:, hf, c * P:(c + 1) * P], w1_s[:, hf], start=(hf == 0), stop=(hf == KT - 1))
                    last.then_inc(weff_done, 1)
                    pe.wait_ge(bq_kv_ready, 2)
                    for hf in range(KT):
                        last = pe.matmul(psC[0][:, 0:D], bq_kv[:, hf], w1_s[:, hf], start=(hf == 0), stop=(hf == KT - 1))
                    last.then_inc(beff_done, 1)

                @block.vector
                def _(dve):
                    dve.tensor_copy(wq_c[:].rearrange("p k (h c) -> p k h c", h=MH),
                                    wqkv_s[:].rearrange("p k (h c) -> p k h c", h=MH)[:, :, :, 0:HC]).then_inc(wq_ready, 1)
                    dve.tensor_copy(bq_c[:].rearrange("p (h c) -> p h c", h=MH),
                                    bqkv_b[0:1].rearrange("p (h c) -> p h c", h=MH)[:, :, 0:HC]).then_inc(wq_ready, 1)
                    for hf in range(KT):
                        dve.tensor_tensor(kvm[:, hf], psD[hf][:, 0:P], head_mask[:], ALU.mult).then_inc(kvm_ready, 1)
                    dve.wait_ge(wq_turned, 1)
                    for hf in range(KT):
                        dve.tensor_copy(wqT[:, hf], psA[hf][:, 0:D]).then_inc(wqT_ready, 1)
                    dve.wait_ge(bq_turned, 1)
                    dve.tensor_copy(bq_col[:], psC[0][:, 0:KT]).then_inc(bq_col_ready, 1)
                    dve.wait_ge(qkv_done, 1)
                    for hf in range(KT):
                        dve.tensor_copy(qkvT[:, hf], psB[hf][:, 0:D]).then_inc(qkvT_ready, 1)
                    dve.wait_ge(bq_kv_done, 1)
                    for hf in range(KT):
                        dve.tensor_copy(bq_kv[:, hf], psC[1][:, hf:hf + 1].broadcast_to([P, P])).then_inc(bq_kv_ready, 1)
                    dve.wait_ge(weff_done, 1)
                    for c in range(KT):
                        dve.tensor_tensor(weff[:, c], psA[c][:, 0:D], w1_s[:, c], ALU.add).then_inc(folded, 1)
                    dve.wait_ge(beff_done, 1)
                    dve.tensor_tensor(beff[:], psC[0][:, 0:D], b1_b[:], ALU.add).then_inc(folded, 1)
                    a_src, a_dst = acc[:, :, D:D + HEADS], acc[:, :, D + HEADS:HW_]
                    dve.tensor_reduce(smax[:], a_src.rearrange("p t h -> p h t"), AX_X, ALU.max).then_inc(smax_ready, 1)
                    dve.tensor_copy(adm[:, :, 0:HEADS], a_dst).then_inc(adm_part, 1)
                    dve.wait_ge(smax_spread, 1)
                    dve.tensor_tensor(za[:], a_dst, smax_all[:].unsqueeze(1).broadcast_to([P, NT, HEADS]), ALU.add).then_inc(adm_part, 1)
                    dve.wait_ge(adm_part, 2)
                    dve.scalar_tensor_tensor(out=adm[:, :, HEADS:2 * HEADS], in0=za[:], scalar=SLOPE, in1=za[:],
                                             op0=ALU.mult, op1=ALU.max).then_inc(adm_part, 1)
                    dve.wait_ge(adm_part, 3)
                    dve.tensor_tensor(za[:], a_src, a_dst, ALU.add).then_inc(self_part, 1)
                    dve.wait_ge(self_part, 1)
                    dve.scalar_tensor_tensor(out=zl[:], in0=za[:], scalar=SLOPE, in1=za[:],
                                             op0=ALU.mult, op1=ALU.max).then_inc(self_part, 1)
                    dve.wait_ge(self_part, 2)
                    dve.tensor_tensor(za[:], zl[:], adm[:, :, HEADS:2 * HEADS], ALU.subtract).then_inc(self_part, 1)
                    dve.wait_ge(p_self_ready, 1)
                    h_v = acc[:, :, 0:D].rearrange("p t (h c) -> p t h c", h=HEADS)
                    for t in range(NT):
                        dve.tensor_tensor(h_v[:, t], h_v[:, t], p_self[:, t].unsqueeze(2).broadcast_to([P, HEADS, C]), ALU.mult)
                    dve.tensor_copy(acc[:, :, D:AW], p_self[:])

        with ExitStack() as ph:
            base = sb("base2", [P, 2, D], c=ph)
            mixed = sb("mixed2", [P, 2, D], c=ph)
            hpre = sb("hpre", [P, 2, D], c=ph)
            hid = sb("hid", [P, 2, D], c=ph)
            hidT = sb("hidT", [P, 2, KT, P], c=ph)
            m_xnT_in, m_base_in, m_out = ([sem(f"{n}{q}") for q in range(2)] for n in ("m_xnT_in", "m_base_in", "m_out"))
            up_done, up_biased, gelu_done, hid_turned, hidT_ready, down_done, mixed_ready = (sem(n) for n in (
                "up_done", "up_biased", "gelu_done", "hid_turned", "hidT_ready", "down_done", "mixed_ready"))
            with nc.Block() as block:
                @block.sync
                def _(sp):
                    def load(i, q, rows):
                        if later(i, 2):
                            sp.wait_ge(mixed_ready, i - 1)
                        sp.dma_start(xnT[:, q, :, 0:rows], xnT_dram[bass.ds(i, 1), :, :, 0:rows].rearrange("o p k n -> p (o k) n")
                                     ).then_inc(m_xnT_in[q], 16)
                        sp.dma_start(base[0:rows, q], base_dram[node_rows(i, rows)]).then_inc(m_base_in[q], 16)

                    def tile(i, q, rows, it):
                        sp.wait_ge(mixed_ready, i + 1)
                        sp.dma_start(mixed_dram[node_rows(i, rows)], mixed[0:rows, q]).then_inc(m_out[q], 16)
                        if isinstance(i, int) and i + 2 > FULL:
                            return
                        load(i + 2, q, TAIL if isinstance(i, int) and i + 2 == FULL else P)

                    for i in range(2):
                        load(i, i, P)
                    each_tile(sp, tile)
                    for q in range(2):
                        sp.wait_ge(m_out[q], 16 * (NT // 2 + (1 - q)))

                @block.tensor
                def _(pe):
                    def tile(i, q, rows, it):
                        pe.wait_ge(m_xnT_in[q], it * 16 + 16)
                        if later(i, 2):
                            pe.wait_ge(up_biased, i - 1)
                        for k in range(KT):
                            last = pe.matmul(psA[q][0:rows, 0:D], xnT[:, q, k, 0:rows], weff[:, k], start=(k == 0), stop=(k == KT - 1))
                        last.then_inc(up_done, 1)
                        pe.wait_ge(gelu_done, i + 1)
                        if later(i, 2):
                            pe.wait_ge(hidT_ready, i - 1)
                        for k in range(KT):
                            last = pe.transpose(psB[q][:, k * P:k * P + rows], hid[0:rows, q, k * P:(k + 1) * P], ident[0:rows, 0:rows])
                        last.then_inc(hid_turned, 1)
                        pe.wait_ge(hidT_ready, i + 1)
                        if later(i, 2):
                            pe.wait_ge(mixed_ready, i - 1)
                        for k in range(KT):
                            last = pe.matmul(psC[q][0:rows, 0:D], hidT[:, q, k, 0:rows], w2_s[:, k], start=(k == 0), stop=(k == KT - 1))
                        last.then_inc(down_done, 1)

                    each_tile(pe, tile)

                @block.scalar
                def _(act):
                    def tile(i, q, rows, it):
                        act.wait_ge(up_biased, i + 1)
                        if later(i, 2):
                            act.wait_ge(hid_turned, i - 1)
                        act.activation(hid[0:rows, q], hpre[0:rows, q], ACT.Gelu).then_inc(gelu_done, 1)
                        act.wait_ge(hid_turned, i + 1)
                        if later(i, 2):
                            act.wait_ge(down_done, i - 1)
                        act.activation(hidT[:, q, :, 0:rows], psB[q][:, 0:KT * P].rearrange("p (k n) -> p k n", k=KT)[:, :, 0:rows],
                                       ACT.Copy).then_inc(hidT_ready, 1)

                    each_tile(act, tile)

                @block.vector
                def _(dve):
                    def tile(i, q, rows, it):
                        dve.wait_ge(up_done, i + 1)
                        if later(i, 2):
                            dve.wait_ge(gelu_done, i - 1)
                        dve.tensor_tensor(hpre[0:rows, q], psA[q][0:rows, 0:D], beff[0:rows], ALU.add).then_inc(up_biased, 1)
                        dve.wait_ge(down_done, i + 1)
                        dve.wait_ge(m_base_in[q], it * 16 + 16)
                        if later(i, 2):
                            dve.wait_ge(m_out[q], it * 16)
                        dve.tensor_tensor(mixed[0:rows, q], psC[q][0:rows, 0:D], base[0:rows, q], ALU.add).then_inc(mixed_ready, 1)

                    each_tile(dve, tile)

        with ExitStack() as ph:
            iota_all = sb("iota_all", [P, NT * P], c=ph)
            iota_set = sem("iota_set")
            src_idx = sb("src_idx", [P, RING, GB], I32, c=ph)
            dst_col = sb("dst_col", [P, RING, GB], I32, c=ph)
            dst_row = sb("dst_row", [P, RING, SB], I32, c=ph)
            rows_g = sb("rows_g", [P, RING, GB, HW_], c=ph)
            pick_e = sb("pick_e", [P, 2, GB, P], c=ph)
            pick_n = sb("pick_n", [P, 2, SB], c=ph)
            ze = sb("ze", [P, 2, GB, HEADS], c=ph)
            zle = sb("zle", [P, 2, GB, HEADS], c=ph)
            ye = sb("ye", [P, 2, GB, HEADS], c=ph)
            pe_h = sb("pe_h", [P, 2, GB, AW], c=ph)
            idx_in, dst_in, row_in, gathered = ([sem(f"{n}{r}") for r in range(RING)] for n in ("idx_in", "dst_in", "row_in", "gathered"))
            pick_e_ready, pick_n_ready, picked, z_ready, zl_ready, y_ready, p_ready, ph_ready, summed, added = (sem(n) for n in (
                "pick_e_ready", "pick_n_ready", "picked", "z_ready", "zl_ready", "y_ready", "p_ready", "ph_ready", "summed", "added"))
            src_v = edge_src.rearrange("(b p j) -> b p j", p=P, j=GB)
            dst_v = edge_dst.rearrange("(b p j) -> b p j", p=P, j=GB)

            def each_step(eng, body):
                for s in range(RING):
                    body(s, s, 0)
                with eng.Fori(1, NS // RING - 1) as it:
                    for r in range(RING):
                        body(it * RING + r, r, it)
                for s in range(NS - RING, NS):
                    body(s, s % RING, s // RING)

            def step_value(eng, w, s, top):
                return eng.value_load(steps_row[0:1, w, bass.ds(s, 1)], min_val=0, max_val=top)

            with nc.Block() as block:
                @block.sync
                def _(sp):
                    def step(s, r, it):
                        b = step_value(sp, 0, s, NSB)
                        if later(s, RING):
                            sp.wait_ge(gathered[r], it * (16 * GB))
                        sp.dma_start(src_idx[:, r].unsqueeze(1), src_v[bass.ds(b, 1)].rearrange("b p j -> p b j")).then_inc(idx_in[r], 16)
                        if later(s, RING):
                            sp.wait_ge(pick_e_ready, s - (RING - 1))
                            sp.wait_ge(pick_n_ready, s - (RING - 1))
                        sp.dma_start(dst_col[:, r].unsqueeze(1), dst_v[bass.ds(b, 1)].rearrange("b p j -> p b j")).then_inc(dst_in[r], 16)
                        sp.dma_start(dst_row[:, r], edge_dst[bass.ds(b * SB, SB)].partition_broadcast(P)).then_inc(row_in[r], 16)

                    each_step(sp, step)

                @block.gpsimd
                def _(pool):
                    def step(s, r, it):
                        if later(s, RING):
                            pool.wait_ge(ph_ready, s - (RING - 1))
                        pool.wait_ge(idx_in[r], it * 16 + 16)
                        pool.sem_inc(pool_gate, 1)
                        for j in range(GB):
                            pool.indirect_dma_start(out=rows_g[:, r, j], out_offset=None, in_=node_table,
                                                    in_offset=bass.IndirectOffsetOnAxis(ap=src_idx[:, r, j:j + 1], axis=0)
                                                    ).then_inc(gathered[r], 16)

                    pool.iota(iota_all[:], pattern=[[1, NT * P]], base=0, channel_multiplier=0,
                              allow_small_or_imprecise_dtypes=True).then_inc(iota_set, 1)
                    each_step(pool, step)

                @block.vector
                def _(dve):
                    def picks(s, r, it):
                        t = step_value(dve, 1, s, NT - 1)
                        q = r % 2
                        dve.wait_ge(row_in[r], it * 16 + 16)
                        if later(s, 2):
                            dve.wait_ge(picked, s - 1)
                        dve.tensor_scalar(pick_n[:, q], dst_row[:, r], node_ids[:, bass.ds(t, 1)], None, ALU.is_equal).then_inc(pick_n_ready, 1)
                        dve.wait_ge(dst_in[r], it * 16 + 16)
                        if later(s, 2):
                            dve.wait_ge(summed, s - 1)
                        dve.tensor_tensor(pick_e[:, q], iota_all[:, bass.ds(t * P, P)].unsqueeze(1).broadcast_to([P, GB, P]),
                                          dst_col[:, r].unsqueeze(2).broadcast_to([P, GB, P]), ALU.is_equal).then_inc(pick_e_ready, 1)

                    def logits(s, r, it):
                        q = r % 2
                        dve.wait_ge(picked, s + 1)
                        dve.wait_ge(gathered[r], it * (16 * GB) + 16 * GB)
                        sel = psA[q][:, 0:GB * 2 * HEADS].rearrange("p (j a) -> p j a", j=GB)
                        dve.tensor_tensor(ze[:, q], rows_g[:, r, :, D:D + HEADS], sel[:, :, 0:HEADS], ALU.add).then_inc(z_ready, 1)
                        dve.wait_ge(z_ready, s + 1)
                        dve.scalar_tensor_tensor(out=zle[:, q], in0=ze[:, q], scalar=SLOPE, in1=ze[:, q],
                                                 op0=ALU.mult, op1=ALU.max).then_inc(zl_ready, 1)
                        dve.wait_ge(zl_ready, s + 1)
                        dve.tensor_tensor(ye[:, q], zle[:, q], sel[:, :, HEADS:2 * HEADS], ALU.subtract).then_inc(y_ready, 1)

                    def products(s, r):
                        q = r % 2
                        dve.wait_ge(p_ready, s + 1)
                        dve.tensor_tensor(pe_h[:, q, :, 0:D].rearrange("p j (h c) -> p j h c", h=HEADS),
                                          rows_g[:, r, :, 0:D].rearrange("p j (h c) -> p j h c", h=HEADS),
                                          pe_h[:, q, :, D:AW].unsqueeze(3).broadcast_to([P, GB, HEADS, C]),
                                          ALU.mult).then_inc(ph_ready, 1)

                    def add_up(s, r):
                        t = step_value(dve, 1, s, NT - 1)
                        q = r % 2
                        dve.wait_ge(summed, s + 1)
                        if later(s, 1):
                            dve.wait_ge(added, s)
                        at = acc[:, bass.ds(t, 1), 0:AW]
                        dve.tensor_tensor(at, at, psB[q][:, 0:AW].unsqueeze(1), ALU.add).then_inc(added, 1)

                    def step(s, r, it):
                        last = isinstance(s, int) and s == NS - 1
                        if not last:
                            picks(s + 1, (r + 1) % RING, it + (r + 1) // RING)
                        if later(s, 1):
                            add_up(s - 1, (r - 1) % RING)
                        products(s, r)
                        if not last:
                            logits(s + 1, (r + 1) % RING, it + (r + 1) // RING)

                    dve.wait_ge(iota_set, 1)
                    picks(0, 0, 0)
                    logits(0, 0, 0)
                    each_step(dve, step)
                    add_up(NS - 1, (NS - 1) % RING)

                @block.scalar
                def _(act):
                    def step(s, r, it):
                        q = r % 2
                        act.wait_ge(y_ready, s + 1)
                        if later(s, 2):
                            act.wait_ge(summed, s - 1)
                        act.activation(pe_h[:, q, :, D:AW], ye[:, q], ACT.Exp).then_inc(p_ready, 1)

                    each_step(act, step)

                @block.tensor
                def _(pe):
                    def pick(s, r):
                        t = step_value(pe, 1, s, NT - 1)
                        q = r % 2
                        pe.wait_ge(pick_n_ready, s + 1)
                        if later(s, 2):
                            pe.wait_ge(y_ready, s - 1)
                        for j in range(GB):
                            last = pe.matmul(psA[q][:, j * 2 * HEADS:(j + 1) * 2 * HEADS],
                                             pick_n[:, q].rearrange("p (e j) -> p e j", j=GB)[:, :, j], adm[:, bass.ds(t, 1)],
                                             start=True, stop=True)
                        last.then_inc(picked, 1)

                    def sums(s, r):
                        q = r % 2
                        pe.wait_ge(ph_ready, s + 1)
                        if later(s, 2):
                            pe.wait_ge(added, s - 1)
                        for j in range(GB):
                            last = pe.matmul(psB[q][:, 0:AW], pick_e[:, q, j], pe_h[:, q, j], start=(j == 0), stop=(j == GB - 1))
                        last.then_inc(summed, 1)

                    def step(s, r, it):
                        if not (isinstance(s, int) and s == NS - 1):
                            pick(s + 1, (r + 1) % RING)
                        sums(s, r)

                    pick(0, 0)
                    each_step(pe, step)

        with ExitStack() as ph:
            W1_s = sb("W1_s", [P, NE, KT, H], c=ph)
            W2_s = sb("W2_s", [P, NE, HK, D], c=ph)
            fb1_b = sb("fb1_b", [P, NE, H], c=ph)
            fb2_b = sb("fb2_b", [P, NE, D], c=ph)
            den = sb("den", [P, 2, HEADS], c=ph)
            rden = sb("rden", [P, 2, HEADS], c=ph)
            gat = sb("gat", [P, 2, D], c=ph)
            gat_b = sb("gat_b", [P, 2, D], c=ph)
            x1 = sb("x1", [P, 2, D], c=ph)
            xa, xb = xin, xn
            xc = sb("xc", [P, 2, D], c=ph)
            xd = sb("xd", [P, 2, D], c=ph)
            logit = sb("logit", [P, 2, NE], c=ph)
            top = sb("top", [P, 2, 8], c=ph)
            top_at = sb("top_at", [P, 2, 8], U32, c=ph)
            top_f = sb("top_f", [P, 2, 2], c=ph)
            gap = sb("gap", [P, 2, 1], c=ph)
            ex = sb("ex", [P, 2, 1], c=ph)
            ex1 = sb("ex1", [P, 2, 1], c=ph)
            wa = sb("wa", [P, 2, 2], c=ph)
            wfull = sb("wfull", [P, 2, 2, NE], c=ph)
            mix_slot = sb("mix_slot", [P, 2, D], c=ph)
            hb = sb("hb", [P, 2, H], c=ph)
            hg = sb("hg", [P, 2, H], c=ph)
            hT = sb("hT", [P, 2, HK, P], c=ph)
            ye4 = sb("ye4", [P, 2, D], c=ph)
            total = sb("total", [P, 2, D], c=ph)
            f_in = [sem("f_in0"), sem("f_in1")]
            f_out = [sem("f_out0"), sem("f_out1")]
            weights_in = sem("weights_in")
            (den_ready, rden_ready, gat_ready, gat_biased, x1_ready, total_ready, f_turned, f_xT_ready, logits_done, logit_ready,
             top_ready, top_at_ready, top_f_ready, gap_ready, ex_ready, ex1_ready, wa_ready, wb_ready, wfirst_ready, wsecond_ready,
             wfull_ready, xa_ready, xb_ready, xc_ready, xd_ready, up4_done, hb_ready, hg_ready, h_turned, hT_ready, down4_done,
             y4_ready, y4_added) = (sem("f_" + n) for n in (
                "den_ready rden_ready gat_ready gat_biased x1_ready total_ready turned xT_ready logits_done logit_ready "
                "top_ready top_at_ready top_f_ready gap_ready ex_ready ex1_ready wa_ready wb_ready wfirst_ready wsecond_ready "
                "wfull_ready xa_ready xb_ready xc_ready xd_ready up_done hb_ready hg_ready h_turned hT_ready down_done "
                "y_ready y_added").split())
            ln_stats, ln_mv, ln_std, ln_rstd = ([sem(f"f_{n}{k}") for k in range(2)] for n in ("stats", "mv", "std", "rstd"))
            with nc.Block() as block:
                @block.sync
                def _(sp):
                    def load(i, q, rows):
                        if later(i, 2):
                            sp.wait_ge(x1_ready, i - 1)
                        sp.dma_start(mix_slot[0:rows, q], mixed_dram[node_rows(i, rows)]).then_inc(f_in[q], 16)

                    def tile(i, q, rows, it):
                        sp.wait_ge(y4_added, i * NE + NE)
                        sp.dma_start(out[node_rows(i, rows)], total[0:rows, q]).then_inc(f_out[q], 16)
                        if isinstance(i, int) and i + 2 > FULL:
                            return
                        load(i + 2, q, TAIL if isinstance(i, int) and i + 2 == FULL else P)

                    for i in range(2):
                        load(i, i, P)
                    sp.dma_start(W1_s[:], W1.rearrange("e (k p) n -> p e k n", p=P)).then_inc(weights_in, 16)
                    sp.dma_start(W2_s[:], W2.rearrange("e (k p) n -> p e k n", p=P)).then_inc(weights_in, 16)
                    sp.dma_start(fb1_b[:], fb1.partition_broadcast(P)).then_inc(weights_in, 16)
                    sp.dma_start(fb2_b[:], fb2.partition_broadcast(P)).then_inc(weights_in, 16)
                    each_tile(sp, tile)
                    for q in range(2):
                        sp.wait_ge(f_out[q], 16 * (NT // 2 + (1 - q)))

                @block.vector
                def _(dve):
                    def norm(k, i, q, rows, src_t, src_ready, dst_t, dst_ready):
                        dve.wait_ge(src_ready, i + 1)
                        dve.bn_stats(stats[0:rows, q], src_t[0:rows, q]).then_inc(ln_stats[k], 1)
                        dve.wait_ge(ln_stats[k], i + 1)
                        dve.sem_inc(dve_gate, 1)
                        dve.bn_aggr(mv[0:rows, q], stats[0:rows, q]).then_inc(ln_mv[k], 1)
                        dve.wait_ge(ln_std[k], i + 1)
                        dve.reciprocal(rstd[0:rows, q], std[0:rows, q]).then_inc(ln_rstd[k], 1)
                        dve.wait_ge(ln_rstd[k], i + 1)
                        dve.tensor_scalar(dst_t[0:rows, q], src_t[0:rows, q], mv[0:rows, q, 0:1], rstd[0:rows, q],
                                          ALU.subtract, ALU.mult).then_inc(dst_ready, 1)

                    def front(i, q, rows, it):
                        a = acc[0:rows, bass.ds(i, 1)]
                        dve.tensor_scalar(den[0:rows, q].unsqueeze(1), a[:, :, D:AW], 1e-16, None, ALU.add).then_inc(den_ready, 1)
                        dve.wait_ge(den_ready, i + 1)
                        dve.reciprocal(rden[0:rows, q], den[0:rows, q]).then_inc(rden_ready, 1)
                        dve.wait_ge(rden_ready, i + 1)
                        dve.tensor_tensor(gat[0:rows, q].rearrange("p (o h c) -> p (o h) c", o=1, h=HEADS),
                                          a[:, :, 0:D].rearrange("p o (h c) -> p (o h) c", h=HEADS),
                                          rden[0:rows, q].unsqueeze(2).broadcast_to([rows, HEADS, C]), ALU.mult).then_inc(gat_ready, 1)
                        dve.wait_ge(gat_ready, i + 1)
                        dve.tensor_tensor(gat_b[0:rows, q], gat[0:rows, q], gnn_bias_b[0:rows], ALU.add).then_inc(gat_biased, 1)
                        dve.wait_ge(gat_biased, i + 1)
                        dve.wait_ge(f_in[q], it * 16 + 16)
                        dve.scalar_tensor_tensor(out=x1[0:rows, q], in0=gat_b[0:rows, q], scalar=0.0, in1=mix_slot[0:rows, q],
                                                 op0=ALU.max, op1=ALU.add).then_inc(x1_ready, 1)
                        norm(0, i, q, rows, x1, x1_ready, xa, xa_ready)
                        norm(1, i, q, rows, xa, xa_ready, xb, xb_ready)
                        dve.wait_ge(xb_ready, i + 1)
                        dve.tensor_tensor(xc[0:rows, q], xb[0:rows, q], gam_b[0:rows], ALU.mult).then_inc(xc_ready, 1)
                        dve.wait_ge(xc_ready, i + 1)
                        if later(i, 2):
                            dve.wait_ge(f_turned, i - 1)
                        dve.tensor_tensor(xd[0:rows, q], xc[0:rows, q], bet_b[0:rows], ALU.add).then_inc(xd_ready, 1)
                        if later(i, 2):
                            dve.wait_ge(f_out[q], it * 16)
                        dve.tensor_scalar(total[0:rows, q], x1[0:rows, q], 1.0, None, ALU.mult).then_inc(total_ready, 1)

                    def route(i, q, rows):
                        R = slice(0, rows)
                        dve.wait_ge(logits_done, i + 1)
                        dve.tensor_tensor(logit[R, q], psD[q][R, 0:NE], br_b[R], ALU.add).then_inc(logit_ready, 1)
                        dve.wait_ge(logit_ready, i + 1)
                        dve.sem_inc(dve_gate, 1)
                        dve.max(top[R, q], logit[R, q]).then_inc(top_ready, 1)
                        dve.wait_ge(top_ready, i + 1)
                        dve.sem_inc(dve_gate, 1)
                        dve.max_index(top_at[R, q], top[R, q], logit[R, q]).then_inc(top_at_ready, 1)
                        dve.tensor_tensor(gap[R, q], top[R, q, 1:2], top[R, q, 0:1], ALU.subtract).then_inc(gap_ready, 1)
                        dve.wait_ge(top_at_ready, i + 1)
                        dve.tensor_scalar(top_f[R, q], top_at[R, q, 0:2], 0.0, None, ALU.add).then_inc(top_f_ready, 1)
                        dve.wait_ge(ex_ready, i + 1)
                        dve.tensor_scalar(ex1[R, q], ex[R, q], 1.0, None, ALU.add).then_inc(ex1_ready, 1)
                        dve.wait_ge(ex1_ready, i + 1)
                        dve.reciprocal(wa[R, q, 0:1], ex1[R, q]).then_inc(wa_ready, 1)
                        dve.wait_ge(wa_ready, i + 1)
                        dve.tensor_tensor(wa[R, q, 1:2], ex[R, q], wa[R, q, 0:1], ALU.mult).then_inc(wb_ready, 1)
                        dve.wait_ge(top_f_ready, i + 1)
                        dve.tensor_scalar(wfull[R, q, 0], iota8[R], top_f[R, q, 0:1], wa[R, q, 0:1], ALU.is_equal,
                                          ALU.mult).then_inc(wfirst_ready, 1)
                        dve.wait_ge(wb_ready, i + 1)
                        dve.tensor_scalar(wfull[R, q, 1], iota8[R], top_f[R, q, 1:2], wa[R, q, 1:2], ALU.is_equal,
                                          ALU.mult).then_inc(wsecond_ready, 1)
                        dve.wait_ge(wfirst_ready, i + 1)
                        dve.wait_ge(wsecond_ready, i + 1)
                        dve.tensor_tensor(wfull[R, q, 0], wfull[R, q, 0], wfull[R, q, 1], ALU.add).then_inc(wfull_ready, 1)

                    def hidden_bias(k, e, rows):
                        u = e % 2
                        dve.wait_ge(up4_done, k + 1)
                        if later(k, 2):
                            dve.wait_ge(hg_ready, k - 1)
                        dve.tensor_tensor(hb[0:rows, u], psA[u][0:rows, :], fb1_b[0:rows, e], ALU.add).then_inc(hb_ready, 1)

                    def take(i, k, e, q, rows):
                        u = e % 2
                        dve.wait_ge(down4_done, k + 1)
                        dve.tensor_tensor(ye4[0:rows, u], psC[u][0:rows, 0:D], fb2_b[0:rows, e], ALU.add).then_inc(y4_ready, 1)
                        dve.wait_ge(y4_ready, k + 1)
                        if e == 0:
                            dve.wait_ge(wfull_ready, i + 1)
                            dve.wait_ge(total_ready, i + 1)
                        if later(k, 1):
                            dve.wait_ge(y4_added, k)
                        dve.scalar_tensor_tensor(out=total[0:rows, q], in0=ye4[0:rows, u], scalar=wfull[0:rows, q, 0, e:e + 1],
                                                 in1=total[0:rows, q], op0=ALU.mult, op1=ALU.add).then_inc(y4_added, 1)

                    def tile(i, q, rows, it):
                        front(i, q, rows, it)
                        route(i, q, rows)
                        hidden_bias(i * NE, 0, rows)
                        for e in range(NE):
                            if e + 1 < NE:
                                hidden_bias(i * NE + e + 1, e + 1, rows)
                            take(i, i * NE + e, e, q, rows)

                    dve.wait_ge(weights_in, 64)
                    each_tile(dve, tile)

                @block.scalar
                def _(act):
                    def gelu(k, e, rows):
                        u = e % 2
                        act.wait_ge(hb_ready, k + 1)
                        if later(k, 2):
                            act.wait_ge(h_turned, k - 1)
                        act.activation(hg[0:rows, u], hb[0:rows, u], ACT.Gelu).then_inc(hg_ready, 1)

                    def hidden_copy(k, e, rows):
                        u = e % 2
                        act.wait_ge(h_turned, k + 1)
                        if later(k, 2):
                            act.wait_ge(down4_done, k - 1)
                        act.activation(hT[:, u, :, 0:rows], psB[u][:, :].rearrange("p (c n) -> p c n", c=HK)[:, :, 0:rows],
                                       ACT.Copy).then_inc(hT_ready, 1)

                    def tile(i, q, rows, it):
                        for k in range(2):
                            act.wait_ge(ln_mv[k], i + 1)
                            act.activation(std[0:rows, q], mv[0:rows, q, 1:2], ACT.Sqrt, bias=eps_col[0:rows]).then_inc(ln_std[k], 1)
                        act.wait_ge(f_turned, i + 1)
                        if later(i, 2):
                            act.wait_ge(up4_done, (i - 1) * NE)
                        act.activation(xnT[:, q, :, 0:rows], psD[q][:, P:P + KT * P].rearrange("p (k n) -> p k n", k=KT)[:, :, 0:rows],
                                       ACT.Copy).then_inc(f_xT_ready, 1)
                        act.wait_ge(gap_ready, i + 1)
                        act.activation(ex[0:rows, q], gap[0:rows, q], ACT.Exp).then_inc(ex_ready, 1)
                        gelu(i * NE, 0, rows)
                        for e in range(NE):
                            if e + 1 < NE:
                                gelu(i * NE + e + 1, e + 1, rows)
                            hidden_copy(i * NE + e, e, rows)

                    each_tile(act, tile)

                @block.tensor
                def _(pe):
                    def up(k, e, q, rows):
                        u = e % 2
                        if later(k, 2):
                            pe.wait_ge(hb_ready, k - 1)
                        for c in range(KT):
                            last = pe.matmul(psA[u][0:rows, :], xnT[:, q, c, 0:rows], W1_s[:, e, c], start=(c == 0), stop=(c == KT - 1))
                        last.then_inc(up4_done, 1)

                    def turn(k, e, rows):
                        u = e % 2
                        pe.wait_ge(hg_ready, k + 1)
                        if later(k, 2):
                            pe.wait_ge(hT_ready, k - 1)
                        for c in range(HK):
                            last = pe.transpose(psB[u][:, c * P:c * P + rows], hg[0:rows, u, c * P:(c + 1) * P], ident[0:rows, 0:rows])
                        last.then_inc(h_turned, 1)

                    def down(k, e, rows):
                        u = e % 2
                        pe.wait_ge(hT_ready, k + 1)
                        if later(k, 2):
                            pe.wait_ge(y4_ready, k - 1)
                        for c in range(HK):
                            last = pe.matmul(psC[u][0:rows, 0:D], hT[:, u, c, 0:rows], W2_s[:, e, c], start=(c == 0), stop=(c == HK - 1))
                        last.then_inc(down4_done, 1)

                    def tile(i, q, rows, it):
                        pe.wait_ge(xd_ready, i + 1)
                        for k in range(KT):
                            last = pe.transpose(psD[q][:, P + k * P:P + k * P + rows], xd[0:rows, q, k * P:(k + 1) * P],
                                                ident[0:rows, 0:rows])
                        last.then_inc(f_turned, 1)
                        pe.wait_ge(f_xT_ready, i + 1)
                        for k in range(KT):
                            last = pe.matmul(psD[q][0:rows, 0:NE], xnT[:, q, k, 0:rows], wr_s[:, k], start=(k == 0), stop=(k == KT - 1))
                        last.then_inc(logits_done, 1)
                        up(i * NE, 0, q, rows)
                        for e in range(NE):
                            if e + 1 < NE:
                                up(i * NE + e + 1, e + 1, q, rows)
                            turn(i * NE + e, e, rows)
                            if e >= 1:
                                down(i * NE + e - 1, e - 1, rows)
                        down(i * NE + NE - 1, NE - 1, rows)

                    pe.wait_ge(weights_in, 64)
                    each_tile(pe, tile)


_INS = ['x', 'src', 'dst', 'L0_gnn_W', 'L0_gnn_att_src', 'L0_gnn_att_dst', 'L0_gnn_bias', 'L0_mix_w_qkv', 'L0_mix_b_qkv',
        'L0_mix_kln_g', 'L0_mix_kln_b', 'L0_mix_vln_g', 'L0_mix_vln_b', 'L0_mix_w1', 'L0_mix_b1', 'L0_mix_w2', 'L0_mix_b2',
        'L0_ffn_gamma', 'L0_ffn_beta', 'L0_ffn_Wr', 'L0_ffn_br', 'L0_ffn_W1', 'L0_ffn_b1', 'L0_ffn_W2', 'L0_ffn_b2']


def kernel(**inputs):
    import numpy as _np
    import concourse.bacc as _bacc
    from concourse import mybir as _mybir
    from concourse.bass_utils import run_bass_kernel_spmd as _run

    nc = _bacc.Bacc("TRN2", target_bir_lowering=False, num_devices=1)
    arrays, args = {}, []
    for name in _INS:
        a = _np.ascontiguousarray(inputs[name])
        arrays[f"in_{name}_dram"] = a
        args.append(nc.dram_tensor(f"in_{name}_dram", a.shape, _mybir.dt.from_np(a.dtype), kind="ExternalInput").ap())
    out = nc.dram_tensor("out_0_dram", inputs["x"].shape, F32, kind="ExternalOutput").ap()
    gps_layer(nc, *args, out)
    r = _run(nc, [arrays], core_ids=[0])
    return r.results[0]["out_0_dram"]
```

```python
from contextlib import ExitStack, contextmanager

import concourse.bass as bass
from concourse import mybir

P = 128
F32 = mybir.dt.float32
I32 = mybir.dt.int32
U32 = mybir.dt.uint32
ALU = mybir.AluOpType
ACT = mybir.ActivationFunctionType
AX_X = mybir.AxisListType.X

EPS = 1e-5
SLOPE = 0.2
HEADS = 4
MH = 8
GB = 4
SB = GB * P
RING = 4


def gps_layer(nc, x, src, dst, gnn_W, att_src, att_dst, gnn_bias, w_qkv, b_qkv, kln_g, kln_b, vln_g, vln_b,
              w1, b1, w2, b2, gamma, beta, Wr, br, W1, fb1, W2, fb2, out):
    N, D = x.shape
    E = src.shape[0]
    NT = -(-N // P)
    TAIL = N - (NT - 1) * P
    FULL = NT - 1
    NSB = -(-E // SB)
    PAD = (NSB + 1) * SB - E
    NS = -(-(NSB + NT - 1) // RING) * RING
    NCH = -(-NS // P)
    C = D // HEADS
    HW_ = D + 2 * HEADS
    AW = D + HEADS
    KT = D // P
    HC = D // MH
    NE, _, H = W1.shape
    HK = H // P
    assert FULL % 2 == 0 and NSB <= 512 and NS // RING >= 3 and NCH <= NT

    REGION = (NT + 1) * P
    NBLK = -(-((2 * N + NE * (P - 1)) // P) // 2) * 2
    SPARE = NBLK - -(-2 * N // P)
    assert NBLK <= P and NBLK >= 6

    sent_dram = nc.dram_tensor("sent_dram", (NE * REGION + SPARE * P, D), F32).ap()
    done_dram = nc.dram_tensor("done_dram", (NBLK * P, D), F32).ap()
    block_table = nc.dram_tensor("block_table", (2, P), I32).ap()
    node_table = nc.dram_tensor("node_table", (NT * P, HW_), F32).ap()
    edge_src = nc.dram_tensor("edge_src", ((NSB + 1) * SB,), I32).ap()
    edge_dst = nc.dram_tensor("edge_dst", ((NSB + 1) * SB,), I32).ap()
    step_table = nc.dram_tensor("step_table", (2, NCH * P), I32).ap()
    xnT_dram = nc.dram_tensor("xnT_dram", (NT, P, KT, P), F32).ap()
    base_dram = nc.dram_tensor("base_dram", (NT * P, D), F32).ap()
    mixed_dram = nc.dram_tensor("mixed_dram", (NT * P, D), F32).ap()

    with ExitStack() as ctx:
        def sem(name):
            return ctx.enter_context(nc.semaphore(name))

        def sb(name, shape, dt=F32, c=ctx):
            return c.enter_context(nc.sbuf_tensor(name, shape, dt))

        ident = sb("ident", [P, P])
        node_ids = sb("node_ids", [P, NT])
        iota8 = sb("iota8", [P, NE])
        ones_row = sb("ones_row", [1, P])
        eps_col = sb("eps_col", [P, 1])
        W_ext = sb("W_ext", [P, KT, HW_])
        gnn_bias_b = sb("gnn_bias_b", [P, D])
        wqkv_s = sb("wqkv_s", [P, KT, 3 * D])
        bqkv_b = sb("bqkv_b", [P, 3 * D])
        w1_s = sb("w1_s", [P, KT, D])
        w2_s = sb("w2_s", [P, KT, D])
        b1_b = sb("b1_b", [P, D])
        b2_b = sb("b2_b", [P, D])
        ln_g = sb("ln_g", [P, 2, HC])
        ln_b = sb("ln_b", [P, 2, HC])
        head_mask = sb("head_mask", [P, P])
        weff = sb("weff", [P, KT, D])
        beff = sb("beff", [P, D])
        gam_b = sb("gam_b", [P, D])
        bet_b = sb("bet_b", [P, D])
        wr_s = sb("wr_s", [P, KT, NE])
        br_b = sb("br_b", [P, NE])
        acc = sb("acc", [P, NT, HW_])
        adm = sb("adm", [P, NT, 2 * HEADS])
        smax = sb("smax", [P, HEADS])
        smax_all = sb("smax_all", [P, HEADS])
        steps_row = sb("steps_row", [1, 2, NCH * P], I32)
        share = sb("share", [P, NT, 2])
        places_f = sb("places_f", [P, NT, 2])
        places = sb("places", [P, NT, 2], I32)
        choices = sb("choices", [P, NT, 2, NE])
        place_s = sb("place_s", [P, 2, 2], I32)
        seen = sb("seen", [P, NE])
        region = sb("region", [P, NE])
        blocks_row = sb("blocks_row", [1, 2, P], I32)
        xin = sb("xin", [P, 2, D])
        xn = sb("xn", [P, 2, D])
        xnT = sb("xnT", [P, 2, KT, P])
        stats = sb("stats", [P, 2, 6])
        mv = sb("mv", [P, 2, 2])
        std = sb("std", [P, 2, 1])
        rstd = sb("rstd", [P, 2, 1])

        psA = [ctx.enter_context(nc.psum_tensor(f"psA{q}", [P, 512], F32)) for q in range(2)]
        psB = [ctx.enter_context(nc.psum_tensor(f"psB{q}", [P, 512], F32)) for q in range(2)]
        psC = [ctx.enter_context(nc.psum_tensor(f"psC{q}", [P, 512], F32)) for q in range(2)]
        psD = [ctx.enter_context(nc.psum_tensor(f"psD{q}", [P, 512], F32)) for q in range(2)]

        loads_done = sem("loads_done")
        act_gate, dve_gate, pool_gate = sem("act_gate"), sem("dve_gate"), sem("pool_gate")

        LOADS = [
            (W_ext[:, :, 0:D], gnn_W.rearrange("(k p) n -> p k n", p=P)),
            (gnn_bias_b[:], gnn_bias.partition_broadcast(P)),
            (wqkv_s[:], w_qkv.rearrange("(k p) n -> p k n", p=P)),
            (bqkv_b[:], b_qkv.partition_broadcast(P)),
            (w1_s[:], w1.rearrange("(k p) n -> p k n", p=P)),
            (w2_s[:], w2.rearrange("(k p) n -> p k n", p=P)),
            (b1_b[:], b1.partition_broadcast(P)),
            (b2_b[:], b2.partition_broadcast(P)),
            (ln_g[:, 0], kln_g.partition_broadcast(P)),
            (ln_g[:, 1], vln_g.partition_broadcast(P)),
            (ln_b[:, 0], kln_b.partition_broadcast(P)),
            (ln_b[:, 1], vln_b.partition_broadcast(P)),
            (gam_b[:], gamma.partition_broadcast(P)),
            (bet_b[:], beta.partition_broadcast(P)),
            (wr_s[:], Wr.rearrange("(k p) n -> p k n", p=P)),
            (br_b[:], br.partition_broadcast(P)),
        ]


        @contextmanager
        def phase():
            own = []

            def phase_sem(name):
                own.append(nc.alloc_semaphore(name))
                return own[-1]

            with ExitStack() as ph:
                yield ph, phase_sem
            nc.clear_and_free_semaphores(own)
            nc.all_engine_barrier()

        def each_tile(eng, body):
            for i in range(2):
                body(i, i % 2, P, 0)
            with eng.Fori(1, FULL // 2 - 1) as it:
                for q in range(2):
                    body(it * 2 + q, q, P, it)
            for i in range(FULL - 2, FULL):
                body(i, i % 2, P, i // 2)
            body(FULL, 0, TAIL, FULL // 2)

        def later(i, n):
            return not (isinstance(i, int) and i < n)

        def has_next(i):
            return not (isinstance(i, int) and i == FULL)

        def next_tile(i, q, it):
            return i + 1, 1 - q, TAIL if isinstance(i, int) and i + 1 == FULL else P, it + q

        def node_rows(i, rows):
            return bass.ds(i * P, rows)

        with phase() as (ph, sem):
            att_b = sb("att_b", [P, 2, D], c=ph)
            att_prod = sb("att_prod", [P, KT, D], c=ph)
            pad_row = sb("pad_row", [1, 2, PAD], I32, c=ph)
            last_dst = sb("last_dst", [1, NSB], I32, c=ph)
            last_tile = sb("last_tile", [1, NSB], I32, c=ph)
            last_step = sb("last_step", [1, NSB], c=ph)
            sb_ids = sb("sb_ids", [1, NSB], c=ph)
            below = sb("below", [P, NSB], c=ph)
            sb_done = sb("sb_done", [P, NCH], c=ph)
            tile_of = sb("tile_of", [P, NCH], c=ph)
            steps_i = sb("steps_i", [P, 2, NCH], I32, c=ph)
            pads_set, edges_in, last_in = sem("pads_set"), sem("edges_in"), sem("last_in")
            consts_set, ident_zero, rows_set = sem("consts_set"), sem("ident_zero"), sem("rows_set")
            att_prod_ready, att_cols_ready = sem("att_prod_ready"), sem("att_cols_ready")
            last_tile_ready, last_step_ready, last_step_spread = sem("last_tile_ready"), sem("last_step_ready"), sem("last_step_spread")
            sb_done_ready, tile_of_ready = sem("sb_done_ready"), sem("tile_of_ready")
            steps_ready, steps_out, steps_in, mask_zero = sem("steps_ready"), sem("steps_out"), sem("steps_in"), sem("mask_zero")
            NLOADS = len(LOADS) + 2

            with nc.Block() as block:
                @block.sync
                def _(sp):
                    sp.dma_start(edge_src[0:E], src).then_inc(edges_in, 16)
                    sp.dma_start(edge_dst[0:E], dst).then_inc(edges_in, 16)
                    sp.wait_ge(pads_set, 2)
                    sp.dma_start(edge_src[E:E + PAD].unsqueeze(0), pad_row[:, 0]).then_inc(edges_in, 16)
                    sp.dma_start(edge_dst[E:E + PAD].unsqueeze(0), pad_row[:, 1]).then_inc(edges_in, 16)
                    sp.wait_ge(edges_in, 64)
                    sp.dma_start(last_dst[:], edge_dst.rearrange("(b e) -> e b", e=SB)[SB - 1:SB, 0:NSB],
                                 allow_slow_non_contiguous=True).then_inc(last_in, 16)
                    sp.wait_ge(steps_ready, 2)
                    for w in range(2):
                        sp.dma_start(step_table[w].rearrange("(c p) -> p c", p=P), steps_i[:, w],
                                     allow_slow_non_contiguous=True).then_inc(steps_out, 16)
                    sp.wait_ge(steps_out, 32)
                    sp.dma_start(steps_row[:], step_table.unsqueeze(0)).then_inc(steps_in, 16)
                    sp.wait_ge(steps_in, 16)

                @block.scalar
                def _(act):
                    for w, a in enumerate((att_src, att_dst)):
                        act.dma_start(att_b[:, w], a.rearrange("h c -> (h c)").partition_broadcast(P)).then_inc(loads_done, 16)
                    for to, frm in LOADS:
                        act.dma_start(to, frm).then_inc(loads_done, 16)
                    act.wait_ge(loads_done, 16 * NLOADS)

                @block.gpsimd
                def _(pool):
                    pool.memset(ident[:], 0.0).then_inc(ident_zero, 1)
                    for ids, step, mult in ((node_ids, P, 1), (sb_ids, 1, 0), (iota8, 1, 0)):
                        pool.iota(ids[:], pattern=[[step, ids.shape[1]]], base=0, channel_multiplier=mult,
                                  allow_small_or_imprecise_dtypes=True).then_inc(consts_set, 1)
                    pool.wait_ge(ident_zero, 1)
                    pool.affine_select(out=ident[:], in_=ident[:], compare_op=ALU.not_equal, fill=1.0, base=0,
                                       pattern=[[-1, P]], channel_multiplier=1).then_inc(consts_set, 1)

                @block.tensor
                def _(pe):
                    pe.wait_ge(rows_set, 1)
                    pe.wait_ge(last_step_ready, 1)
                    pe.matmul(psA[0][:, 0:NSB], ones_row[:], last_step[:], start=True, stop=True).then_inc(last_step_spread, 1)

                @block.vector
                def _(dve):
                    dve.memset(pad_row[:, 0], 0).then_inc(pads_set, 1)
                    dve.memset(pad_row[:, 1], NT * P).then_inc(pads_set, 1)
                    dve.memset(ones_row[:], 1.0).then_inc(rows_set, 1)
                    dve.memset(eps_col[:], EPS)
                    dve.memset(acc[:, NT - 1], 0.0)
                    dve.memset(head_mask[:], 0.0).then_inc(mask_zero, 1)
                    dve.wait_ge(mask_zero, 1)
                    for j in range(P // HC):
                        dve.memset(head_mask[HC * j:HC * (j + 1), HC * j:HC * (j + 1)], 1.0 / N)
                    dve.wait_ge(loads_done, 16 * NLOADS)
                    for w in range(2):
                        if w:
                            dve.wait_ge(att_cols_ready, 1)
                        dve.tensor_tensor(att_prod[:], W_ext[:, :, 0:D], att_b[:, w].unsqueeze(1).broadcast_to([P, KT, D]),
                                          ALU.mult).then_inc(att_prod_ready, 1)
                        dve.wait_ge(att_prod_ready, w + 1)
                        for k in range(KT):
                            last = dve.tensor_reduce(W_ext[:, k, D + HEADS * w:D + HEADS * (w + 1)],
                                                     att_prod[:, k].rearrange("p (h c) -> p h c", h=HEADS), AX_X, ALU.add)
                        last.then_inc(att_cols_ready, 1)
                    dve.wait_ge(last_in, 16)
                    dve.tensor_scalar(last_tile[:], last_dst[:], P.bit_length() - 1, None,
                                      ALU.logical_shift_right).then_inc(last_tile_ready, 1)
                    dve.wait_ge(last_tile_ready, 1)
                    dve.wait_ge(consts_set, 4)
                    dve.scalar_tensor_tensor(out=last_step[:], in0=last_tile[:], scalar=float(NT - 1), in1=sb_ids[:],
                                             op0=ALU.min, op1=ALU.add).then_inc(last_step_ready, 1)
                    dve.wait_ge(last_step_spread, 1)
                    for c in range(NCH):
                        last = dve.tensor_scalar(below[:], psA[0][:, 0:NSB], node_ids[:, c:c + 1], 0.0, ALU.is_lt, ALU.add,
                                                 accum_out=sb_done[:, c:c + 1])
                        last.then_inc(sb_done_ready, 1)
                        dve.wait_ge(sb_done_ready, c + 1)
                    dve.tensor_tensor(tile_of[:], node_ids[:, 0:NCH], sb_done[:], ALU.subtract).then_inc(tile_of_ready, 1)
                    dve.tensor_copy(steps_i[:, 0], sb_done[:]).then_inc(steps_ready, 1)
                    dve.wait_ge(tile_of_ready, 1)
                    dve.tensor_scalar(steps_i[:, 1], tile_of[:], float(NT - 1), None, ALU.min).then_inc(steps_ready, 1)

        with phase() as (ph, sem):
            kvx = sb("kvx", [P, 2, MH, 2 * HC], c=ph)
            kvc = sb("kvc", [P, 2, MH, 2 * HC], c=ph)
            kvsq = sb("kvsq", [P, 2, MH, 2 * HC], c=ph)
            kvo = sb("kvo", [P, 2, 2, MH, HC], c=ph)
            kvsum = sb("kvsum", [P, 2, 2 * MH], c=ph)
            kvvar = sb("kvvar", [P, 2, 2 * MH], c=ph)
            kvstd = sb("kvstd", [P, 2, 2 * MH], c=ph)
            kvrstd = sb("kvrstd", [P, 2, 2 * MH], c=ph)
            base = sb("base1", [P, 2, D], c=ph)
            x_in = [sem("x_in0"), sem("x_in1")]
            xnT_out = [sem("xnT_out0"), sem("xnT_out1")]
            base_out = [sem("base_out0"), sem("base_out1")]
            table_out = sem("table_out")
            stats_ready, mv_ready, std_ready, rstd_ready, xn_ready = (sem(n) for n in ("stats_ready", "mv_ready", "std_ready", "rstd_ready", "xn_ready"))
            base_sum, base_ready, turned, xnT_ready = sem("base_sum"), sem("base_ready"), sem("turned"), sem("xnT_ready")
            h_done, h_copied, kv_done, kv_biased = sem("h_done"), sem("h_copied"), sem("kv_done"), sem("kv_biased")
            kv_summed, kv_centred, kv_squared, kv_var_ready = sem("kv_summed"), sem("kv_centred"), sem("kv_squared"), sem("kv_var_ready")
            kv_std_ready, kv_rstd_ready, kv_normed, kv_scaled, kvo_ready, kvo_used = (sem(n) for n in (
                "kv_std_ready", "kv_rstd_ready", "kv_normed", "kv_scaled", "kvo_ready", "kvo_used"))
            with nc.Block() as block:
                @block.sync
                def _(sp):
                    def load_x(i, q, rows):
                        sp.dma_start(xin[0:rows, q], x[node_rows(i, rows)]).then_inc(x_in[q], 16)

                    def tile(i, q, rows, it):
                        sp.wait_ge(base_ready, i + 1)
                        if not (isinstance(i, int) and i + 2 > FULL):
                            load_x(i + 2, q, TAIL if isinstance(i, int) and i + 2 == FULL else P)
                        sp.dma_start(base_dram[node_rows(i, rows)], base[0:rows, q]).then_inc(base_out[q], 16)
                        sp.wait_ge(xnT_ready, i + 1)
                        sp.dma_start(xnT_dram[bass.ds(i, 1), :, :, 0:rows].rearrange("o p k n -> p (o k) n"),
                                     xnT[:, q, :, 0:rows]).then_inc(xnT_out[q], 16)
                        sp.wait_ge(h_copied, i + 1)
                        sp.dma_start(node_table[node_rows(i, P)].unsqueeze(1), acc[:, bass.ds(i, 1)]).then_inc(table_out, 16)

                    for i in range(2):
                        load_x(i, i, P)
                    each_tile(sp, tile)
                    sp.wait_ge(table_out, 16 * NT)
                    for q in range(2):
                        sp.wait_ge(xnT_out[q], 16 * (NT // 2 + (1 - q)))
                        sp.wait_ge(base_out[q], 16 * (NT // 2 + (1 - q)))

                @block.vector
                def _(dve):
                    def normalise(i, q, rows, it):
                        if later(i, 2):
                            dve.wait_ge(turned, i - 1)
                        dve.wait_ge(x_in[q], it * 16 + 16)
                        dve.bn_stats(stats[0:rows, q], xin[0:rows, q]).then_inc(stats_ready, 1)
                        dve.wait_ge(stats_ready, i + 1)
                        dve.sem_inc(dve_gate, 1)
                        dve.bn_aggr(mv[0:rows, q], stats[0:rows, q]).then_inc(mv_ready, 1)
                        dve.wait_ge(std_ready, i + 1)
                        dve.reciprocal(rstd[0:rows, q], std[0:rows, q]).then_inc(rstd_ready, 1)
                        dve.wait_ge(rstd_ready, i + 1)
                        dve.tensor_scalar(xn[0:rows, q], xin[0:rows, q], mv[0:rows, q, 0:1], rstd[0:rows, q],
                                          ALU.subtract, ALU.mult).then_inc(xn_ready, 1)
                        dve.wait_ge(xn_ready, i + 1)
                        if later(i, 2):
                            dve.wait_ge(base_out[q], it * 16)
                        dve.tensor_tensor(base[0:rows, q], xin[0:rows, q], xn[0:rows, q], ALU.add).then_inc(base_sum, 1)
                        dve.wait_ge(base_sum, i + 1)
                        dve.tensor_tensor(base[0:rows, q], base[0:rows, q], b2_b[0:rows], ALU.add).then_inc(base_ready, 1)

                    def keys_values(i, q, rows):
                        groups = lambda t: t[0:rows, q].rearrange("p h (s c) -> p (h s) c", s=2)
                        spread = lambda t: t[0:rows, q].unsqueeze(2).broadcast_to([rows, 2 * MH, HC])
                        heads = lambda t: t[0:rows].rearrange("p s c -> p (s c)").unsqueeze(1).broadcast_to([rows, MH, 2 * HC])
                        dve.wait_ge(kv_done, i + 1)
                        dve.tensor_tensor(kvx[0:rows, q], psC[q][0:rows, :].rearrange("p (h c) -> p h c", h=MH),
                                          bqkv_b[0:rows].rearrange("p (h c) -> p h c", h=MH)[:, :, HC:3 * HC],
                                          ALU.add).then_inc(kv_biased, 1)
                        dve.wait_ge(kv_biased, i + 1)
                        dve.tensor_reduce(kvsum[0:rows, q], groups(kvx), AX_X, ALU.add).then_inc(kv_summed, 1)
                        dve.wait_ge(kv_summed, i + 1)
                        dve.scalar_tensor_tensor(out=groups(kvc), in0=spread(kvsum), scalar=-1.0 / HC, in1=groups(kvx),
                                                 op0=ALU.mult, op1=ALU.add).then_inc(kv_centred, 1)
                        dve.wait_ge(kv_squared, i + 1)
                        dve.tensor_reduce(kvvar[0:rows, q], groups(kvsq), AX_X, ALU.add).then_inc(kv_var_ready, 1)
                        dve.wait_ge(kv_std_ready, i + 1)
                        dve.reciprocal(kvrstd[0:rows, q], kvstd[0:rows, q]).then_inc(kv_rstd_ready, 1)
                        dve.wait_ge(kv_rstd_ready, i + 1)
                        dve.tensor_tensor(groups(kvx), groups(kvc), spread(kvrstd), ALU.mult).then_inc(kv_normed, 1)
                        dve.wait_ge(kv_normed, i + 1)
                        dve.tensor_tensor(kvc[0:rows, q], kvx[0:rows, q], heads(ln_g), ALU.mult).then_inc(kv_scaled, 1)
                        dve.wait_ge(kv_scaled, i + 1)
                        if later(i, 2):
                            dve.wait_ge(kvo_used, i - 1)
                        dve.tensor_tensor(kvo[0:rows, q].rearrange("p s h c -> p h s c"),
                                          kvc[0:rows, q].rearrange("p h (s c) -> p h s c", s=2),
                                          ln_b[0:rows].unsqueeze(1).broadcast_to([rows, MH, 2, HC]),
                                          ALU.add).then_inc(kvo_ready, 1)

                    def tile(i, q, rows, it):
                        if has_next(i):
                            normalise(*next_tile(i, q, it))
                        dve.wait_ge(h_done, i + 1)
                        dve.tensor_scalar(acc[0:rows, bass.ds(i, 1)], psB[q][0:rows, 0:HW_].unsqueeze(1), 1.0, None,
                                          ALU.mult).then_inc(h_copied, 1)
                        keys_values(i, q, rows)

                    normalise(0, 0, P, 0)
                    each_tile(dve, tile)

                @block.scalar
                def _(act):
                    def root_and_turn(i, q, rows, it):
                        act.wait_ge(mv_ready, i + 1)
                        act.activation(std[0:rows, q], mv[0:rows, q, 1:2], ACT.Sqrt, bias=eps_col[0:rows]).then_inc(std_ready, 1)
                        act.wait_ge(turned, i + 1)
                        if later(i, 2):
                            act.wait_ge(xnT_out[q], it * 16)
                            act.wait_ge(kv_done, i - 1)
                        act.activation(xnT[:, q, :, 0:rows], psA[q][:, 0:KT * P].rearrange("p (k n) -> p k n", k=KT)[:, :, 0:rows],
                                       ACT.Copy).then_inc(xnT_ready, 1)

                    def tile(i, q, rows, it):
                        if has_next(i):
                            root_and_turn(*next_tile(i, q, it))
                        act.wait_ge(kv_centred, i + 1)
                        act.activation(kvsq[0:rows, q], kvc[0:rows, q], ACT.Square).then_inc(kv_squared, 1)
                        act.wait_ge(kv_var_ready, i + 1)
                        act.activation(kvstd[0:rows, q], kvvar[0:rows, q], ACT.Sqrt, bias=eps_col[0:rows],
                                       scale=1.0 / HC).then_inc(kv_std_ready, 1)

                    root_and_turn(0, 0, P, 0)
                    each_tile(act, tile)

                @block.tensor
                def _(pe):
                    def key_value_product(i, q, rows):
                        pe.wait_ge(kvo_ready, i + 1)
                        for hf in range(KT):
                            k, v = (kvo[0:rows, q, s].rearrange("p h c -> p (h c)")[:, hf * P:(hf + 1) * P] for s in range(2))
                            last = pe.matmul(psD[hf][:, 0:P], k, v, start=not later(i, 1), stop=isinstance(i, int) and i == FULL,
                                             skip_group_check=True)
                        last.then_inc(kvo_used, 1)

                    def turn(i, q, rows, it):
                        pe.wait_ge(xn_ready, i + 1)
                        if later(i, 2):
                            pe.wait_ge(xnT_ready, i - 1)
                        for k in range(KT):
                            last = pe.transpose(psA[q][:, k * P:k * P + rows], xn[0:rows, q, k * P:(k + 1) * P],
                                                ident[0:rows, 0:rows])
                        last.then_inc(turned, 1)

                    def tile(i, q, rows, it):
                        pe.wait_ge(xnT_ready, i + 1)
                        if later(i, 2):
                            pe.wait_ge(h_copied, i - 1)
                        for k in range(KT):
                            last = pe.matmul(psB[q][0:rows, 0:HW_], xnT[:, q, k, 0:rows], W_ext[:, k],
                                             start=(k == 0), stop=(k == KT - 1))
                        last.then_inc(h_done, 1)
                        if later(i, 2):
                            pe.wait_ge(kv_biased, i - 1)
                        for k in range(KT):
                            last = pe.matmul(psC[q][0:rows, :], xnT[:, q, k, 0:rows],
                                             wqkv_s[:, k].rearrange("p (h c) -> p h c", h=MH)[:, :, HC:3 * HC],
                                             start=(k == 0), stop=(k == KT - 1))
                        last.then_inc(kv_done, 1)
                        if has_next(i):
                            turn(*next_tile(i, q, it))
                        if later(i, 1):
                            key_value_product(i - 1, 1 - q, P)

                    turn(0, 0, P, 0)
                    each_tile(pe, tile)
                    key_value_product(FULL, 0, TAIL)

        with phase() as (ph, sem):
            wq_c = sb("wq_c", [P, KT, D], c=ph)
            bq_c = sb("bq_c", [1, D], c=ph)
            wqT = sb("wqT", [P, KT, D], c=ph)
            kvm = sb("kvm", [P, KT, P], c=ph)
            bq_col = sb("bq_col", [P, KT], c=ph)
            qkvT = sb("qkvT", [P, KT, D], c=ph)
            bq_kv = sb("bq_kv", [P, KT, P], c=ph)
            za = sb("za", [P, NT, HEADS], c=ph)
            zl = sb("zl", [P, NT, HEADS], c=ph)
            p_self = sb("p_self", [P, NT, HEADS], c=ph)
            wq_ready, wq_turned, wqT_ready, kvm_ready = sem("wq_ready"), sem("wq_turned"), sem("wqT_ready"), sem("kvm_ready")
            bq_turned, bq_col_ready, qkv_done, qkvT_ready = sem("bq_turned"), sem("bq_col_ready"), sem("qkv_done"), sem("qkvT_ready")
            weff_done, beff_done, bq_kv_done, bq_kv_ready, folded = (sem(n) for n in ("weff_done", "beff_done", "bq_kv_done", "bq_kv_ready", "folded"))
            smax_ready, smax_spread, adm_part, self_part, p_self_ready = (sem(n) for n in ("smax_ready", "smax_spread", "adm_part", "self_part", "p_self_ready"))
            with nc.Block() as block:
                @block.gpsimd
                def _(pool):
                    pool.wait_ge(smax_ready, 1)
                    pool.partition_all_reduce(smax_all[:], smax[:], P, bass.bass_isa.ReduceOp.max).then_inc(smax_spread, 1)

                @block.scalar
                def _(act):
                    act.wait_ge(self_part, 3)
                    act.activation(p_self[:], za[:], ACT.Exp).then_inc(p_self_ready, 1)

                @block.tensor
                def _(pe):
                    pe.wait_ge(wq_ready, 2)
                    for hf in range(KT):
                        for k in range(KT):
                            last = pe.transpose(psA[hf][:, k * P:(k + 1) * P], wq_c[:, k, hf * P:(hf + 1) * P], ident[:])
                    last.then_inc(wq_turned, 1)
                    for hf in range(KT):
                        last = pe.matmul(psC[0][:, hf:hf + 1], bq_c[:, hf * P:(hf + 1) * P], ones_row[:, 0:1], start=True, stop=True)
                    last.then_inc(bq_turned, 1)
                    pe.wait_ge(wqT_ready, 2)
                    pe.wait_ge(kvm_ready, 2)
                    for hf in range(KT):
                        last = pe.matmul(psB[hf][:, 0:D], kvm[:, hf], wqT[:, hf], start=True, stop=True)
                    last.then_inc(qkv_done, 1)
                    pe.wait_ge(bq_col_ready, 1)
                    for hf in range(KT):
                        last = pe.matmul(psC[1][:, hf:hf + 1], kvm[:, hf], bq_col[:, hf:hf + 1], start=True, stop=True)
                    last.then_inc(bq_kv_done, 1)
                    pe.wait_ge(qkvT_ready, 2)
                    for c in range(KT):
                        for hf in range(KT):
                            last = pe.matmul(psA[c][:, 0:D], qkvT[:, hf, c * P:(c + 1) * P], w1_s[:, hf], start=(hf == 0), stop=(hf == KT - 1))
                    last.then_inc(weff_done, 1)
                    pe.wait_ge(bq_kv_ready, 2)
                    for hf in range(KT):
                        last = pe.matmul(psC[0][:, 0:D], bq_kv[:, hf], w1_s[:, hf], start=(hf == 0), stop=(hf == KT - 1))
                    last.then_inc(beff_done, 1)

                @block.vector
                def _(dve):
                    dve.tensor_copy(wq_c[:].rearrange("p k (h c) -> p k h c", h=MH),
                                    wqkv_s[:].rearrange("p k (h c) -> p k h c", h=MH)[:, :, :, 0:HC]).then_inc(wq_ready, 1)
                    dve.tensor_copy(bq_c[:].rearrange("p (h c) -> p h c", h=MH),
                                    bqkv_b[0:1].rearrange("p (h c) -> p h c", h=MH)[:, :, 0:HC]).then_inc(wq_ready, 1)
                    for hf in range(KT):
                        dve.tensor_tensor(kvm[:, hf], psD[hf][:, 0:P], head_mask[:], ALU.mult).then_inc(kvm_ready, 1)
                    dve.wait_ge(wq_turned, 1)
                    for hf in range(KT):
                        dve.tensor_copy(wqT[:, hf], psA[hf][:, 0:D]).then_inc(wqT_ready, 1)
                    dve.wait_ge(bq_turned, 1)
                    dve.tensor_copy(bq_col[:], psC[0][:, 0:KT]).then_inc(bq_col_ready, 1)
                    dve.wait_ge(qkv_done, 1)
                    for hf in range(KT):
                        dve.tensor_copy(qkvT[:, hf], psB[hf][:, 0:D]).then_inc(qkvT_ready, 1)
                    dve.wait_ge(bq_kv_done, 1)
                    for hf in range(KT):
                        dve.tensor_copy(bq_kv[:, hf], psC[1][:, hf:hf + 1].broadcast_to([P, P])).then_inc(bq_kv_ready, 1)
                    dve.wait_ge(weff_done, 1)
                    for c in range(KT):
                        dve.tensor_tensor(weff[:, c], psA[c][:, 0:D], w1_s[:, c], ALU.add).then_inc(folded, 1)
                    dve.wait_ge(beff_done, 1)
                    dve.tensor_tensor(beff[:], psC[0][:, 0:D], b1_b[:], ALU.add).then_inc(folded, 1)
                    a_src, a_dst = acc[:, :, D:D + HEADS], acc[:, :, D + HEADS:HW_]
                    dve.tensor_reduce(smax[:], a_src.rearrange("p t h -> p h t"), AX_X, ALU.max).then_inc(smax_ready, 1)
                    dve.tensor_copy(adm[:, :, 0:HEADS], a_dst).then_inc(adm_part, 1)
                    dve.wait_ge(smax_spread, 1)
                    dve.tensor_tensor(za[:], a_dst, smax_all[:].unsqueeze(1).broadcast_to([P, NT, HEADS]), ALU.add).then_inc(adm_part, 1)
                    dve.wait_ge(adm_part, 2)
                    dve.scalar_tensor_tensor(out=adm[:, :, HEADS:2 * HEADS], in0=za[:], scalar=SLOPE, in1=za[:],
                                             op0=ALU.mult, op1=ALU.max).then_inc(adm_part, 1)
                    dve.wait_ge(adm_part, 3)
                    dve.tensor_tensor(za[:], a_src, a_dst, ALU.add).then_inc(self_part, 1)
                    dve.wait_ge(self_part, 1)
                    dve.scalar_tensor_tensor(out=zl[:], in0=za[:], scalar=SLOPE, in1=za[:],
                                             op0=ALU.mult, op1=ALU.max).then_inc(self_part, 1)
                    dve.wait_ge(self_part, 2)
                    dve.tensor_tensor(za[:], zl[:], adm[:, :, HEADS:2 * HEADS], ALU.subtract).then_inc(self_part, 1)
                    dve.wait_ge(p_self_ready, 1)
                    h_v = acc[:, :, 0:D].rearrange("p t (h c) -> p t h c", h=HEADS)
                    for t in range(NT):
                        dve.tensor_tensor(h_v[:, t], h_v[:, t], p_self[:, t].unsqueeze(2).broadcast_to([P, HEADS, C]), ALU.mult)
                    dve.tensor_copy(acc[:, :, D:AW], p_self[:])

        with phase() as (ph, sem):
            base = sb("base2", [P, 2, D], c=ph)
            mixed = sb("mixed2", [P, 2, D], c=ph)
            hpre = sb("hpre", [P, 2, D], c=ph)
            hid = sb("hid", [P, 2, D], c=ph)
            hidT = sb("hidT", [P, 2, KT, P], c=ph)
            m_xnT_in, m_base_in, m_out = ([sem(f"{n}{q}") for q in range(2)] for n in ("m_xnT_in", "m_base_in", "m_out"))
            up_done, up_biased, gelu_done, hid_turned, hidT_ready, down_done, mixed_ready = (sem(n) for n in (
                "up_done", "up_biased", "gelu_done", "hid_turned", "hidT_ready", "down_done", "mixed_ready"))
            with nc.Block() as block:
                @block.sync
                def _(sp):
                    def load(i, q, rows):
                        if later(i, 2):
                            sp.wait_ge(mixed_ready, i - 1)
                        sp.dma_start(xnT[:, q, :, 0:rows], xnT_dram[bass.ds(i, 1), :, :, 0:rows].rearrange("o p k n -> p (o k) n")
                                     ).then_inc(m_xnT_in[q], 16)
                        sp.dma_start(base[0:rows, q], base_dram[node_rows(i, rows)]).then_inc(m_base_in[q], 16)

                    def tile(i, q, rows, it):
                        sp.wait_ge(mixed_ready, i + 1)
                        sp.dma_start(mixed_dram[node_rows(i, rows)], mixed[0:rows, q]).then_inc(m_out[q], 16)
                        if isinstance(i, int) and i + 2 > FULL:
                            return
                        load(i + 2, q, TAIL if isinstance(i, int) and i + 2 == FULL else P)

                    for i in range(2):
                        load(i, i, P)
                    each_tile(sp, tile)
                    for q in range(2):
                        sp.wait_ge(m_out[q], 16 * (NT // 2 + (1 - q)))

                @block.tensor
                def _(pe):
                    def tile(i, q, rows, it):
                        pe.wait_ge(m_xnT_in[q], it * 16 + 16)
                        if later(i, 2):
                            pe.wait_ge(up_biased, i - 1)
                        for k in range(KT):
                            last = pe.matmul(psA[q][0:rows, 0:D], xnT[:, q, k, 0:rows], weff[:, k], start=(k == 0), stop=(k == KT - 1))
                        last.then_inc(up_done, 1)
                        pe.wait_ge(gelu_done, i + 1)
                        if later(i, 2):
                            pe.wait_ge(hidT_ready, i - 1)
                        for k in range(KT):
                            last = pe.transpose(psB[q][:, k * P:k * P + rows], hid[0:rows, q, k * P:(k + 1) * P], ident[0:rows, 0:rows])
                        last.then_inc(hid_turned, 1)
                        pe.wait_ge(hidT_ready, i + 1)
                        if later(i, 2):
                            pe.wait_ge(mixed_ready, i - 1)
                        for k in range(KT):
                            last = pe.matmul(psC[q][0:rows, 0:D], hidT[:, q, k, 0:rows], w2_s[:, k], start=(k == 0), stop=(k == KT - 1))
                        last.then_inc(down_done, 1)

                    each_tile(pe, tile)

                @block.scalar
                def _(act):
                    def tile(i, q, rows, it):
                        act.wait_ge(up_biased, i + 1)
                        if later(i, 2):
                            act.wait_ge(hid_turned, i - 1)
                        act.activation(hid[0:rows, q], hpre[0:rows, q], ACT.Gelu).then_inc(gelu_done, 1)
                        act.wait_ge(hid_turned, i + 1)
                        if later(i, 2):
                            act.wait_ge(down_done, i - 1)
                        act.activation(hidT[:, q, :, 0:rows], psB[q][:, 0:KT * P].rearrange("p (k n) -> p k n", k=KT)[:, :, 0:rows],
                                       ACT.Copy).then_inc(hidT_ready, 1)

                    each_tile(act, tile)

                @block.vector
                def _(dve):
                    def tile(i, q, rows, it):
                        dve.wait_ge(up_done, i + 1)
                        if later(i, 2):
                            dve.wait_ge(gelu_done, i - 1)
                        dve.tensor_tensor(hpre[0:rows, q], psA[q][0:rows, 0:D], beff[0:rows], ALU.add).then_inc(up_biased, 1)
                        dve.wait_ge(down_done, i + 1)
                        dve.wait_ge(m_base_in[q], it * 16 + 16)
                        if later(i, 2):
                            dve.wait_ge(m_out[q], it * 16)
                        dve.tensor_tensor(mixed[0:rows, q], psC[q][0:rows, 0:D], base[0:rows, q], ALU.add).then_inc(mixed_ready, 1)

                    each_tile(dve, tile)

        with phase() as (ph, sem):
            iota_all = sb("iota_all", [P, NT * P], c=ph)
            iota_set = sem("iota_set")
            ps_sum = [psB[0], psB[1], psC[0], psC[1]]
            src_idx = sb("src_idx", [P, RING, GB], I32, c=ph)
            dst_col = sb("dst_col", [P, RING, GB], I32, c=ph)
            dst_row = sb("dst_row", [P, RING, SB], I32, c=ph)
            rows_g = sb("rows_g", [P, RING, GB, HW_], c=ph)
            pick_e = sb("pick_e", [P, RING, GB, P], c=ph)
            pick_n = sb("pick_n", [P, 2, SB], c=ph)
            ze = sb("ze", [P, 2, GB, HEADS], c=ph)
            zle = sb("zle", [P, 2, GB, HEADS], c=ph)
            ye = sb("ye", [P, 2, GB, HEADS], c=ph)
            pe_h = sb("pe_h", [P, RING, GB, AW], c=ph)
            idx_in, dst_in, row_in, gathered = ([sem(f"{n}{r}") for r in range(RING)] for n in ("idx_in", "dst_in", "row_in", "gathered"))
            pick_e_ready, pick_n_ready, picked, z_ready, zl_ready, y_ready, p_ready, ph_ready, summed, added = (sem(n) for n in (
                "pick_e_ready", "pick_n_ready", "picked", "z_ready", "zl_ready", "y_ready", "p_ready", "ph_ready", "summed", "added"))
            src_v = edge_src.rearrange("(b p j) -> b p j", p=P, j=GB)
            dst_v = edge_dst.rearrange("(b p j) -> b p j", p=P, j=GB)

            def each_step(eng, body):
                for s in range(RING):
                    body(s, s, 0)
                with eng.Fori(1, NS // RING - 1) as it:
                    for r in range(RING):
                        body(it * RING + r, r, it)
                for s in range(NS - RING, NS):
                    body(s, s % RING, s // RING)

            def step_value(eng, w, s, top):
                return eng.value_load(steps_row[0:1, w, bass.ds(s, 1)], min_val=0, max_val=top)

            with nc.Block() as block:
                @block.sync
                def _(sp):
                    def step(s, r, it):
                        b = step_value(sp, 0, s, NSB)
                        if later(s, RING):
                            sp.wait_ge(gathered[r], it * (16 * GB))
                        sp.dma_start(src_idx[:, r].unsqueeze(1), src_v[bass.ds(b, 1)].rearrange("b p j -> p b j")).then_inc(idx_in[r], 16)
                        if later(s, RING):
                            sp.wait_ge(pick_e_ready, s - (RING - 1))
                            sp.wait_ge(pick_n_ready, s - (RING - 1))
                        sp.dma_start(dst_col[:, r].unsqueeze(1), dst_v[bass.ds(b, 1)].rearrange("b p j -> p b j")).then_inc(dst_in[r], 16)
                        sp.dma_start(dst_row[:, r], edge_dst[bass.ds(b * SB, SB)].partition_broadcast(P)).then_inc(row_in[r], 16)

                    each_step(sp, step)

                @block.gpsimd
                def _(pool):
                    def step(s, r, it):
                        if later(s, RING):
                            pool.wait_ge(ph_ready, s - (RING - 1))
                        pool.wait_ge(idx_in[r], it * 16 + 16)
                        pool.sem_inc(pool_gate, 1)
                        for j in range(GB):
                            pool.indirect_dma_start(out=rows_g[:, r, j], out_offset=None, in_=node_table,
                                                    in_offset=bass.IndirectOffsetOnAxis(ap=src_idx[:, r, j:j + 1], axis=0)
                                                    ).then_inc(gathered[r], 16)

                    pool.iota(iota_all[:], pattern=[[1, NT * P]], base=0, channel_multiplier=0,
                              allow_small_or_imprecise_dtypes=True).then_inc(iota_set, 1)
                    each_step(pool, step)

                @block.vector
                def _(dve):
                    def picks(s, r, it):
                        t = step_value(dve, 1, s, NT - 1)
                        q = r % 2
                        dve.wait_ge(row_in[r], it * 16 + 16)
                        if later(s, 2):
                            dve.wait_ge(picked, s - 1)
                        dve.tensor_scalar(pick_n[:, q], dst_row[:, r], node_ids[:, bass.ds(t, 1)], None, ALU.is_equal).then_inc(pick_n_ready, 1)
                        dve.wait_ge(dst_in[r], it * 16 + 16)
                        if later(s, RING):
                            dve.wait_ge(summed, s - (RING - 1))
                        dve.tensor_tensor(pick_e[:, r], iota_all[:, bass.ds(t * P, P)].unsqueeze(1).broadcast_to([P, GB, P]),
                                          dst_col[:, r].unsqueeze(2).broadcast_to([P, GB, P]), ALU.is_equal).then_inc(pick_e_ready, 1)

                    def logits(s, r, it):
                        q = r % 2
                        dve.wait_ge(picked, s + 1)
                        dve.wait_ge(gathered[r], it * (16 * GB) + 16 * GB)
                        sel = psA[q][:, 0:GB * 2 * HEADS].rearrange("p (j a) -> p j a", j=GB)
                        dve.tensor_tensor(ze[:, q], rows_g[:, r, :, D:D + HEADS], sel[:, :, 0:HEADS], ALU.add).then_inc(z_ready, 1)
                        dve.wait_ge(z_ready, s + 1)
                        dve.scalar_tensor_tensor(out=zle[:, q], in0=ze[:, q], scalar=SLOPE, in1=ze[:, q],
                                                 op0=ALU.mult, op1=ALU.max).then_inc(zl_ready, 1)
                        dve.wait_ge(zl_ready, s + 1)
                        dve.tensor_tensor(ye[:, q], zle[:, q], sel[:, :, HEADS:2 * HEADS], ALU.subtract).then_inc(y_ready, 1)

                    def products(s, r):
                        dve.wait_ge(p_ready, s + 1)
                        dve.tensor_tensor(pe_h[:, r, :, 0:D].rearrange("p j (h c) -> p j h c", h=HEADS),
                                          rows_g[:, r, :, 0:D].rearrange("p j (h c) -> p j h c", h=HEADS),
                                          pe_h[:, r, :, D:AW].unsqueeze(3).broadcast_to([P, GB, HEADS, C]),
                                          ALU.mult).then_inc(ph_ready, 1)

                    def add_up(s, r):
                        t = step_value(dve, 1, s, NT - 1)
                        dve.wait_ge(summed, s + 1)
                        if later(s, 1):
                            dve.wait_ge(added, s)
                        at = acc[:, bass.ds(t, 1), 0:AW]
                        dve.tensor_tensor(at, at, ps_sum[r][:, 0:AW].unsqueeze(1), ALU.add).then_inc(added, 1)

                    def step(s, r, it):
                        last = isinstance(s, int) and s == NS - 1
                        if not last:
                            picks(s + 1, (r + 1) % RING, it + (r + 1) // RING)
                        if later(s, 2):
                            add_up(s - 2, (r - 2) % RING)
                        products(s, r)
                        if not last:
                            logits(s + 1, (r + 1) % RING, it + (r + 1) // RING)

                    dve.wait_ge(iota_set, 1)
                    picks(0, 0, 0)
                    logits(0, 0, 0)
                    each_step(dve, step)
                    for s in (NS - 2, NS - 1):
                        add_up(s, s % RING)

                @block.scalar
                def _(act):
                    def step(s, r, it):
                        q = r % 2
                        act.wait_ge(y_ready, s + 1)
                        if later(s, RING):
                            act.wait_ge(summed, s - (RING - 1))
                        act.activation(pe_h[:, r, :, D:AW], ye[:, q], ACT.Exp).then_inc(p_ready, 1)

                    each_step(act, step)

                @block.tensor
                def _(pe):
                    def pick(s, r):
                        t = step_value(pe, 1, s, NT - 1)
                        q = r % 2
                        pe.wait_ge(pick_n_ready, s + 1)
                        if later(s, 2):
                            pe.wait_ge(y_ready, s - 1)
                        for j in range(GB):
                            last = pe.matmul(psA[q][:, j * 2 * HEADS:(j + 1) * 2 * HEADS],
                                             pick_n[:, q].rearrange("p (e j) -> p e j", j=GB)[:, :, j], adm[:, bass.ds(t, 1)],
                                             start=True, stop=True)
                        last.then_inc(picked, 1)

                    def sums(s, r):
                        pe.wait_ge(ph_ready, s + 1)
                        if later(s, RING):
                            pe.wait_ge(added, s - (RING - 1))
                        for j in range(GB):
                            last = pe.matmul(ps_sum[r][:, 0:AW], pick_e[:, r, j], pe_h[:, r, j], start=(j == 0), stop=(j == GB - 1))
                        last.then_inc(summed, 1)

                    def step(s, r, it):
                        if not (isinstance(s, int) and s == NS - 1):
                            pick(s + 1, (r + 1) % RING)
                        sums(s, r)

                    pick(0, 0)
                    each_step(pe, step)

        with phase() as (ph, sem):
            after = sb("after", [P, P], c=ph)
            ones_sq = sb("ones_sq", [P, P], c=ph)
            den = sb("den", [P, 2, HEADS], c=ph)
            rden = sb("rden", [P, 2, HEADS], c=ph)
            gat = sb("gat", [P, 2, D], c=ph)
            gat_b = sb("gat_b", [P, 2, D], c=ph)
            xa, xb = xin, xn
            xc = sb("xc", [P, 2, D], c=ph)
            xd = sb("xd", [P, 2, D], c=ph)
            logit = sb("logit", [P, 2, NE], c=ph)
            top = sb("top", [P, 2, 8], c=ph)
            top_at = sb("top_at", [P, 2, 8], U32, c=ph)
            top_f = sb("top_f", [P, 2, 2], c=ph)
            gaps = sb("gaps", [P, NT], c=ph)
            ex = sb("ex", [P, NT], c=ph)
            ex1 = sb("ex1", [P, NT], c=ph)
            ex_ready = sem("f_ex_ready")
            chosen = sb("chosen", [P, 2, 2, NE], c=ph)
            both = sb("both", [P, 2, NE], c=ph)
            place = sb("place", [P, 2, NE], c=ph)
            hit = sb("hit", [P, 2, 2, NE], c=ph)
            place_f = sb("place_f", [P, 2, 2], c=ph)
            mix_slot = sb("mix_slot", [P, 2, D], c=ph)
            zero_rows = sb("zero_rows", [P, D], c=ph)
            fill_at = sb("fill_at", [P, NE], I32, c=ph)
            fill_f = sb("fill_f", [P, NE], c=ph)
            nblk_i = sb("nblk_i", [P, 2, NE], I32, c=ph)
            nblk_f = sb("nblk_f", [P, NE], c=ph)
            blk_end = sb("blk_end", [P, NE], c=ph)
            blk_gone = sb("blk_gone", [P, 2, NE], c=ph)
            blk_e = sb("blk_e", [P, 1], c=ph)
            moved = sb("moved", [P, NE], c=ph)
            moved2 = sb("moved2", [P, NE], c=ph)
            shift = sb("shift", [P, NT, 2], c=ph)
            blk_e7 = sb("blk_e7", [P, 1], c=ph)
            blk_before = sb("blk_before", [P, 1], c=ph)
            blk_j = sb("blk_j", [P, 1], c=ph)
            blk_i = sb("blk_i", [P, 2], I32, c=ph)
            f_in = [sem("f_in0"), sem("f_in1")]
            sent = [sem("sent0"), sem("sent1")]
            names = ("den_ready rden_ready gat_ready gat_biased x1_ready turned xT_ready logits_done logit_ready "
                     "top_ready top_at_ready top_f_ready gap_ready chosen_ready both_ready "
                     "xa_ready xb_ready xc_ready xd_ready counted place_ready hit_ready place_f_ready place_i_ready seen_ready").split()
            f = {n: sem("f_" + n) for n in names}
            f_set, f_tri, totals_done, blk_chain, blk_ready, fill_ready, fills_out, empty_out, blk_out, blk_in = (
                sem("f_" + n) for n in "set tri totals_done blk_chain blk_ready fill_ready fills_out empty_out blk_out blk_in".split())
            ln_stats, ln_mv, ln_std, ln_rstd = ([sem(f"f_{n}{k}") for k in range(2)] for n in ("stats", "mv", "std", "rstd"))
            with nc.Block() as block:
                @block.sync
                def _(sp):
                    def load(i, q, rows):
                        if later(i, 2):
                            sp.wait_ge(f["x1_ready"], i - 1)
                        sp.dma_start(mix_slot[0:rows, q], mixed_dram[node_rows(i, rows)]).then_inc(f_in[q], 16)

                    def tile(i, q, rows, it):
                        if isinstance(i, int) and i + 2 > FULL:
                            return
                        load(i + 2, q, TAIL if isinstance(i, int) and i + 2 == FULL else P)

                    for i in range(2):
                        load(i, i, P)
                    each_tile(sp, tile)
                    sp.wait_ge(f_set, 4)
                    for b in range(SPARE):
                        sp.dma_start(sent_dram[NE * REGION + b * P:NE * REGION + (b + 1) * P], zero_rows[:]).then_inc(empty_out, 16)
                    sp.wait_ge(blk_ready, 2)
                    for w in range(2):
                        sp.dma_start(block_table[w].unsqueeze(1), blk_i[:, w:w + 1],
                                     allow_slow_non_contiguous=True).then_inc(blk_out, 16)
                    sp.wait_ge(blk_out, 32)
                    sp.dma_start(blocks_row[:], block_table.unsqueeze(0)).then_inc(blk_in, 16)
                    sp.wait_ge(blk_in, 16)
                    sp.wait_ge(fills_out, 16 * NE)
                    sp.wait_ge(empty_out, 16 * SPARE)

                @block.vector
                def _(dve):
                    def norm(k, i, q, rows, src_v, src_ready, dst_t, dst_ready):
                        dve.wait_ge(src_ready, i + 1)
                        dve.sem_inc(dve_gate, 1)
                        dve.bn_stats(stats[0:rows, q], src_v).then_inc(ln_stats[k], 1)
                        dve.wait_ge(ln_stats[k], i + 1)
                        dve.sem_inc(dve_gate, 1)
                        dve.bn_aggr(mv[0:rows, q], stats[0:rows, q]).then_inc(ln_mv[k], 1)
                        dve.wait_ge(ln_std[k], i + 1)
                        dve.reciprocal(rstd[0:rows, q], std[0:rows, q]).then_inc(ln_rstd[k], 1)
                        dve.wait_ge(ln_rstd[k], i + 1)
                        dve.tensor_scalar(dst_t[0:rows, q], src_v, mv[0:rows, q, 0:1], rstd[0:rows, q],
                                          ALU.subtract, ALU.mult).then_inc(dst_ready, 1)

                    def front_a(i, q, rows, it):
                        a = acc[0:rows, bass.ds(i, 1)]
                        x1 = a[:, :, 0:D].rearrange("p o c -> p (o c)")
                        dve.tensor_scalar(den[0:rows, q].unsqueeze(1), a[:, :, D:AW], 1e-16, None, ALU.add).then_inc(f["den_ready"], 1)
                        dve.wait_ge(f["den_ready"], i + 1)
                        dve.reciprocal(rden[0:rows, q], den[0:rows, q]).then_inc(f["rden_ready"], 1)
                        dve.wait_ge(f["rden_ready"], i + 1)
                        dve.tensor_tensor(gat[0:rows, q].rearrange("p (o h c) -> p (o h) c", o=1, h=HEADS),
                                          a[:, :, 0:D].rearrange("p o (h c) -> p (o h) c", h=HEADS),
                                          rden[0:rows, q].unsqueeze(2).broadcast_to([rows, HEADS, C]), ALU.mult).then_inc(f["gat_ready"], 1)
                        dve.wait_ge(f["gat_ready"], i + 1)
                        dve.tensor_tensor(gat_b[0:rows, q], gat[0:rows, q], gnn_bias_b[0:rows], ALU.add).then_inc(f["gat_biased"], 1)
                        dve.wait_ge(f["gat_biased"], i + 1)
                        dve.wait_ge(f_in[q], it * 16 + 16)
                        dve.scalar_tensor_tensor(out=x1, in0=gat_b[0:rows, q], scalar=0.0, in1=mix_slot[0:rows, q],
                                                 op0=ALU.max, op1=ALU.add).then_inc(f["x1_ready"], 1)
                        norm(0, i, q, rows, x1, f["x1_ready"], xa, f["xa_ready"])

                    def front_b(i, q, rows, it):
                        norm(1, i, q, rows, xa[0:rows, q], f["xa_ready"], xb, f["xb_ready"])
                        dve.wait_ge(f["xb_ready"], i + 1)
                        dve.tensor_tensor(xc[0:rows, q], xb[0:rows, q], gam_b[0:rows], ALU.mult).then_inc(f["xc_ready"], 1)
                        dve.wait_ge(f["xc_ready"], i + 1)
                        if later(i, 2):
                            dve.wait_ge(f["turned"], i - 1)
                            dve.wait_ge(sent[q], it * 32)
                        dve.tensor_tensor(xd[0:rows, q], xc[0:rows, q], bet_b[0:rows], ALU.add).then_inc(f["xd_ready"], 1)

                    def route_a(i, q, rows, it):
                        R = slice(0, rows)
                        dve.wait_ge(f["logits_done"], i + 1)
                        dve.tensor_tensor(logit[R, q], psD[q][R, 0:NE], br_b[R], ALU.add).then_inc(f["logit_ready"], 1)
                        dve.wait_ge(f["logit_ready"], i + 1)
                        dve.sem_inc(dve_gate, 1)
                        dve.max(top[R, q], logit[R, q]).then_inc(f["top_ready"], 1)
                        dve.wait_ge(f["top_ready"], i + 1)
                        dve.sem_inc(dve_gate, 1)
                        dve.max_index(top_at[R, q], top[R, q], logit[R, q]).then_inc(f["top_at_ready"], 1)
                        dve.tensor_tensor(gaps[R, bass.ds(i, 1)], top[R, q, 1:2], top[R, q, 0:1], ALU.subtract).then_inc(f["gap_ready"], 1)
                        dve.wait_ge(f["top_at_ready"], i + 1)
                        dve.tensor_scalar(top_f[R, q], top_at[R, q, 0:2], 0.0, None, ALU.add).then_inc(f["top_f_ready"], 1)
                        dve.wait_ge(f["top_f_ready"], i + 1)
                        dve.tensor_tensor(chosen[R, q], iota8[R].unsqueeze(1).broadcast_to([rows, 2, NE]),
                                          top_f[R, q].unsqueeze(2).broadcast_to([rows, 2, NE]), ALU.is_equal).then_inc(f["chosen_ready"], 1)
                        dve.wait_ge(f["chosen_ready"], i + 1)
                        dve.tensor_tensor(both[R, q], chosen[R, q, 0], chosen[R, q, 1], ALU.add).then_inc(f["both_ready"], 1)

                    def route_b(i, q, rows, it):
                        R = slice(0, rows)
                        dve.wait_ge(f["counted"], i + 1)
                        dve.tensor_tensor(place[R, q], psD[q][R, 16:16 + NE], region[R], ALU.add).then_inc(f["place_ready"], 1)
                        dve.wait_ge(f["place_ready"], i + 1)
                        dve.tensor_tensor(hit[R, q], chosen[R, q], place[R, q].unsqueeze(1).broadcast_to([rows, 2, NE]),
                                          ALU.mult).then_inc(f["hit_ready"], 1)
                        dve.wait_ge(f["hit_ready"], i + 1)
                        dve.tensor_reduce(place_f[R, q], hit[R, q], AX_X, ALU.add).then_inc(f["place_f_ready"], 1)
                        dve.wait_ge(f["place_f_ready"], i + 1)
                        if later(i, 2):
                            dve.wait_ge(sent[q], it * 32)
                        dve.tensor_scalar(place_s[R, q], place_f[R, q], 1.0, None, ALU.mult).then_inc(f["place_i_ready"], 1)
                        dve.tensor_scalar(places_f[R, bass.ds(i, 1)], place_f[R, q].unsqueeze(1), 1.0, None, ALU.mult)
                        dve.tensor_scalar(choices[R, bass.ds(i, 1)].rearrange("p o c e -> p o (c e)"),
                                          chosen[R, q].rearrange("p c e -> p (c e)").unsqueeze(1), 1.0, None, ALU.mult)
                        dve.tensor_tensor(seen[R], seen[R], both[R, q], ALU.add).then_inc(f["seen_ready"], 1)

                    def tile(i, q, rows, it):
                        if has_next(i):
                            front_a(*next_tile(i, q, it))
                        route_a(i, q, rows, it)
                        if has_next(i):
                            front_b(*next_tile(i, q, it))
                        route_b(i, q, rows, it)

                    dve.memset(places_f[:], 0.0)
                    dve.memset(gaps[:], 0.0)
                    dve.memset(choices[:], 0.0)
                    dve.memset(seen[:], 0.0).then_inc(f_set, 1)
                    dve.memset(ones_sq[:], 1.0).then_inc(f_set, 1)
                    dve.memset(zero_rows[:], 0.0).then_inc(f_set, 1)
                    dve.wait_ge(f_tri, 2)
                    dve.tensor_scalar(region[:], iota8[:], float(REGION), None, ALU.mult).then_inc(f_set, 1)
                    dve.wait_ge(f_set, 4)
                    front_a(0, 0, P, 0)
                    front_b(0, 0, P, 0)
                    each_tile(dve, tile)

                    step = [0]

                    def then(ins):
                        step[0] += 1
                        ins.then_inc(blk_chain, 1)
                        dve.wait_ge(blk_chain, step[0])

                    dve.wait_ge(totals_done, 1)
                    then(dve.tensor_tensor(fill_f[:], psA[0][:, 0:NE], region[:], ALU.add))
                    dve.tensor_scalar(fill_at[:], fill_f[:], node_ids[:, 0:1], None, ALU.add).then_inc(fill_ready, 1)
                    then(dve.tensor_scalar(nblk_i[:, 0], psA[0][:, 0:NE], float(P - 1), None, ALU.add))
                    then(dve.tensor_scalar(nblk_i[:, 1], nblk_i[:, 0], P.bit_length() - 1, None, ALU.logical_shift_right))
                    then(dve.tensor_copy(nblk_f[:], nblk_i[:, 1]))
                    then(dve.tensor_tensor_scan(blk_end[:], nblk_f[:], nblk_f[:], 0.0, ALU.add, ALU.bypass))
                    then(dve.tensor_scalar(blk_gone[:, 0], blk_end[:], node_ids[:, 0:1], 0.0, ALU.is_le, ALU.add, accum_out=blk_e[:]))
                    then(dve.tensor_tensor(blk_gone[:, 1], blk_gone[:, 0], nblk_f[:], ALU.mult))
                    then(dve.tensor_reduce(blk_before[:], blk_gone[:, 1], AX_X, ALU.add))
                    then(dve.tensor_tensor(blk_j[:], node_ids[:, 0:1], blk_before[:], ALU.subtract))
                    then(dve.tensor_scalar(blk_e7[:], blk_e[:], float(REGION // P), None, ALU.mult))
                    dve.tensor_tensor(blk_i[:, 0:1], blk_e7[:], blk_j[:], ALU.add).then_inc(blk_ready, 1)
                    dve.tensor_scalar(blk_i[:, 1:2], blk_e[:], float(NE - 1), None, ALU.min).then_inc(blk_ready, 1)
                    then(dve.tensor_tensor(moved[:], blk_end[:], nblk_f[:], ALU.subtract))
                    then(dve.scalar_tensor_tensor(out=moved2[:], in0=moved[:], scalar=float(P), in1=region[:],
                                                  op0=ALU.mult, op1=ALU.subtract))
                    then(dve.tensor_tensor(choices[:].rearrange("p t c e -> p (t c) e"), choices[:].rearrange("p t c e -> p (t c) e"),
                                           moved2[:].unsqueeze(1).broadcast_to([P, 2 * NT, NE]), ALU.mult))
                    then(dve.tensor_reduce(shift[:].rearrange("p t c -> p (t c)"), choices[:].rearrange("p t c e -> p (t c) e"), AX_X, ALU.add))
                    dve.tensor_tensor(places[:], places_f[:], shift[:], ALU.add)
                    dve.wait_ge(ex_ready, 1)
                    then(dve.tensor_scalar(ex1[:], ex[:], 1.0, None, ALU.add))
                    then(dve.reciprocal(share[:, :, 0], ex1[:]))
                    dve.tensor_tensor(share[:, :, 1], ex[:], share[:, :, 0], ALU.mult)

                @block.scalar
                def _(act):
                    def norm_and_turn(i, q, rows, it):
                        for k in range(2):
                            act.wait_ge(ln_mv[k], i + 1)
                            act.activation(std[0:rows, q], mv[0:rows, q, 1:2], ACT.Sqrt, bias=eps_col[0:rows]).then_inc(ln_std[k], 1)
                        act.wait_ge(f["turned"], i + 1)
                        if later(i, 2):
                            act.wait_ge(f["logits_done"], i - 1)
                        act.activation(xnT[:, q, :, 0:rows], psC[q][:, 0:KT * P].rearrange("p (k n) -> p k n", k=KT)[:, :, 0:rows],
                                       ACT.Copy).then_inc(f["xT_ready"], 1)

                    each_tile(act, norm_and_turn)
                    act.wait_ge(f["gap_ready"], NT)
                    act.activation(ex[:], gaps[:], ACT.Exp).then_inc(ex_ready, 1)

                @block.gpsimd
                def _(pool):
                    pool.memset(after[:], 1.0).then_inc(f_tri, 1)
                    pool.wait_ge(f_tri, 1)
                    pool.affine_select(out=after[:], in_=after[:], compare_op=ALU.is_gt, fill=0.0, base=0,
                                       pattern=[[1, P]], channel_multiplier=-1).then_inc(f_tri, 1)

                    def tile(i, q, rows, it):
                        pool.wait_ge(f["place_i_ready"], i + 1)
                        pool.sem_inc(pool_gate, 1)
                        for c in range(2):
                            pool.indirect_dma_start(out=sent_dram, out_offset=bass.IndirectOffsetOnAxis(ap=place_s[0:rows, q, c:c + 1], axis=0),
                                                    in_=xd[0:rows, q], in_offset=None).then_inc(sent[q], 16)

                    each_tile(pool, tile)
                    pool.wait_ge(fill_ready, 1)
                    for q in range(2):
                        pool.wait_ge(sent[q], 32 * (NT // 2 + (1 - q)))
                    for e in range(NE):
                        pool.indirect_dma_start(out=sent_dram, out_offset=bass.IndirectOffsetOnAxis(ap=fill_at[:, e:e + 1], axis=0),
                                                in_=zero_rows[:], in_offset=None).then_inc(fills_out, 16)

                @block.tensor
                def _(pe):
                    def logits(i, q, rows, it):
                        pe.wait_ge(f["xd_ready"], i + 1)
                        if later(i, 2):
                            pe.wait_ge(f["xT_ready"], i - 1)
                        for k in range(KT):
                            last = pe.transpose(psC[q][:, k * P:k * P + rows], xd[0:rows, q, k * P:(k + 1) * P],
                                                ident[0:rows, 0:rows])
                        last.then_inc(f["turned"], 1)
                        pe.wait_ge(f["xT_ready"], i + 1)
                        if later(i, 2):
                            pe.wait_ge(f["place_ready"], i - 1)
                        for k in range(KT):
                            last = pe.matmul(psD[q][0:rows, 0:NE], xnT[:, q, k, 0:rows], wr_s[:, k], start=(k == 0), stop=(k == KT - 1))
                        last.then_inc(f["logits_done"], 1)

                    def tile(i, q, rows, it):
                        if has_next(i):
                            logits(*next_tile(i, q, it))
                        pe.wait_ge(f["both_ready"], i + 1)
                        if later(i, 1):
                            pe.wait_ge(f["seen_ready"], i)
                        pe.matmul(psD[q][0:rows, 16:16 + NE], after[0:rows, 0:rows], both[0:rows, q], start=True, stop=False)
                        pe.matmul(psD[q][0:rows, 16:16 + NE], ones_sq[:, 0:rows], seen[:], start=False, stop=True).then_inc(f["counted"], 1)

                    pe.wait_ge(f_set, 3)
                    pe.wait_ge(f_tri, 2)
                    logits(0, 0, P, 0)
                    each_tile(pe, tile)
                    pe.wait_ge(f["seen_ready"], NT)
                    pe.matmul(psA[0][:, 0:NE], ones_sq[:], seen[:], start=True, stop=True).then_inc(totals_done, 1)

        with phase() as (ph, sem):
            W1_s = sb("W1_s", [P, NE, KT, H], c=ph)
            W2_s = sb("W2_s", [P, NE, HK, D], c=ph)
            fb1_b = sb("fb1_b", [P, NE, H], c=ph)
            fb2_b = sb("fb2_b", [P, NE, D], c=ph)
            xe = sb("xe", [P, 2, D], c=ph)
            xeT = sb("xeT", [P, 2, KT, P], c=ph)
            hb = sb("hb", [P, 2, H], c=ph)
            hg = sb("hg", [P, 2, H], c=ph)
            hT = sb("hT", [P, 2, HK, P], c=ph)
            ys = sb("ys", [P, 2, D], c=ph)
            weights_in = sem("weights_in")
            xe_in, ys_out = [sem("xe_in0"), sem("xe_in1")], [sem("ys_out0"), sem("ys_out1")]
            x_turned, xeT_ready, up_done5, hb_ready, hg_ready, h_turned, hT_ready, down_done5, ys_ready = (
                sem("e_" + n) for n in "x_turned xeT_ready up_done hb_ready hg_ready h_turned hT_ready down_done ys_ready".split())

            def each_block(eng, body):
                for k in range(2):
                    body(k, k, 0)
                with eng.Fori(1, NBLK // 2 - 1) as it:
                    for u in range(2):
                        body(it * 2 + u, u, it)
                for k in range(NBLK - 2, NBLK):
                    body(k, k % 2, k // 2)

            def block_value(eng, w, k, top_v):
                return eng.value_load(blocks_row[0:1, w, bass.ds(k, 1)], min_val=0, max_val=top_v)

            def ahead(k):
                return not (isinstance(k, int) and k == NBLK - 1)

            with nc.Block() as block:
                @block.sync
                def _(sp):
                    LASTB = NE * REGION // P + SPARE - 1

                    def load(k, u):
                        b = block_value(sp, 0, k, LASTB)
                        if later(k, 2):
                            sp.wait_ge(x_turned, k - 1)
                        sp.dma_start(xe[:, u], sent_dram[bass.ds(b * P, P)]).then_inc(xe_in[u], 16)

                    def store(k, u):
                        sp.wait_ge(ys_ready, k + 1)
                        sp.dma_start(done_dram[bass.ds(k * P, P)], ys[:, u]).then_inc(ys_out[u], 16)

                    def one(k, u, it):
                        if not (isinstance(k, int) and k + 2 >= NBLK):
                            load(k + 2, u)
                        if later(k, 1):
                            store(k - 1, 1 - u)

                    load(0, 0)
                    load(1, 1)
                    each_block(sp, one)
                    store(NBLK - 1, (NBLK - 1) % 2)
                    for u in range(2):
                        sp.wait_ge(ys_out[u], 16 * (NBLK // 2))

                @block.gpsimd
                def _(pool):
                    pass

                @block.scalar
                def _(act):
                    for to, frm in ((W1_s, W1.rearrange("e (k p) n -> p e k n", p=P)), (W2_s, W2.rearrange("e (k p) n -> p e k n", p=P)),
                                    (fb1_b, fb1.partition_broadcast(P)), (fb2_b, fb2.partition_broadcast(P))):
                        act.dma_start(to[:], frm).then_inc(weights_in, 16)

                    def turn_x(k, u):
                        act.wait_ge(x_turned, k + 1)
                        if later(k, 2):
                            act.wait_ge(up_done5, k - 1)
                        act.activation(xeT[:, u], psD[u][:, 0:KT * P].rearrange("p (k n) -> p k n", k=KT), ACT.Copy).then_inc(xeT_ready, 1)

                    def one(k, u, it):
                        act.wait_ge(hb_ready, k + 1)
                        if later(k, 2):
                            act.wait_ge(h_turned, k - 1)
                        act.activation(hg[:, u], hb[:, u], ACT.Gelu).then_inc(hg_ready, 1)
                        if ahead(k):
                            turn_x(k + 1, 1 - u)
                        act.wait_ge(h_turned, k + 1)
                        if later(k, 2):
                            act.wait_ge(down_done5, k - 1)
                        act.activation(hT[:, u], psB[u][:, :].rearrange("p (c n) -> p c n", c=HK), ACT.Copy).then_inc(hT_ready, 1)

                    turn_x(0, 0)
                    each_block(act, one)

                @block.vector
                def _(dve):
                    def hidden_bias(k, u, it):
                        e = block_value(dve, 1, k, NE - 1)
                        dve.wait_ge(up_done5, k + 1)
                        if later(k, 2):
                            dve.wait_ge(hg_ready, k - 1)
                        dve.tensor_tensor(hb[:, u].unsqueeze(1), psA[u][:, :].unsqueeze(1), fb1_b[:, bass.ds(e, 1)], ALU.add).then_inc(hb_ready, 1)

                    def result(k, u, it):
                        e = block_value(dve, 1, k, NE - 1)
                        dve.wait_ge(down_done5, k + 1)
                        if later(k, 2):
                            dve.wait_ge(ys_out[u], it * 16)
                        dve.tensor_tensor(ys[:, u].unsqueeze(1), psC[u][:, 0:D].unsqueeze(1), fb2_b[:, bass.ds(e, 1)], ALU.add).then_inc(ys_ready, 1)

                    def one(k, u, it):
                        if ahead(k):
                            hidden_bias(k + 1, 1 - u, it)
                        result(k, u, it)

                    dve.wait_ge(weights_in, 64)
                    hidden_bias(0, 0, 0)
                    each_block(dve, one)

                @block.tensor
                def _(pe):
                    def turn_x(k, u, it):
                        pe.wait_ge(xe_in[u], it * 16 + 16)
                        if later(k, 2):
                            pe.wait_ge(xeT_ready, k - 1)
                        for c in range(KT):
                            last = pe.transpose(psD[u][:, c * P:(c + 1) * P], xe[:, u, c * P:(c + 1) * P], ident[:])
                        last.then_inc(x_turned, 1)

                    def up(k, u):
                        e = block_value(pe, 1, k, NE - 1)
                        pe.wait_ge(xeT_ready, k + 1)
                        if later(k, 2):
                            pe.wait_ge(hb_ready, k - 1)
                        for c in range(KT):
                            last = pe.matmul(psA[u][:, :], xeT[:, u, c], W1_s[:, bass.ds(e, 1), c], start=(c == 0), stop=(c == KT - 1))
                        last.then_inc(up_done5, 1)

                    def turn_h(k, u):
                        pe.wait_ge(hg_ready, k + 1)
                        if later(k, 2):
                            pe.wait_ge(hT_ready, k - 1)
                        for c in range(HK):
                            last = pe.transpose(psB[u][:, c * P:(c + 1) * P], hg[:, u, c * P:(c + 1) * P], ident[:])
                        last.then_inc(h_turned, 1)

                    def down(k, u):
                        e = block_value(pe, 1, k, NE - 1)
                        pe.wait_ge(hT_ready, k + 1)
                        if later(k, 2):
                            pe.wait_ge(ys_ready, k - 1)
                        for c in range(HK):
                            last = pe.matmul(psC[u][:, 0:D], hT[:, u, c], W2_s[:, bass.ds(e, 1), c], start=(c == 0), stop=(c == HK - 1))
                        last.then_inc(down_done5, 1)

                    def one(k, u, it):
                        if ahead(k):
                            up(k + 1, 1 - u)
                        turn_h(k, u)
                        if ahead(k) and not (isinstance(k, int) and k == NBLK - 2):
                            turn_x(k + 2, u, it + 1)
                        down(k, u)

                    turn_x(0, 0, 0)
                    turn_x(1, 1, 0)
                    pe.wait_ge(weights_in, 64)
                    up(0, 0)
                    each_block(pe, one)

        with phase() as (ph, sem):
            picked_rows = sb("picked_rows", [P, 4, 2, D], c=ph)
            at_slot = sb("at_slot", [P, 4, 2], I32, c=ph)
            y_first = sb("y_first", [P, 4, D], c=ph)
            y_all = sb("y_all", [P, 4, D], c=ph)
            rows_in, y_out = [sem(f"g_rows_in{r}") for r in range(4)], [sem(f"g_y_out{r}") for r in range(4)]
            at_ready, first_ready, all_ready = sem("g_at_ready"), sem("g_first_ready"), sem("g_all_ready")
            QUADS = FULL // 4

            def each_quad(eng, body):
                for i in range(4):
                    body(i, i, P, 0)
                if QUADS > 2:
                    with eng.Fori(1, QUADS - 1) as it:
                        for r in range(4):
                            body(it * 4 + r, r, P, it)
                for i in range(max(QUADS - 1, 1) * 4, NT):
                    body(i, i % 4, P if i < FULL else TAIL, i // 4)

            with nc.Block() as block:
                @block.gpsimd
                def _(pool):
                    def tile(i, r, rows, it):
                        pool.wait_ge(at_ready, i + 1)
                        if later(i, 4):
                            pool.wait_ge(all_ready, i - 3)
                        pool.sem_inc(pool_gate, 1)
                        for c in range(2):
                            pool.indirect_dma_start(out=picked_rows[0:rows, r, c], out_offset=None, in_=done_dram,
                                                    in_offset=bass.IndirectOffsetOnAxis(ap=at_slot[0:rows, r, c:c + 1], axis=0)
                                                    ).then_inc(rows_in[r], 16)

                    each_quad(pool, tile)

                @block.vector
                def _(dve):
                    def row_numbers(i, r, rows, it):
                        if later(i, 4):
                            dve.wait_ge(rows_in[r], it * 32)
                        dve.tensor_scalar(at_slot[0:rows, r].unsqueeze(1), places[0:rows, bass.ds(i, 1)], 1.0, None, ALU.mult).then_inc(at_ready, 1)

                    def sums(i, r, rows, it):
                        x1 = acc[0:rows, bass.ds(i, 1), 0:D].rearrange("p o c -> p (o c)")
                        w = share[0:rows, bass.ds(i, 1)].rearrange("p o c -> p (o c)")
                        dve.wait_ge(rows_in[r], it * 32 + 32)
                        dve.scalar_tensor_tensor(out=y_first[0:rows, r], in0=picked_rows[0:rows, r, 0], scalar=w[:, 0:1], in1=x1,
                                                 op0=ALU.mult, op1=ALU.add).then_inc(first_ready, 1)
                        dve.wait_ge(first_ready, i + 1)
                        if later(i, 4):
                            dve.wait_ge(y_out[r], it * 16)
                        dve.scalar_tensor_tensor(out=y_all[0:rows, r], in0=picked_rows[0:rows, r, 1], scalar=w[:, 1:2],
                                                 in1=y_first[0:rows, r], op0=ALU.mult, op1=ALU.add).then_inc(all_ready, 1)

                    def tile(i, r, rows, it):
                        if not (isinstance(i, int) and i + 2 > FULL):
                            row_numbers(i + 2, (r + 2) % 4, TAIL if isinstance(i, int) and i + 2 == FULL else P, it + (r + 2) // 4)
                        sums(i, r, rows, it)

                    row_numbers(0, 0, P, 0)
                    row_numbers(1, 1, P, 0)
                    each_quad(dve, tile)

                @block.sync
                def _(sp):
                    def tile(i, r, rows, it):
                        sp.wait_ge(all_ready, i + 1)
                        sp.dma_start(out[node_rows(i, rows)], y_all[0:rows, r]).then_inc(y_out[r], 16)

                    each_quad(sp, tile)
                    for r in range(4):
                        sp.wait_ge(y_out[r], 16 * len(range(r, NT, 4)))


_INS = ['x', 'src', 'dst', 'L0_gnn_W', 'L0_gnn_att_src', 'L0_gnn_att_dst', 'L0_gnn_bias', 'L0_mix_w_qkv', 'L0_mix_b_qkv',
        'L0_mix_kln_g', 'L0_mix_kln_b', 'L0_mix_vln_g', 'L0_mix_vln_b', 'L0_mix_w1', 'L0_mix_b1', 'L0_mix_w2', 'L0_mix_b2',
        'L0_ffn_gamma', 'L0_ffn_beta', 'L0_ffn_Wr', 'L0_ffn_br', 'L0_ffn_W1', 'L0_ffn_b1', 'L0_ffn_W2', 'L0_ffn_b2']


def kernel(**inputs):
    import numpy as _np
    import concourse.bacc as _bacc
    from concourse import mybir as _mybir
    from concourse.bass_utils import run_bass_kernel_spmd as _run

    nc = _bacc.Bacc("TRN2", target_bir_lowering=False, num_devices=1)
    arrays, args = {}, []
    for name in _INS:
        a = _np.ascontiguousarray(inputs[name])
        arrays[f"in_{name}_dram"] = a
        args.append(nc.dram_tensor(f"in_{name}_dram", a.shape, _mybir.dt.from_np(a.dtype), kind="ExternalInput").ap())
    out = nc.dram_tensor("out_0_dram", inputs["x"].shape, F32, kind="ExternalOutput").ap()
    gps_layer(nc, *args, out)
    r = _run(nc, [arrays], core_ids=[0])
    return r.results[0]["out_0_dram"]
```

```python
from contextlib import ExitStack, contextmanager

import concourse.bass as bass
from concourse import mybir

P = 128
F32 = mybir.dt.float32
I32 = mybir.dt.int32
U32 = mybir.dt.uint32
ALU = mybir.AluOpType
ACT = mybir.ActivationFunctionType
AX_X = mybir.AxisListType.X

EPS = 1e-5
SLOPE = 0.2
HEADS = 4
MH = 8
GB = 4
SB = GB * P
MAX_SPAN = 16.0
MAX_TOP = 60.0
RING = 4
STRIDE = 2 * RING


def gps_layer(nc, x, src, dst, gnn_W, att_src, att_dst, gnn_bias, w_qkv, b_qkv, kln_g, kln_b, vln_g, vln_b,
              w1, b1, w2, b2, gamma, beta, Wr, br, W1, fb1, W2, fb2, out):
    N, D = x.shape
    E = src.shape[0]
    NT = -(-N // P)
    TAIL = N - (NT - 1) * P
    FULL = NT - 1
    NSB = -(-E // SB)
    PAD = (NSB + 1) * SB - E
    NS = max(-(-(NSB + NT - 1) // STRIDE), NT + 3) * STRIDE
    NCH = -(-NS // P)
    C = D // HEADS
    HW_ = D + 2 * HEADS
    AW = D + HEADS
    KT = D // P
    HC = D // MH
    NE, _, H = W1.shape
    HK = H // P
    assert FULL % 2 == 0 and NSB <= 512 and NCH <= NT

    REGION = (NT + 1) * P
    NBLK = -(-((2 * N + NE * (P - 1)) // P) // 2) * 2
    SPARE = NBLK - -(-2 * N // P)
    assert NBLK <= P and NBLK >= 6

    sent_dram = nc.dram_tensor("sent_dram", (NE * REGION + SPARE * P, D), F32).ap()
    done_dram = nc.dram_tensor("done_dram", (NBLK * P, D), F32).ap()
    block_table = nc.dram_tensor("block_table", (2, P), I32).ap()
    node_table = nc.dram_tensor("node_table", (NT * P, HW_), F32).ap()
    edge_src = nc.dram_tensor("edge_src", ((NSB + 1) * SB,), I32).ap()
    edge_dst_1 = nc.dram_tensor("edge_dst", ((NSB + 1) * SB + 1,), I32).ap()
    edge_dst = edge_dst_1[0:(NSB + 1) * SB]
    step_table = nc.dram_tensor("step_table", (2, NCH * P), I32).ap()
    xnT_dram = nc.dram_tensor("xnT_dram", (NT, P, KT, P), F32).ap()
    base_dram = nc.dram_tensor("base_dram", (NT * P, D), F32).ap()
    mixed_dram = nc.dram_tensor("mixed_dram", (NT * P, D), F32).ap()

    with ExitStack() as ctx:
        def sem(name):
            return ctx.enter_context(nc.semaphore(name))

        def sb(name, shape, dt=F32, c=ctx):
            return c.enter_context(nc.sbuf_tensor(name, shape, dt))

        ident = sb("ident", [P, P])
        node_ids = sb("node_ids", [P, NT])
        iota8 = sb("iota8", [P, NE])
        ones_row = sb("ones_row", [1, P])
        eps_col = sb("eps_col", [P, 1])
        W_ext = sb("W_ext", [P, KT, HW_])
        gnn_bias_b = sb("gnn_bias_b", [P, D])
        wqkv_s = sb("wqkv_s", [P, KT, 3 * D])
        bqkv_b = sb("bqkv_b", [P, 3 * D])
        w1_s = sb("w1_s", [P, KT, D])
        w2_s = sb("w2_s", [P, KT, D])
        b1_b = sb("b1_b", [P, D])
        b2_b = sb("b2_b", [P, D])
        ln_g = sb("ln_g", [P, 2, HC])
        ln_b = sb("ln_b", [P, 2, HC])
        head_mask = sb("head_mask", [P, P])
        weff = sb("weff", [P, KT, D])
        beff = sb("beff", [P, D])
        gam_b = sb("gam_b", [P, D])
        bet_b = sb("bet_b", [P, D])
        wr_s = sb("wr_s", [P, KT, NE])
        br_b = sb("br_b", [P, NE])
        acc = sb("acc", [P, NT, HW_])
        adm = sb("adm", [P, NT, 2 * HEADS])
        smax = sb("smax", [P, 2 * HEADS + 1])
        smax_all = sb("smax_all", [P, 2 * HEADS + 1])
        general = sb("general", [1, 1], I32)
        steps_row = sb("steps_row", [1, 2, NCH * P], I32)
        share = sb("share", [P, NT, 2])
        places_f = sb("places_f", [P, NT, 2])
        places = sb("places", [P, NT, 2], I32)
        choices = sb("choices", [P, NT, 2, NE])
        place_s = sb("place_s", [P, 2, 2], I32)
        seen = sb("seen", [P, NE])
        region = sb("region", [P, NE])
        blocks_row = sb("blocks_row", [1, 2, P], I32)
        xin = sb("xin", [P, 2, D])
        xn = sb("xn", [P, 2, D])
        xnT = sb("xnT", [P, 2, KT, P])
        stats = sb("stats", [P, 2, 6])
        mv = sb("mv", [P, 2, 2])
        std = sb("std", [P, 2, 1])
        rstd = sb("rstd", [P, 2, 1])

        psA = [ctx.enter_context(nc.psum_tensor(f"psA{q}", [P, 512], F32)) for q in range(2)]
        psB = [ctx.enter_context(nc.psum_tensor(f"psB{q}", [P, 512], F32)) for q in range(2)]
        psC = [ctx.enter_context(nc.psum_tensor(f"psC{q}", [P, 512], F32)) for q in range(2)]
        psD = [ctx.enter_context(nc.psum_tensor(f"psD{q}", [P, 512], F32)) for q in range(2)]

        loads_done = sem("loads_done")
        weights_in = sem("weights_in")
        dve_gate, pool_gate = sem("dve_gate"), sem("pool_gate")

        LOADS = [
            (W_ext[:, :, 0:D], gnn_W.rearrange("(k p) n -> p k n", p=P)),
            (gnn_bias_b[:], gnn_bias.partition_broadcast(P)),
            (wqkv_s[:], w_qkv.rearrange("(k p) n -> p k n", p=P)),
            (bqkv_b[:], b_qkv.partition_broadcast(P)),
            (w1_s[:], w1.rearrange("(k p) n -> p k n", p=P)),
            (w2_s[:], w2.rearrange("(k p) n -> p k n", p=P)),
            (b1_b[:], b1.partition_broadcast(P)),
            (b2_b[:], b2.partition_broadcast(P)),
            (ln_g[:, 0], kln_g.partition_broadcast(P)),
            (ln_g[:, 1], vln_g.partition_broadcast(P)),
            (ln_b[:, 0], kln_b.partition_broadcast(P)),
            (ln_b[:, 1], vln_b.partition_broadcast(P)),
            (gam_b[:], gamma.partition_broadcast(P)),
            (bet_b[:], beta.partition_broadcast(P)),
            (wr_s[:], Wr.rearrange("(k p) n -> p k n", p=P)),
            (br_b[:], br.partition_broadcast(P)),
        ]


        @contextmanager
        def phase():
            own = []

            def phase_sem(name):
                own.append(nc.alloc_semaphore(name))
                return own[-1]

            with ExitStack() as ph:
                yield ph, phase_sem
            nc.clear_and_free_semaphores(own)
            nc.all_engine_barrier()

        def each_tile(eng, body):
            for i in range(2):
                body(i, i % 2, P, 0)
            with eng.Fori(1, FULL // 2 - 1) as it:
                for q in range(2):
                    body(it * 2 + q, q, P, it)
            for i in range(FULL - 2, FULL):
                body(i, i % 2, P, i // 2)
            body(FULL, 0, TAIL, FULL // 2)

        def later(i, n):
            return not (isinstance(i, int) and i < n)

        def has_next(i):
            return not (isinstance(i, int) and i == FULL)

        def next_tile(i, q, it):
            return i + 1, 1 - q, TAIL if isinstance(i, int) and i + 1 == FULL else P, it + q

        def node_rows(i, rows):
            return bass.ds(i * P, rows)

        def self_loop_product(eng, t, p_self):
            h_v = acc[:, t, 0:D].rearrange("p (h c) -> p h c", h=HEADS)
            eng.tensor_tensor(h_v, h_v, p_self[:, t].unsqueeze(2).broadcast_to([P, HEADS, C]), ALU.mult)

        def maxima_and_self_loops(dve, top, za, zl, p_self, adm_part, self_part, p_self_ready, first=0):
            a_src, a_dst = acc[:, :, D:D + HEADS], acc[:, :, D + HEADS:HW_]
            dve.tensor_copy(adm[:, :, 0:HEADS], a_dst).then_inc(adm_part, 1)
            dve.tensor_tensor(za[:], a_dst, top, ALU.add).then_inc(adm_part, 1)
            dve.wait_ge(adm_part, 2)
            dve.scalar_tensor_tensor(out=adm[:, :, HEADS:2 * HEADS], in0=za[:], scalar=SLOPE, in1=za[:],
                                     op0=ALU.mult, op1=ALU.max).then_inc(adm_part, 1)
            dve.wait_ge(adm_part, 3)
            dve.tensor_tensor(za[:], a_src, a_dst, ALU.add).then_inc(self_part, 1)
            dve.wait_ge(self_part, 1)
            dve.scalar_tensor_tensor(out=zl[:], in0=za[:], scalar=SLOPE, in1=za[:],
                                     op0=ALU.mult, op1=ALU.max).then_inc(self_part, 1)
            dve.wait_ge(self_part, 2)
            dve.tensor_tensor(za[:], zl[:], adm[:, :, HEADS:2 * HEADS], ALU.subtract).then_inc(self_part, 1)
            dve.wait_ge(p_self_ready, 1)
            for t in range(first, NT):
                self_loop_product(dve, t, p_self)
            dve.tensor_copy(acc[:, :, D:AW], p_self[:]).then_inc(adm_part, 1)

        def general_value(eng):
            return eng.value_load(general[0:1, 0:1], min_val=0, max_val=1)

        with phase() as (ph, sem):
            att_b = sb("att_b", [P, 2, D], c=ph)
            att_prod = sb("att_prod", [P, KT, D], c=ph)
            pad_row = sb("pad_row", [1, 2, PAD + 1], I32, c=ph)
            last_dst = sb("last_dst", [1, NSB], I32, c=ph)
            last_tile = sb("last_tile", [1, NSB], I32, c=ph)
            last_step = sb("last_step", [1, NSB], c=ph)
            sb_ids = sb("sb_ids", [1, NSB], c=ph)
            below = sb("below", [P, NSB], c=ph)
            sb_done = sb("sb_done", [P, NCH], c=ph)
            tile_of = sb("tile_of", [P, NCH], c=ph)
            steps_i = sb("steps_i", [P, 2, NCH], I32, c=ph)
            pads_set, edges_in, last_in = sem("pads_set"), sem("edges_in"), sem("last_in")
            consts_set, ident_zero, rows_set = sem("consts_set"), sem("ident_zero"), sem("rows_set")
            att_prod_ready, att_cols_ready = sem("att_prod_ready"), sem("att_cols_ready")
            last_tile_ready, last_step_ready, last_step_spread = sem("last_tile_ready"), sem("last_step_ready"), sem("last_step_spread")
            sb_done_ready, tile_of_ready = sem("sb_done_ready"), sem("tile_of_ready")
            steps_ready, steps_out, steps_in, mask_zero = sem("steps_ready"), sem("steps_out"), sem("steps_in"), sem("mask_zero")
            NLOADS = len(LOADS) + 2

            with nc.Block() as block:
                @block.sync
                def _(sp):
                    sp.dma_start(edge_src[0:E], src).then_inc(edges_in, 16)
                    sp.dma_start(edge_dst[0:E], dst).then_inc(edges_in, 16)
                    sp.wait_ge(pads_set, 2)
                    sp.dma_start(edge_src[E:E + PAD].unsqueeze(0), pad_row[:, 0, 0:PAD]).then_inc(edges_in, 16)
                    sp.dma_start(edge_dst_1[E:E + PAD + 1].unsqueeze(0), pad_row[:, 1]).then_inc(edges_in, 16)
                    sp.wait_ge(edges_in, 64)
                    sp.dma_start(last_dst[:], edge_dst.rearrange("(b e) -> e b", e=SB)[SB - 1:SB, 0:NSB],
                                 allow_slow_non_contiguous=True).then_inc(last_in, 16)
                    sp.wait_ge(steps_ready, 2)
                    for w in range(2):
                        sp.dma_start(step_table[w].rearrange("(c p) -> p c", p=P), steps_i[:, w],
                                     allow_slow_non_contiguous=True).then_inc(steps_out, 16)
                    sp.wait_ge(steps_out, 32)
                    sp.dma_start(steps_row[:], step_table.unsqueeze(0)).then_inc(steps_in, 16)
                    sp.wait_ge(steps_in, 16)

                @block.scalar
                def _(act):
                    for w, a in enumerate((att_src, att_dst)):
                        act.dma_start(att_b[:, w], a.rearrange("h c -> (h c)").partition_broadcast(P)).then_inc(loads_done, 16)
                    for to, frm in LOADS:
                        act.dma_start(to, frm).then_inc(loads_done, 16)
                    act.wait_ge(loads_done, 16 * NLOADS)

                @block.gpsimd
                def _(pool):
                    pool.memset(ident[:], 0.0).then_inc(ident_zero, 1)
                    for ids, step, mult in ((node_ids, P, 1), (sb_ids, 1, 0), (iota8, 1, 0)):
                        pool.iota(ids[:], pattern=[[step, ids.shape[1]]], base=0, channel_multiplier=mult,
                                  allow_small_or_imprecise_dtypes=True).then_inc(consts_set, 1)
                    pool.wait_ge(ident_zero, 1)
                    pool.affine_select(out=ident[:], in_=ident[:], compare_op=ALU.not_equal, fill=1.0, base=0,
                                       pattern=[[-1, P]], channel_multiplier=1).then_inc(consts_set, 1)

                @block.tensor
                def _(pe):
                    pe.wait_ge(rows_set, 1)
                    pe.wait_ge(last_step_ready, 1)
                    pe.matmul(psA[0][:, 0:NSB], ones_row[:], last_step[:], start=True, stop=True).then_inc(last_step_spread, 1)

                @block.vector
                def _(dve):
                    dve.memset(pad_row[:, 0], 0).then_inc(pads_set, 1)
                    dve.memset(pad_row[:, 1], NT * P).then_inc(pads_set, 1)
                    dve.memset(ones_row[:], 1.0).then_inc(rows_set, 1)
                    dve.memset(eps_col[:], EPS)
                    dve.memset(acc[:, NT - 1], 0.0)
                    dve.memset(head_mask[:], 0.0).then_inc(mask_zero, 1)
                    dve.wait_ge(mask_zero, 1)
                    for j in range(P // HC):
                        dve.memset(head_mask[HC * j:HC * (j + 1), HC * j:HC * (j + 1)], 1.0 / N)
                    dve.wait_ge(loads_done, 16 * NLOADS)
                    for w in range(2):
                        if w:
                            dve.wait_ge(att_cols_ready, 1)
                        dve.tensor_tensor(att_prod[:], W_ext[:, :, 0:D], att_b[:, w].unsqueeze(1).broadcast_to([P, KT, D]),
                                          ALU.mult).then_inc(att_prod_ready, 1)
                        dve.wait_ge(att_prod_ready, w + 1)
                        for k in range(KT):
                            last = dve.tensor_reduce(W_ext[:, k, D + HEADS * w:D + HEADS * (w + 1)],
                                                     att_prod[:, k].rearrange("p (h c) -> p h c", h=HEADS), AX_X, ALU.add)
                        last.then_inc(att_cols_ready, 1)
                    dve.wait_ge(last_in, 16)
                    dve.tensor_scalar(last_tile[:], last_dst[:], P.bit_length() - 1, None,
                                      ALU.logical_shift_right).then_inc(last_tile_ready, 1)
                    dve.wait_ge(last_tile_ready, 1)
                    dve.wait_ge(consts_set, 4)
                    dve.scalar_tensor_tensor(out=last_step[:], in0=last_tile[:], scalar=float(NT - 1), in1=sb_ids[:],
                                             op0=ALU.min, op1=ALU.add).then_inc(last_step_ready, 1)
                    dve.wait_ge(last_step_spread, 1)
                    for c in range(NCH):
                        last = dve.tensor_scalar(below[:], psA[0][:, 0:NSB], node_ids[:, c:c + 1], 0.0, ALU.is_lt, ALU.add,
                                                 accum_out=sb_done[:, c:c + 1])
                        last.then_inc(sb_done_ready, 1)
                        dve.wait_ge(sb_done_ready, c + 1)
                    dve.tensor_tensor(tile_of[:], node_ids[:, 0:NCH], sb_done[:], ALU.subtract).then_inc(tile_of_ready, 1)
                    dve.tensor_copy(steps_i[:, 0], sb_done[:]).then_inc(steps_ready, 1)
                    dve.wait_ge(tile_of_ready, 1)
                    dve.tensor_scalar(steps_i[:, 1], tile_of[:], float(NT - 1), None, ALU.min).then_inc(steps_ready, 1)

        with phase() as (ph, sem):
            wkv_sum = sb("wkv_sum", [P, KT, MH, 2], c=ph)
            wkv_s = sb("wkv_s", [P, KT, 2 * D], c=ph)
            bkv_sum = sb("bkv_sum", [P, MH, 2], c=ph)
            bkv_b = sb("bkv_b", [P, 2 * D], c=ph)
            kvx = sb("kvx", [P, 2, 2 * D], c=ph)
            kvsq = sb("kvsq", [P, 2, 2 * D], c=ph)
            kvvar = sb("kvvar", [P, 2, 2 * MH], c=ph)
            kvstd = sb("kvstd", [P, 2, 2 * MH], c=ph)
            kvrstd = sb("kvrstd", [P, 2, 2 * MH], c=ph)
            kn = sb("kn", [P, 2, D], c=ph)
            kg = sb("kg", [P, 2, D], c=ph)
            kf = sb("kf", [P, 2, D], c=ph)
            vn = sb("vn", [P, 2, KT, P + 1], c=ph)
            base = sb("base1", [P, 2, D], c=ph)
            x_in = [sem("x_in0"), sem("x_in1")]
            xnT_out = [sem("xnT_out0"), sem("xnT_out1")]
            base_out = [sem("base_out0"), sem("base_out1")]
            table_out = sem("table_out")
            stats_ready, mv_ready, std_ready, rstd_ready, xn_ready = (sem(n) for n in ("stats_ready", "mv_ready", "std_ready", "rstd_ready", "xn_ready"))
            base_sum, base_ready, turned, xnT_ready = sem("base_sum"), sem("base_ready"), sem("turned"), sem("xnT_ready")
            h_done, h_copied, kv_done, kv_biased = sem("h_done"), sem("h_copied"), sem("kv_done"), sem("kv_biased")
            sums_zero = sem("sums_zero")
            w_summed, w_centred, kv_squared, kv_var_ready = sem("w_summed"), sem("w_centred"), sem("kv_squared"), sem("kv_var_ready")
            kv_std_ready, kv_rstd_ready, vn_ready, kn_ready, kg_ready, kf_ready, kv_used = (sem(n) for n in (
                "kv_std_ready", "kv_rstd_ready", "vn_ready", "kn_ready", "kg_ready", "kf_ready", "kv_used"))
            with nc.Block() as block:
                @block.sync
                def _(sp):
                    def load_x(i, q, rows):
                        sp.dma_start(xin[0:rows, q], x[node_rows(i, rows)]).then_inc(x_in[q], 16)

                    def tile(i, q, rows, it):
                        sp.wait_ge(base_ready, i + 1)
                        if not (isinstance(i, int) and i + 2 > FULL):
                            load_x(i + 2, q, TAIL if isinstance(i, int) and i + 2 == FULL else P)
                        sp.dma_start(base_dram[node_rows(i, rows)], base[0:rows, q]).then_inc(base_out[q], 16)
                        sp.wait_ge(xnT_ready, i + 1)
                        sp.dma_start(xnT_dram[bass.ds(i, 1), :, :, 0:rows].rearrange("o p k n -> p (o k) n"),
                                     xnT[:, q, :, 0:rows]).then_inc(xnT_out[q], 16)
                        sp.wait_ge(h_copied, i + 1)
                        sp.dma_start(node_table[node_rows(i, P)].unsqueeze(1), acc[:, bass.ds(i, 1)]).then_inc(table_out, 16)

                    for i in range(2):
                        load_x(i, i, P)
                    each_tile(sp, tile)
                    sp.wait_ge(table_out, 16 * NT)
                    for q in range(2):
                        sp.wait_ge(xnT_out[q], 16 * (NT // 2 + (1 - q)))
                        sp.wait_ge(base_out[q], 16 * (NT // 2 + (1 - q)))

                @block.vector
                def _(dve):
                    def moments(i, q, rows, it):
                        dve.wait_ge(x_in[q], it * 16 + 16)
                        dve.bn_stats(stats[0:rows, q], xin[0:rows, q]).then_inc(stats_ready, 1)

                    def mean_variance(i, q, rows, it):
                        dve.wait_ge(stats_ready, i + 1)
                        dve.sem_inc(dve_gate, 1)
                        dve.bn_aggr(mv[0:rows, q], stats[0:rows, q]).then_inc(mv_ready, 1)

                    def inverse_deviation(i, q, rows, it):
                        dve.wait_ge(std_ready, i + 1)
                        dve.reciprocal(rstd[0:rows, q], std[0:rows, q]).then_inc(rstd_ready, 1)

                    def normalised(i, q, rows, it):
                        if later(i, 2):
                            dve.wait_ge(turned, i - 1)
                            dve.wait_ge(base_ready, i - 1)
                        dve.wait_ge(rstd_ready, i + 1)
                        dve.tensor_scalar(xn[0:rows, q], xin[0:rows, q], mv[0:rows, q, 0:1], rstd[0:rows, q],
                                          ALU.subtract, ALU.mult).then_inc(xn_ready, 1)

                    def node_row(i, q, rows, it):
                        dve.wait_ge(h_done, i + 1)
                        dve.tensor_scalar(acc[0:rows, bass.ds(i, 1)], psB[q][0:rows, 0:HW_].unsqueeze(1), 1.0, None,
                                          ALU.mult).then_inc(h_copied, 1)

                    def kv_bias(i, q, rows, it):
                        dve.wait_ge(kv_done, i + 1)
                        if later(i, 2):
                            dve.wait_ge(kv_squared, i - 1)
                        dve.tensor_tensor(kvx[0:rows, q], psC[q][0:rows, :], bkv_b[0:rows], ALU.add).then_inc(kv_biased, 1)

                    def kv_squares_sum(i, q, rows, it):
                        dve.wait_ge(kv_squared, i + 1)
                        dve.tensor_reduce(kvvar[0:rows, q], kvsq[0:rows, q].rearrange("p (g c) -> p g c", g=2 * MH), AX_X,
                                          ALU.add).then_inc(kv_var_ready, 1)

                    def kv_inverse_deviation(i, q, rows, it):
                        dve.wait_ge(kv_std_ready, i + 1)
                        dve.reciprocal(kvrstd[0:rows, q], kvstd[0:rows, q]).then_inc(kv_rstd_ready, 1)

                    def kv_normalised(i, q, rows, it):
                        dve.wait_ge(kv_rstd_ready, i + 1)
                        xs = kvx[0:rows, q].rearrange("p (h s c) -> p h s c", h=MH, s=2)
                        rs = kvrstd[0:rows, q].rearrange("p (h s) -> p h s", s=2)
                        wide = lambda s_: rs[:, :, s_].unsqueeze(2).broadcast_to([rows, MH, HC])
                        if later(i, 2):
                            dve.wait_ge(kg_ready, i - 1)
                        dve.tensor_tensor(kn[0:rows, q].rearrange("p (h c) -> p h c", h=MH), xs[:, :, 0], wide(0), ALU.mult).then_inc(kn_ready, 1)
                        if later(i, 2):
                            dve.wait_ge(kv_used, i - 1)
                        for hf in range(KT):
                            hs = slice(hf * MH // KT, (hf + 1) * MH // KT)
                            last = dve.tensor_tensor(vn[0:rows, q, hf, 0:P].rearrange("p (h c) -> p h c", c=HC),
                                                     xs[:, hs, 1], wide(1)[:, hs], ALU.mult)
                        last.then_inc(vn_ready, 1)

                    def tile(i, q, rows, it):
                        def norm(step):
                            if has_next(i):
                                step(*next_tile(i, q, it))

                        def kv(step):
                            if later(i, 1):
                                step(i - 1, 1 - q, P, it)

                        norm(moments)
                        kv(kv_bias)
                        norm(mean_variance)
                        node_row(i, q, rows, it)
                        norm(inverse_deviation)
                        norm(normalised)
                        kv(kv_squares_sum)
                        kv(kv_inverse_deviation)
                        kv(kv_normalised)

                    dve.memset(vn[:, :, :, P:P + 1], 1.0)
                    for hf in range(KT):
                        dve.memset(psD[hf][:, 0:P + 1], 0.0).then_inc(sums_zero, 1)
                    kv_cols = lambda t: t.rearrange("p (h s c) -> p h s c", h=MH, s=3)[:, :, 1:3]
                    parts = [(kv_cols(wqkv_s[:, k]), wkv_sum[:, k], wkv_s[:, k]) for k in range(KT)] + [(kv_cols(bqkv_b[:]), bkv_sum[:], bkv_b[:])]
                    for cols, total, _ in parts:
                        dve.tensor_reduce(total, cols, AX_X, ALU.add).then_inc(w_summed, 1)
                    for n, (cols, total, to) in enumerate(parts):
                        dve.wait_ge(w_summed, n + 1)
                        dve.scalar_tensor_tensor(out=to.rearrange("p (h s c) -> p h s c", h=MH, s=2),
                                                 in0=total.unsqueeze(3).broadcast_to([P, MH, 2, HC]), scalar=-1.0 / HC, in1=cols,
                                                 op0=ALU.mult, op1=ALU.add).then_inc(w_centred, 1)
                    dve.wait_ge(w_centred, KT + 1)
                    for step in (moments, mean_variance, inverse_deviation, normalised):
                        step(0, 0, P, 0)
                    each_tile(dve, tile)
                    for step in (kv_bias, kv_squares_sum, kv_inverse_deviation, kv_normalised):
                        step(FULL, 0, TAIL, FULL // 2)

                @block.gpsimd
                def _(pool):
                    def base_sums(i, q, rows, it):
                        pool.wait_ge(xn_ready, i + 1)
                        if later(i, 2):
                            pool.wait_ge(base_out[q], it * 16)
                        pool.tensor_tensor(base[0:rows, q], xin[0:rows, q], xn[0:rows, q], ALU.add).then_inc(base_sum, 1)
                        pool.wait_ge(base_sum, i + 1)
                        pool.tensor_tensor(base[0:rows, q], base[0:rows, q], b2_b[0:rows], ALU.add).then_inc(base_ready, 1)

                    def keys(i, q, rows):
                        per_head = lambda t: t[0:rows].unsqueeze(1).broadcast_to([rows, MH, HC])
                        heads = lambda t: t[0:rows, q].rearrange("p (h c) -> p h c", h=MH)
                        pool.wait_ge(kn_ready, i + 1)
                        pool.tensor_tensor(heads(kg), heads(kn), per_head(ln_g[:, 0]), ALU.mult).then_inc(kg_ready, 1)
                        pool.wait_ge(kg_ready, i + 1)
                        if later(i, 2):
                            pool.wait_ge(kv_used, i - 1)
                        pool.tensor_tensor(heads(kf), heads(kg), per_head(ln_b[:, 0]), ALU.add).then_inc(kf_ready, 1)

                    def tile(i, q, rows, it):
                        if has_next(i):
                            base_sums(*next_tile(i, q, it))
                        keys(i, q, rows)

                    base_sums(0, 0, P, 0)
                    each_tile(pool, tile)

                @block.scalar
                def _(act):
                    def root(i, q, rows, it):
                        act.wait_ge(mv_ready, i + 1)
                        act.activation(std[0:rows, q], mv[0:rows, q, 1:2], ACT.Sqrt, bias=eps_col[0:rows]).then_inc(std_ready, 1)

                    def turn(i, q, rows, it):
                        act.wait_ge(turned, i + 1)
                        if later(i, 2):
                            act.wait_ge(xnT_out[q], it * 16)
                            act.wait_ge(kv_done, i - 1)
                        act.activation(xnT[:, q, :, 0:rows], psA[q][:, 0:KT * P].rearrange("p (k n) -> p k n", k=KT)[:, :, 0:rows],
                                       ACT.Copy).then_inc(xnT_ready, 1)

                    def kv_squares(i, q, rows):
                        act.wait_ge(kv_biased, i + 1)
                        act.activation(kvsq[0:rows, q], kvx[0:rows, q], ACT.Square).then_inc(kv_squared, 1)

                    def kv_root(i, q, rows):
                        act.wait_ge(kv_var_ready, i + 1)
                        act.activation(kvstd[0:rows, q], kvvar[0:rows, q], ACT.Sqrt, bias=eps_col[0:rows],
                                       scale=1.0 / HC).then_inc(kv_std_ready, 1)

                    def tile(i, q, rows, it):
                        if has_next(i):
                            root(*next_tile(i, q, it))
                        if later(i, 1):
                            kv_squares(i - 1, 1 - q, P)
                        if later(i, 1):
                            kv_root(i - 1, 1 - q, P)
                        if has_next(i):
                            turn(*next_tile(i, q, it))

                    root(0, 0, P, 0)
                    turn(0, 0, P, 0)
                    each_tile(act, tile)
                    kv_squares(FULL, 0, TAIL)
                    kv_root(FULL, 0, TAIL)

                @block.tensor
                def _(pe):
                    def key_value_product(i, q, rows):
                        pe.wait_ge(kf_ready, i + 1)
                        pe.wait_ge(vn_ready, i + 1)
                        for hf in range(KT):
                            last = pe.matmul(psD[hf][:, 0:P + 1], kf[0:rows, q, hf * P:(hf + 1) * P], vn[0:rows, q, hf],
                                             start=False, stop=isinstance(i, int) and i == FULL, skip_group_check=True)
                        last.then_inc(kv_used, 1)

                    def turn(i, q, rows, it):
                        pe.wait_ge(xn_ready, i + 1)
                        if later(i, 2):
                            pe.wait_ge(xnT_ready, i - 1)
                        for k in range(KT):
                            last = pe.transpose(psA[q][:, k * P:k * P + rows], xn[0:rows, q, k * P:(k + 1) * P],
                                                ident[0:rows, 0:rows])
                        last.then_inc(turned, 1)

                    def tile(i, q, rows, it):
                        pe.wait_ge(xnT_ready, i + 1)
                        if later(i, 2):
                            pe.wait_ge(h_copied, i - 1)
                        for k in range(KT):
                            last = pe.matmul(psB[q][0:rows, 0:HW_], xnT[:, q, k, 0:rows], W_ext[:, k],
                                             start=(k == 0), stop=(k == KT - 1))
                        last.then_inc(h_done, 1)
                        if later(i, 2):
                            pe.wait_ge(kv_biased, i - 1)
                        for k in range(KT):
                            last = pe.matmul(psC[q][0:rows, :], xnT[:, q, k, 0:rows], wkv_s[:, k], start=(k == 0), stop=(k == KT - 1))
                        last.then_inc(kv_done, 1)
                        if has_next(i):
                            turn(*next_tile(i, q, it))
                        if later(i, 2):
                            key_value_product(i - 2, q, P)

                    turn(0, 0, P, 0)
                    pe.wait_ge(w_centred, KT + 1)
                    pe.wait_ge(sums_zero, KT)
                    each_tile(pe, tile)
                    key_value_product(FULL - 1, 1, P)
                    key_value_product(FULL, 0, TAIL)

        with phase() as (ph, sem):
            wq_c = sb("wq_c", [P, KT, D], c=ph)
            bq_c = sb("bq_c", [1, D], c=ph)
            wqT = sb("wqT", [P, KT, D], c=ph)
            kvm = sb("kvm", [P, KT, P], c=ph)
            k_total = sb("k_total", [P, KT], c=ph)
            kv_g = sb("kv_g", [P, KT, P], c=ph)
            kv_gb = sb("kv_gb", [P, KT, P], c=ph)
            k_total_ready, kv_gb_ready = sem("k_total_ready"), sem("kv_gb_ready")
            bq_col = sb("bq_col", [P, KT], c=ph)
            qkvT = sb("qkvT", [P, KT, D], c=ph)
            bq_kv = sb("bq_kv", [P, KT, P], c=ph)
            za = sb("za", [P, NT, HEADS], c=ph)
            zl = sb("zl", [P, NT, HEADS], c=ph)
            p_self = sb("p_self", [P, NT, HEADS], c=ph)
            wq_ready, wq_turned, wqT_ready, kvm_ready = sem("wq_ready"), sem("wq_turned"), sem("wqT_ready"), sem("kvm_ready")
            bq_turned, bq_col_ready, qkv_done, qkvT_ready = sem("bq_turned"), sem("bq_col_ready"), sem("qkv_done"), sem("qkvT_ready")
            weff_done, beff_done, bq_kv_done, bq_kv_ready, folded = (sem(n) for n in ("weff_done", "beff_done", "bq_kv_done", "bq_kv_ready", "folded"))
            smax_ready, smax_spread, adm_part, self_part, p_self_ready = (sem(n) for n in ("smax_ready", "smax_spread", "adm_part", "self_part", "p_self_ready"))
            order_in, smin_ready, falls_ready, span_ready, over_ready, any_ready = (sem(n) for n in (
                "order_in", "smin_ready", "falls_ready", "span_ready", "over_ready", "any_ready"))
            EL = (NSB + 1) * SB // P
            POOL_TILES = NT // 3
            dst_here = sb("dst_here", [P, EL], I32, c=ph)
            dst_next = sb("dst_next", [P, EL], I32, c=ph)
            falls = sb("falls", [P, EL], c=ph)
            smin = sb("smin", [P, HEADS], c=ph)
            span = sb("span", [1, HEADS], c=ph)
            over = sb("over", [1, 2 * HEADS + 1], c=ph)
            any_over = sb("any_over", [1, 1], c=ph)
            with nc.Block() as block:
                @block.sync
                def _(sp):
                    sp.dma_start(dst_here[:], edge_dst.rearrange("(p l) -> p l", p=P)).then_inc(order_in, 16)
                    sp.dma_start(dst_next[:], edge_dst_1[1:].rearrange("(p l) -> p l", p=P)).then_inc(order_in, 16)

                @block.gpsimd
                def _(pool):
                    pool.wait_ge(smax_ready, 3)
                    pool.partition_all_reduce(smax_all[:], smax[:], P, bass.bass_isa.ReduceOp.max).then_inc(smax_spread, 1)
                    pool.wait_ge(p_self_ready, 1)
                    for t in range(POOL_TILES):
                        self_loop_product(pool, t, p_self)

                @block.scalar
                def _(act):
                    act.wait_ge(self_part, 3)
                    act.activation(p_self[:], za[:], ACT.Exp).then_inc(p_self_ready, 1)

                @block.tensor
                def _(pe):
                    pe.wait_ge(wq_ready, 2)
                    for hf in range(KT):
                        for k in range(KT):
                            last = pe.transpose(psA[hf][:, k * P:(k + 1) * P], wq_c[:, k, hf * P:(hf + 1) * P], ident[:])
                    last.then_inc(wq_turned, 1)
                    for hf in range(KT):
                        last = pe.matmul(psC[0][:, hf:hf + 1], bq_c[:, hf * P:(hf + 1) * P], ones_row[:, 0:1], start=True, stop=True)
                    last.then_inc(bq_turned, 1)
                    pe.wait_ge(wqT_ready, 2)
                    pe.wait_ge(kvm_ready, 2)
                    for hf in range(KT):
                        last = pe.matmul(psB[hf][:, 0:D], kvm[:, hf], wqT[:, hf], start=True, stop=True)
                    last.then_inc(qkv_done, 1)
                    pe.wait_ge(bq_col_ready, 1)
                    for hf in range(KT):
                        last = pe.matmul(psC[1][:, hf:hf + 1], kvm[:, hf], bq_col[:, hf:hf + 1], start=True, stop=True)
                    last.then_inc(bq_kv_done, 1)
                    pe.wait_ge(qkvT_ready, 2)
                    for c in range(KT):
                        for hf in range(KT):
                            last = pe.matmul(psA[c][:, 0:D], qkvT[:, hf, c * P:(c + 1) * P], w1_s[:, hf], start=(hf == 0), stop=(hf == KT - 1))
                    last.then_inc(weff_done, 1)
                    pe.wait_ge(bq_kv_ready, 2)
                    for hf in range(KT):
                        last = pe.matmul(psC[0][:, 0:D], bq_kv[:, hf], w1_s[:, hf], start=(hf == 0), stop=(hf == KT - 1))
                    last.then_inc(beff_done, 1)

                @block.vector
                def _(dve):
                    dve.tensor_copy(wq_c[:].rearrange("p k (h c) -> p k h c", h=MH),
                                    wqkv_s[:].rearrange("p k (h c) -> p k h c", h=MH)[:, :, :, 0:HC]).then_inc(wq_ready, 1)
                    dve.tensor_copy(bq_c[:].rearrange("p (h c) -> p h c", h=MH),
                                    bqkv_b[0:1].rearrange("p (h c) -> p h c", h=MH)[:, :, 0:HC]).then_inc(wq_ready, 1)
                    a_src = acc[:, :, D:D + HEADS].rearrange("p t h -> p h t")
                    dve.tensor_reduce(smax[:, 0:HEADS], a_src, AX_X, ALU.max).then_inc(smax_ready, 1)
                    dve.tensor_reduce(smin[:], a_src, AX_X, ALU.min).then_inc(smin_ready, 1)
                    dve.wait_ge(smin_ready, 1)
                    dve.tensor_scalar(smax[:, HEADS:2 * HEADS], smin[:], -1.0, None, ALU.mult).then_inc(smax_ready, 1)
                    dve.wait_ge(order_in, 32)
                    dve.tensor_tensor(falls[:], dst_next[:], dst_here[:], ALU.is_lt).then_inc(falls_ready, 1)
                    dve.wait_ge(falls_ready, 1)
                    dve.tensor_reduce(smax[:, 2 * HEADS:], falls[:], AX_X, ALU.max).then_inc(smax_ready, 1)
                    row = lambda t: t[:, 1].unsqueeze(1).broadcast_to([P, P // HC, HC])
                    per_head = lambda t: t.rearrange("p (h c) -> p h c", c=HC)
                    for hf in range(KT):
                        dve.tensor_copy(k_total[:, hf:hf + 1], psD[hf][:, P:P + 1]).then_inc(k_total_ready, 1)
                        dve.tensor_tensor(per_head(kv_g[:, hf]), per_head(psD[hf][:, 0:P]), row(ln_g), ALU.mult).then_inc(k_total_ready, 1)
                        dve.wait_ge(k_total_ready, 2 * hf + 2)
                        dve.scalar_tensor_tensor(out=per_head(kv_gb[:, hf]), in0=row(ln_b), scalar=k_total[:, hf:hf + 1],
                                                 in1=per_head(kv_g[:, hf]), op0=ALU.mult, op1=ALU.add).then_inc(kv_gb_ready, 1)
                        dve.wait_ge(kv_gb_ready, hf + 1)
                        dve.tensor_tensor(kvm[:, hf], kv_gb[:, hf], head_mask[:], ALU.mult).then_inc(kvm_ready, 1)
                    dve.wait_ge(wq_turned, 1)
                    for hf in range(KT):
                        dve.tensor_copy(wqT[:, hf], psA[hf][:, 0:D]).then_inc(wqT_ready, 1)
                    dve.wait_ge(bq_turned, 1)
                    dve.tensor_copy(bq_col[:], psC[0][:, 0:KT]).then_inc(bq_col_ready, 1)
                    dve.wait_ge(qkv_done, 1)
                    for hf in range(KT):
                        dve.tensor_copy(qkvT[:, hf], psB[hf][:, 0:D]).then_inc(qkvT_ready, 1)
                    dve.wait_ge(bq_kv_done, 1)
                    for hf in range(KT):
                        dve.tensor_copy(bq_kv[:, hf], psC[1][:, hf:hf + 1].broadcast_to([P, P])).then_inc(bq_kv_ready, 1)
                    dve.wait_ge(weff_done, 1)
                    for c in range(KT):
                        dve.tensor_tensor(weff[:, c], psA[c][:, 0:D], w1_s[:, c], ALU.add).then_inc(folded, 1)
                    dve.wait_ge(beff_done, 1)
                    dve.tensor_tensor(beff[:], psC[0][:, 0:D], b1_b[:], ALU.add).then_inc(folded, 1)
                    dve.wait_ge(smax_spread, 1)
                    dve.tensor_tensor(span[:, 0:HEADS], smax_all[0:1, 0:HEADS], smax_all[0:1, HEADS:2 * HEADS], ALU.add).then_inc(span_ready, 1)
                    dve.wait_ge(span_ready, 1)
                    dve.tensor_scalar(over[:, 0:HEADS], span[:], MAX_SPAN, None, ALU.is_gt).then_inc(over_ready, 1)
                    dve.tensor_scalar(over[:, HEADS:2 * HEADS], smax_all[0:1, 0:HEADS], MAX_TOP, None, ALU.is_gt).then_inc(over_ready, 1)
                    dve.tensor_copy(over[:, 2 * HEADS:], smax_all[0:1, 2 * HEADS:]).then_inc(over_ready, 1)
                    dve.wait_ge(over_ready, 3)
                    dve.tensor_reduce(any_over[:], over[:], AX_X, ALU.max).then_inc(any_ready, 1)
                    dve.wait_ge(any_ready, 1)
                    dve.tensor_copy(general[:], any_over[:])
                    maxima_and_self_loops(dve, smax_all[:, 0:HEADS].unsqueeze(1).broadcast_to([P, NT, HEADS]), za, zl, p_self,
                                          adm_part, self_part, p_self_ready, first=POOL_TILES)

        with phase() as (ph, sem):
            iota_all = sb("iota_all", [P, NT * P], c=ph)
            iota_set = sem("iota_set")
            ps_sum, ps_turn = psB, psC
            src_idx = sb("src_idx", [P, RING, GB], I32, c=ph)
            dst_col = sb("dst_col", [P, RING, GB], I32, c=ph)
            rows_g = sb("rows_g", [P, RING, GB, HW_], c=ph)
            pick_e = sb("pick_e", [P, RING, GB, P], c=ph)
            pick_n = sb("pick_n", [P, 2, SB], c=ph)
            ze = sb("ze", [P, 2, GB, HEADS], c=ph)
            zle = sb("zle", [P, 2, GB, HEADS], c=ph)
            ye = sb("ye", [P, 2, GB, HEADS], c=ph)
            pe_h = sb("pe_h", [P, RING, GB, AW], c=ph)
            idx_in, dst_in, gathered = ([sem(f"{n}{r}") for r in range(RING)] for n in ("idx_in", "dst_in", "gathered"))
            pick_e_ready, pick_turned, pick_n_ready, picked, z_ready, zl_ready, y_ready, p_ready, ph_ready, summed, added = (sem(n) for n in (
                "pick_e_ready", "pick_turned", "pick_n_ready", "picked", "z_ready", "zl_ready", "y_ready", "p_ready", "ph_ready", "summed", "added"))
            base = sb("base2", [P, D], c=ph)
            mixed = sb("mixed2", [P, D], c=ph)
            hpre = sb("hpre", [P, D], c=ph)
            hid = sb("hid", [P, D], c=ph)
            hidT = sb("hidT", [P, KT, P], c=ph)
            m_xnT_in, m_base_in, m_out = sem("m_xnT_in"), sem("m_base_in"), sem("m_out")
            up_done, up_biased, gelu_done, hid_turned, hidT_ready, down_done, mixed_ready = (sem(n) for n in (
                "up_done", "up_biased", "gelu_done", "hid_turned", "hidT_ready", "down_done", "mixed_ready"))
            src_v = edge_src.rearrange("(b p j) -> b p j", p=P, j=GB)
            dst_v = edge_dst.rearrange("(b p j) -> b p j", p=P, j=GB)

            def each_step(eng, body, mix=None):
                def iteration(it, i=None, rows=P):
                    for u in range(STRIDE):
                        body(it * STRIDE + u, u % RING, it * (STRIDE // RING) + u // RING)
                        if mix and i is not None:
                            mix(u, i, rows)

                iteration(0, 0)
                with eng.Fori(1, FULL) as it:
                    iteration(it, it)
                iteration(FULL, FULL, TAIL)
                with eng.Fori(NT, NS // STRIDE - 1) as it:
                    iteration(it)
                iteration(NS // STRIDE - 1)

            def each_step_or_tile(eng, body, mix, before=None, after=None):
                with eng.If(general_value(eng) == 0):
                    if before:
                        before()
                    each_step(eng, body, mix)
                    if after:
                        after()
                with eng.If(general_value(eng) == 1):
                    def tile(i, q, rows, it):
                        for u in range(STRIDE):
                            mix(u, i, rows)
                    each_tile(eng, tile)

            def step_value(eng, w, s, top):
                return eng.value_load(steps_row[0:1, w, bass.ds(s, 1)], min_val=0, max_val=top)

            with nc.Block() as block:
                @block.sync
                def _(sp):
                    def step(s, r, it):
                        b = step_value(sp, 0, s, NSB)
                        if later(s, RING):
                            sp.wait_ge(gathered[r], it * (16 * GB))
                        sp.dma_start(src_idx[:, r].unsqueeze(1), src_v[bass.ds(b, 1)].rearrange("b p j -> p b j")).then_inc(idx_in[r], 16)
                        if later(s, RING):
                            sp.wait_ge(pick_e_ready, s - (RING - 1))
                        sp.dma_start(dst_col[:, r].unsqueeze(1), dst_v[bass.ds(b, 1)].rearrange("b p j -> p b j")).then_inc(dst_in[r], 16)

                    def mix(u, i, rows):
                        if u == 4:
                            if later(i, 1):
                                store(i - 1, P)
                            sp.dma_start(xnT[:, 0, :, 0:rows], xnT_dram[bass.ds(i, 1), :, :, 0:rows].rearrange("o p k n -> p (o k) n")
                                         ).then_inc(m_xnT_in, 16)
                            sp.dma_start(base[0:rows], base_dram[node_rows(i, rows)]).then_inc(m_base_in, 16)

                    def store(i, rows):
                        sp.wait_ge(mixed_ready, i + 1)
                        sp.dma_start(mixed_dram[node_rows(i, rows)], mixed[0:rows]).then_inc(m_out, 16)

                    each_step_or_tile(sp, step, mix)
                    store(FULL, TAIL)
                    sp.wait_ge(m_out, 16 * NT)

                @block.gpsimd
                def _(pool):
                    def step(s, r, it):
                        if later(s, RING):
                            pool.wait_ge(ph_ready, s - (RING - 1))
                        pool.wait_ge(idx_in[r], it * 16 + 16)
                        pool.sem_inc(pool_gate, 1)
                        for j in range(GB):
                            pool.indirect_dma_start(out=rows_g[:, r, j], out_offset=None, in_=node_table,
                                                    in_offset=bass.IndirectOffsetOnAxis(ap=src_idx[:, r, j:j + 1], axis=0)
                                                    ).then_inc(gathered[r], 16)

                    pool.iota(iota_all[:], pattern=[[1, NT * P]], base=0, channel_multiplier=0,
                              allow_small_or_imprecise_dtypes=True).then_inc(iota_set, 1)
                    with pool.If(general_value(pool) == 0):
                        each_step(pool, step)

                @block.vector
                def _(dve):
                    def picks(s, r, it):
                        t = step_value(dve, 1, s, NT - 1)
                        dve.wait_ge(dst_in[r], it * 16 + 16)
                        if later(s, RING):
                            dve.wait_ge(summed, s - (RING - 1))
                        dve.tensor_tensor(pick_e[:, r], iota_all[:, bass.ds(t * P, P)].unsqueeze(1).broadcast_to([P, GB, P]),
                                          dst_col[:, r].unsqueeze(2).broadcast_to([P, GB, P]), ALU.is_equal).then_inc(pick_e_ready, 1)

                    def logits(s, r, it):
                        q = r % 2
                        dve.wait_ge(picked, s + 1)
                        dve.wait_ge(gathered[r], it * (16 * GB) + 16 * GB)
                        sel = psA[q][:, 0:GB * 2 * HEADS].rearrange("p (j a) -> p j a", j=GB)
                        dve.tensor_tensor(ze[:, q], rows_g[:, r, :, D:D + HEADS], sel[:, :, 0:HEADS], ALU.add).then_inc(z_ready, 1)
                        dve.wait_ge(z_ready, s + 1)
                        dve.scalar_tensor_tensor(out=zle[:, q], in0=ze[:, q], scalar=SLOPE, in1=ze[:, q],
                                                 op0=ALU.mult, op1=ALU.max).then_inc(zl_ready, 1)
                        dve.wait_ge(zl_ready, s + 1)
                        dve.tensor_tensor(ye[:, q], zle[:, q], sel[:, :, HEADS:2 * HEADS], ALU.subtract).then_inc(y_ready, 1)

                    def products(s, r):
                        dve.wait_ge(p_ready, s + 1)
                        dve.tensor_tensor(pe_h[:, r, :, 0:D].rearrange("p j (h c) -> p j h c", h=HEADS),
                                          rows_g[:, r, :, 0:D].rearrange("p j (h c) -> p j h c", h=HEADS),
                                          pe_h[:, r, :, D:AW].unsqueeze(3).broadcast_to([P, GB, HEADS, C]),
                                          ALU.mult).then_inc(ph_ready, 1)

                    def add_up(s, r):
                        t = step_value(dve, 1, s, NT - 1)
                        dve.wait_ge(summed, s + 1)
                        if later(s, 1):
                            dve.wait_ge(added, s)
                        at = acc[:, bass.ds(t, 1), 0:AW]
                        dve.tensor_tensor(at, at, ps_sum[r % 2][:, 0:AW].unsqueeze(1), ALU.add).then_inc(added, 1)

                    def step(s, r, it):
                        last = isinstance(s, int) and s == NS - 1
                        if not (isinstance(s, int) and s >= NS - 2):
                            picks(s + 2, (r + 2) % RING, it + (r + 2) // RING)
                        if later(s, 2):
                            add_up(s - 2, (r - 2) % RING)
                        products(s, r)
                        if not last:
                            logits(s + 1, (r + 1) % RING, it + (r + 1) // RING)

                    def mix(u, i, rows):
                        if u == 3:
                            dve.wait_ge(up_done, i + 1)
                            if later(i, 1):
                                dve.wait_ge(gelu_done, i)
                            dve.tensor_tensor(hpre[0:rows], psD[0][0:rows, 0:D], beff[0:rows], ALU.add).then_inc(up_biased, 1)
                        if u == 7:
                            dve.wait_ge(down_done, i + 1)
                            dve.wait_ge(m_base_in, i * 16 + 16)
                            if later(i, 1):
                                dve.wait_ge(m_out, i * 16)
                            dve.tensor_tensor(mixed[0:rows], psD[0][0:rows, D:2 * D], base[0:rows], ALU.add).then_inc(mixed_ready, 1)

                    def before():
                        picks(0, 0, 0)
                        picks(1, 1, 0)
                        logits(0, 0, 0)

                    def after():
                        for s in (NS - 2, NS - 1):
                            add_up(s, s % RING)

                    dve.wait_ge(iota_set, 1)
                    each_step_or_tile(dve, step, mix, before, after)

                @block.scalar
                def _(act):
                    def pick_rows(s, r):
                        act.wait_ge(pick_turned, s + 1)
                        if later(s, 2):
                            act.wait_ge(picked, s - 1)
                        act.activation(pick_n[:, r % 2], ps_turn[r % 2][:, :], ACT.Copy).then_inc(pick_n_ready, 1)

                    def step(s, r, it):
                        q = r % 2
                        act.wait_ge(y_ready, s + 1)
                        if later(s, RING):
                            act.wait_ge(summed, s - (RING - 1))
                        act.activation(pe_h[:, r, :, D:AW], ye[:, q], ACT.Exp).then_inc(p_ready, 1)
                        if not (isinstance(s, int) and s >= NS - 2):
                            pick_rows(s + 2, (r + 2) % RING)

                    def mix(u, i, rows):
                        if u == 4:
                            act.wait_ge(up_biased, i + 1)
                            if later(i, 1):
                                act.wait_ge(hid_turned, i)
                            act.activation(hid[0:rows], hpre[0:rows], ACT.Gelu).then_inc(gelu_done, 1)
                        if u == 5:
                            act.wait_ge(hid_turned, i + 1)
                            if later(i, 1):
                                act.wait_ge(down_done, i)
                            act.activation(hidT[:, :, 0:rows], psD[1][:, 0:KT * P].rearrange("p (k n) -> p k n", k=KT)[:, :, 0:rows],
                                           ACT.Copy).then_inc(hidT_ready, 1)

                    def before():
                        pick_rows(0, 0)
                        pick_rows(1, 1)

                    each_step_or_tile(act, step, mix, before)

                @block.tensor
                def _(pe):
                    def turn_picks(s, r):
                        pe.wait_ge(pick_e_ready, s + 1)
                        if later(s, 2):
                            pe.wait_ge(pick_n_ready, s - 1)
                        for j in range(GB):
                            last = pe.transpose(ps_turn[r % 2][:, j * P:(j + 1) * P], pick_e[:, r, j], ident[:])
                        last.then_inc(pick_turned, 1)

                    def pick(s, r):
                        t = step_value(pe, 1, s, NT - 1)
                        q = r % 2
                        pe.wait_ge(pick_n_ready, s + 1)
                        if later(s, 2):
                            pe.wait_ge(y_ready, s - 1)
                        for j in range(GB):
                            last = pe.matmul(psA[q][:, j * 2 * HEADS:(j + 1) * 2 * HEADS],
                                             pick_n[:, q, j * P:(j + 1) * P], adm[:, bass.ds(t, 1)],
                                             start=True, stop=True)
                        last.then_inc(picked, 1)

                    def sums(s, r):
                        pe.wait_ge(ph_ready, s + 1)
                        if later(s, 2):
                            pe.wait_ge(added, s - 1)
                        for j in range(GB):
                            last = pe.matmul(ps_sum[r % 2][:, 0:AW], pick_e[:, r, j], pe_h[:, r, j], start=(j == 0), stop=(j == GB - 1))
                        last.then_inc(summed, 1)

                    def step(s, r, it):
                        if not (isinstance(s, int) and s == NS - 1):
                            pick(s + 1, (r + 1) % RING)
                        if not (isinstance(s, int) and s >= NS - 2):
                            turn_picks(s + 2, (r + 2) % RING)
                        sums(s, r)

                    def mix(u, i, rows):
                        if u == 2:
                            pe.wait_ge(m_xnT_in, i * 16 + 16)
                            if later(i, 1):
                                pe.wait_ge(up_biased, i)
                            for k in range(KT):
                                last = pe.matmul(psD[0][0:rows, 0:D], xnT[:, 0, k, 0:rows], weff[:, k], start=(k == 0), stop=(k == KT - 1))
                            last.then_inc(up_done, 1)
                        if u == 5:
                            pe.wait_ge(gelu_done, i + 1)
                            if later(i, 1):
                                pe.wait_ge(hidT_ready, i)
                            for k in range(KT):
                                last = pe.transpose(psD[1][:, k * P:k * P + rows], hid[0:rows, k * P:(k + 1) * P], ident[0:rows, 0:rows])
                            last.then_inc(hid_turned, 1)
                        if u == 6:
                            pe.wait_ge(hidT_ready, i + 1)
                            if later(i, 1):
                                pe.wait_ge(mixed_ready, i)
                            for k in range(KT):
                                last = pe.matmul(psD[0][0:rows, D:2 * D], hidT[:, k, 0:rows], w2_s[:, k], start=(k == 0), stop=(k == KT - 1))
                            last.then_inc(down_done, 1)

                    def before():
                        turn_picks(0, 0)
                        turn_picks(1, 1)
                        pick(0, 0)

                    each_step_or_tile(pe, step, mix, before)

        with phase() as (ph, sem):
            iota_all = sb("g_iota_all", [P, NT * P], c=ph)
            ones_sq = sb("g_ones_sq", [P, P], c=ph)
            src_idx = sb("g_src_idx", [P, GB], I32, c=ph)
            dst_col = sb("g_dst_col", [P, GB], I32, c=ph)
            dst_row = sb("g_dst_row", [P, SB], I32, c=ph)
            rows_g = sb("g_rows", [P, GB, HW_], c=ph)
            diag = sb("g_diag", [P, GB, HEADS, P], c=ph)
            a_row = sb("g_a_row", [P, HEADS, GB, P], c=ph)
            pick_n = sb("g_pick_n", [P, SB], c=ph)
            pick_e = sb("g_pick_e", [P, GB, P], c=ph)
            fence = sb("g_fence", [P, SB], c=ph)
            fenced = sb("g_fenced", [P, HEADS, SB], c=ph)
            tile_top = sb("g_tile_top", [P, HEADS], c=ph)
            node_top = sb("g_node_top", [P, NT, HEADS], c=ph)
            za = sb("g_za", [P, NT, HEADS], c=ph)
            zl = sb("g_zl", [P, NT, HEADS], c=ph)
            p_self = sb("g_p_self", [P, NT, HEADS], c=ph)
            ze = sb("g_ze", [P, GB, HEADS], c=ph)
            zle = sb("g_zle", [P, GB, HEADS], c=ph)
            yd = sb("g_yd", [P, GB, HEADS], c=ph)
            ye = sb("g_ye", [P, GB, HEADS], c=ph)
            pe_h = sb("g_pe_h", [P, GB, AW], c=ph)
            g = {n: sem("g_" + n) for n in (
                "iota_set acc_in ones_set top_set idx_in col_in row_in gathered_max gathered_sum diag_ready spread_done a_row_ready "
                "max_pick fence_ready fenced_ready tile_top_ready node_top_ready max_free adm_part self_part p_self_ready "
                "pick_n_ready pick_e_ready picked z_ready zl_ready yd_ready y_ready p_ready ph_ready summed added sum_free").split()}
            banks = [psB[0], psB[1], psC[0], psC[1]]

            with nc.Block() as block:
                @block.sync
                def _(sp):
                    with sp.If(general_value(sp) == 1):
                        sp.dma_start(acc[:], node_table.rearrange("(t p) c -> p t c", p=P)).then_inc(g["acc_in"], 16)
                        with sp.Fori(0, NSB) as b:
                            sp.wait_ge(g["max_free"], b + 1)
                            sp.dma_start(src_idx[:].unsqueeze(1), src_v[bass.ds(b, 1)].rearrange("b p j -> p b j")).then_inc(g["idx_in"], 16)
                            sp.dma_start(dst_row[:], edge_dst[bass.ds(b * SB, SB)].partition_broadcast(P)).then_inc(g["row_in"], 16)
                        with sp.Fori(0, NSB) as b:
                            sp.wait_ge(g["max_free"], NSB + 1)
                            sp.wait_ge(g["sum_free"], b + 1)
                            sp.dma_start(src_idx[:].unsqueeze(1), src_v[bass.ds(b, 1)].rearrange("b p j -> p b j")).then_inc(g["idx_in"], 16)
                            sp.dma_start(dst_col[:].unsqueeze(1), dst_v[bass.ds(b, 1)].rearrange("b p j -> p b j")).then_inc(g["col_in"], 16)
                            sp.dma_start(dst_row[:], edge_dst[bass.ds(b * SB, SB)].partition_broadcast(P)).then_inc(g["row_in"], 16)

                @block.gpsimd
                def _(pool):
                    with pool.If(general_value(pool) == 1):
                        pool.iota(iota_all[:], pattern=[[1, NT * P]], base=0, channel_multiplier=0,
                                  allow_small_or_imprecise_dtypes=True).then_inc(g["iota_set"], 1)
                        for first, gathered in ((0, g["gathered_max"]), (NSB, g["gathered_sum"])):
                            with pool.Fori(0, NSB) as b:
                                pool.wait_ge(g["idx_in"], (b + first) * 16 + 16)
                                pool.sem_inc(pool_gate, 1)
                                for j in range(GB):
                                    pool.indirect_dma_start(out=rows_g[:, j], out_offset=None, in_=node_table,
                                                            in_offset=bass.IndirectOffsetOnAxis(ap=src_idx[:, j:j + 1], axis=0)
                                                            ).then_inc(gathered, 16)

                @block.tensor
                def _(pe):
                    with pe.If(general_value(pe) == 1):
                        with pe.Fori(0, NSB) as b:
                            pe.wait_ge(g["ones_set"], 1)
                            pe.wait_ge(g["diag_ready"], b * GB + GB)
                            for j in range(GB):
                                last = pe.matmul(banks[j][:, :], ones_sq[:], diag[:, j].rearrange("p h e -> p (h e)"), start=True, stop=True)
                            last.then_inc(g["spread_done"], 1)
                        with pe.Fori(0, NSB) as b:
                            with pe.Fori(0, NT) as t:
                                n = b * NT + t
                                pe.wait_ge(g["pick_n_ready"], n + 1)
                                for j in range(GB):
                                    last = pe.matmul(psA[0][:, j * 2 * HEADS:(j + 1) * 2 * HEADS],
                                                     pick_n[:].rearrange("p (e j) -> p e j", j=GB)[:, :, j], adm[:, bass.ds(t, 1)],
                                                     start=True, stop=True)
                                last.then_inc(g["picked"], 1)
                                pe.wait_ge(g["pick_e_ready"], n + 1)
                                pe.wait_ge(g["ph_ready"], n + 1)
                                for j in range(GB):
                                    last = pe.matmul(psB[0][:, 0:AW], pick_e[:, j], pe_h[:, j], start=(j == 0), stop=(j == GB - 1))
                                last.then_inc(g["summed"], 1)

                @block.scalar
                def _(act):
                    with act.If(general_value(act) == 1):
                        act.wait_ge(g["self_part"], 3)
                        act.activation(p_self[:], za[:], ACT.Exp).then_inc(g["p_self_ready"], 1)
                        with act.Fori(0, NSB) as b:
                            with act.Fori(0, NT) as t:
                                act.wait_ge(g["y_ready"], b * NT + t + 1)
                                act.activation(pe_h[:, :, D:AW], ye[:], ACT.Exp).then_inc(g["p_ready"], 1)

                @block.vector
                def _(dve):
                    def largest(b, t):
                        n = b * NT + t
                        dve.tensor_scalar(pick_n[:].rearrange("p (j e) -> p j e", j=GB), dst_row[:].rearrange("p (e j) -> p j e", j=GB),
                                          node_ids[:, bass.ds(t, 1)], None, ALU.is_equal).then_inc(g["max_pick"], 1)
                        dve.wait_ge(g["max_pick"], n + 1)
                        dve.tensor_scalar(fence[:], pick_n[:], 1.0, 1e30, ALU.subtract, ALU.mult).then_inc(g["fence_ready"], 1)
                        dve.wait_ge(g["fence_ready"], n + 1)
                        dve.tensor_tensor(fenced[:], a_row[:].rearrange("p h j e -> p h (j e)"),
                                          fence[:].unsqueeze(1).broadcast_to([P, HEADS, SB]), ALU.add).then_inc(g["fenced_ready"], 1)
                        dve.wait_ge(g["fenced_ready"], n + 1)
                        dve.tensor_reduce(tile_top[:], fenced[:], AX_X, ALU.max).then_inc(g["tile_top_ready"], 1)
                        dve.wait_ge(g["tile_top_ready"], n + 1)
                        at = node_top[:, bass.ds(t, 1)]
                        dve.tensor_tensor(at, at, tile_top[:].unsqueeze(1), ALU.max).then_inc(g["node_top_ready"], 1)
                        dve.wait_ge(g["node_top_ready"], n + 1)

                    def add_edges(b, t):
                        n = b * NT + t
                        dve.tensor_scalar(pick_n[:], dst_row[:], node_ids[:, bass.ds(t, 1)], None, ALU.is_equal).then_inc(g["pick_n_ready"], 1)
                        dve.tensor_tensor(pick_e[:], iota_all[:, bass.ds(t * P, P)].unsqueeze(1).broadcast_to([P, GB, P]),
                                          dst_col[:].unsqueeze(2).broadcast_to([P, GB, P]), ALU.is_equal).then_inc(g["pick_e_ready"], 1)
                        sel = psA[0][:, 0:GB * 2 * HEADS].rearrange("p (j a) -> p j a", j=GB)
                        dve.wait_ge(g["picked"], n + 1)
                        dve.tensor_tensor(ze[:], rows_g[:, :, D:D + HEADS], sel[:, :, 0:HEADS], ALU.add).then_inc(g["z_ready"], 1)
                        dve.wait_ge(g["z_ready"], n + 1)
                        dve.scalar_tensor_tensor(out=zle[:], in0=ze[:], scalar=SLOPE, in1=ze[:],
                                                 op0=ALU.mult, op1=ALU.max).then_inc(g["zl_ready"], 1)
                        dve.wait_ge(g["zl_ready"], n + 1)
                        dve.tensor_tensor(yd[:], zle[:], sel[:, :, HEADS:2 * HEADS], ALU.subtract).then_inc(g["yd_ready"], 1)
                        dve.wait_ge(g["yd_ready"], n + 1)
                        dve.tensor_scalar(ye[:], yd[:], 0.0, None, ALU.min).then_inc(g["y_ready"], 1)
                        dve.wait_ge(g["p_ready"], n + 1)
                        dve.tensor_tensor(pe_h[:, :, 0:D].rearrange("p j (h c) -> p j h c", h=HEADS),
                                          rows_g[:, :, 0:D].rearrange("p j (h c) -> p j h c", h=HEADS),
                                          pe_h[:, :, D:AW].unsqueeze(3).broadcast_to([P, GB, HEADS, C]), ALU.mult).then_inc(g["ph_ready"], 1)
                        dve.wait_ge(g["summed"], n + 1)
                        at = acc[:, bass.ds(t, 1), 0:AW]
                        dve.tensor_tensor(at, at, psB[0][:, 0:AW].unsqueeze(1), ALU.add).then_inc(g["added"], 1)
                        dve.wait_ge(g["added"], n + 1)

                    with dve.If(general_value(dve) == 1):
                        dve.sem_inc(g["max_free"], 1)
                        dve.sem_inc(g["sum_free"], 1)
                        dve.memset(ones_sq[:], 1.0).then_inc(g["ones_set"], 1)
                        dve.wait_ge(g["acc_in"], 16)
                        dve.tensor_copy(node_top[:], acc[:, :, D:D + HEADS]).then_inc(g["top_set"], 1)
                        dve.wait_ge(g["top_set"], 1)
                        dve.sem_inc(dve_gate, 1)
                        with dve.Fori(0, NSB) as b:
                            dve.wait_ge(g["gathered_max"], b * (16 * GB) + 16 * GB)
                            for j in range(GB):
                                dve.tensor_tensor(diag[:, j], ident[:].unsqueeze(1).broadcast_to([P, HEADS, P]),
                                                  rows_g[:, j, D:D + HEADS].unsqueeze(2).broadcast_to([P, HEADS, P]),
                                                  ALU.mult).then_inc(g["diag_ready"], 1)
                            dve.wait_ge(g["spread_done"], b + 1)
                            for j in range(GB):
                                dve.tensor_copy(a_row[:, :, j], banks[j][:, :].rearrange("p (h e) -> p h e", h=HEADS)).then_inc(g["a_row_ready"], 1)
                            dve.wait_ge(g["a_row_ready"], b * GB + GB)
                            dve.wait_ge(g["row_in"], b * 16 + 16)
                            dve.sem_inc(dve_gate, 1)
                            with dve.Fori(0, NT) as t:
                                largest(b, t)
                            dve.sem_inc(g["max_free"], 1)
                        maxima_and_self_loops(dve, node_top[:], za, zl, p_self, g["adm_part"], g["self_part"], g["p_self_ready"])
                        dve.wait_ge(g["adm_part"], 4)
                        dve.wait_ge(g["iota_set"], 1)
                        dve.sem_inc(dve_gate, 1)
                        with dve.Fori(0, NSB) as b:
                            dve.wait_ge(g["gathered_sum"], b * (16 * GB) + 16 * GB)
                            dve.wait_ge(g["col_in"], b * 16 + 16)
                            dve.wait_ge(g["row_in"], (b + NSB) * 16 + 16)
                            dve.sem_inc(dve_gate, 1)
                            with dve.Fori(0, NT) as t:
                                add_edges(b, t)
                            dve.sem_inc(g["sum_free"], 1)

        W1_s = sb("W1_s", [P, NE, KT, H])
        W2_s = sb("W2_s", [P, NE, HK, D])
        fb1_b = sb("fb1_b", [P, NE, H])
        fb2_b = sb("fb2_b", [P, NE, D])

        with phase() as (ph, sem):
            after = sb("after", [P, P], c=ph)
            ones_sq = sb("ones_sq", [P, P], c=ph)
            den = sb("den", [P, 2, HEADS], c=ph)
            rden = sb("rden", [P, 2, HEADS], c=ph)
            gat = sb("gat", [P, 2, D], c=ph)
            gat_b = sb("gat_b", [P, 2, D], c=ph)
            xa, xb = xin, xn
            xc = sb("xc", [P, 2, D], c=ph)
            xd = sb("xd", [P, 2, D], c=ph)
            logit = sb("logit", [P, 2, NE], c=ph)
            top = sb("top", [P, 2, 8], c=ph)
            top_at = sb("top_at", [P, 2, 8], U32, c=ph)
            top_f = sb("top_f", [P, 2, 2], c=ph)
            gaps = sb("gaps", [P, NT], c=ph)
            ex = sb("ex", [P, NT], c=ph)
            ex1 = sb("ex1", [P, NT], c=ph)
            ex_ready = sem("f_ex_ready")
            chosen = sb("chosen", [P, 2, 2, NE], c=ph)
            both = sb("both", [P, 2, NE], c=ph)
            place = sb("place", [P, 2, NE], c=ph)
            hit = sb("hit", [P, 2, 2, NE], c=ph)
            place_f = sb("place_f", [P, 2, 2], c=ph)
            mix_slot = sb("mix_slot", [P, 2, D], c=ph)
            zero_rows = sb("zero_rows", [P, D], c=ph)
            fill_at = sb("fill_at", [P, NE], I32, c=ph)
            fill_f = sb("fill_f", [P, NE], c=ph)
            nblk_i = sb("nblk_i", [P, 2, NE], I32, c=ph)
            nblk_f = sb("nblk_f", [P, NE], c=ph)
            blk_end = sb("blk_end", [P, NE], c=ph)
            blk_gone = sb("blk_gone", [P, 2, NE], c=ph)
            blk_e = sb("blk_e", [P, 1], c=ph)
            moved = sb("moved", [P, NE], c=ph)
            moved2 = sb("moved2", [P, NE], c=ph)
            shift = sb("shift", [P, NT, 2], c=ph)
            blk_e7 = sb("blk_e7", [P, 1], c=ph)
            blk_before = sb("blk_before", [P, 1], c=ph)
            blk_j = sb("blk_j", [P, 1], c=ph)
            blk_i = sb("blk_i", [P, 2], I32, c=ph)
            f_in = [sem("f_in0"), sem("f_in1")]
            sent = [sem("sent0"), sem("sent1")]
            names = ("den_ready rden_ready gat_ready gat_biased x1_ready turned xT_ready logits_done logit_ready "
                     "top_ready top_at_ready top_f_ready gap_ready chosen_ready both_ready "
                     "xa_ready xb_ready xc_ready xd_ready counted place_ready hit_ready place_f_ready place_i_ready seen_ready").split()
            f = {n: sem("f_" + n) for n in names}
            f_set, f_tri, totals_done, blk_chain, blk_ready, fill_ready, fills_out, empty_out, blk_out, blk_in = (
                sem("f_" + n) for n in "set tri totals_done blk_chain blk_ready fill_ready fills_out empty_out blk_out blk_in".split())
            ln_stats, ln_mv, ln_std, ln_rstd = ([sem(f"f_{n}{k}") for k in range(2)] for n in ("stats", "mv", "std", "rstd"))
            with nc.Block() as block:
                @block.sync
                def _(sp):
                    def load(i, q, rows):
                        if later(i, 2):
                            sp.wait_ge(f["x1_ready"], i - 1)
                        sp.dma_start(mix_slot[0:rows, q], mixed_dram[node_rows(i, rows)]).then_inc(f_in[q], 16)

                    def tile(i, q, rows, it):
                        if isinstance(i, int) and i + 2 > FULL:
                            return
                        load(i + 2, q, TAIL if isinstance(i, int) and i + 2 == FULL else P)

                    for i in range(2):
                        load(i, i, P)
                    each_tile(sp, tile)
                    sp.wait_ge(f_set, 4)
                    for b in range(SPARE):
                        sp.dma_start(sent_dram[NE * REGION + b * P:NE * REGION + (b + 1) * P], zero_rows[:]).then_inc(empty_out, 16)
                    sp.wait_ge(blk_ready, 2)
                    for w in range(2):
                        sp.dma_start(block_table[w].unsqueeze(1), blk_i[:, w:w + 1],
                                     allow_slow_non_contiguous=True).then_inc(blk_out, 16)
                    sp.wait_ge(blk_out, 32)
                    sp.dma_start(blocks_row[:], block_table.unsqueeze(0)).then_inc(blk_in, 16)
                    sp.wait_ge(blk_in, 16)
                    sp.wait_ge(fills_out, 16 * NE)
                    sp.wait_ge(empty_out, 16 * SPARE)

                @block.vector
                def _(dve):
                    def x1_of(i, rows):
                        return acc[0:rows, bass.ds(i, 1), 0:D].rearrange("p o c -> p (o c)")

                    def denominators(i, q, rows, it):
                        dve.tensor_scalar(den[0:rows, q].unsqueeze(1), acc[0:rows, bass.ds(i, 1), D:AW], 1e-16, None,
                                          ALU.add).then_inc(f["den_ready"], 1)

                    def inverses(i, q, rows, it):
                        dve.wait_ge(f["den_ready"], i + 1)
                        dve.reciprocal(rden[0:rows, q], den[0:rows, q]).then_inc(f["rden_ready"], 1)

                    def attention(i, q, rows, it):
                        dve.wait_ge(f["rden_ready"], i + 1)
                        dve.tensor_tensor(gat[0:rows, q].rearrange("p (o h c) -> p (o h) c", o=1, h=HEADS),
                                          acc[0:rows, bass.ds(i, 1), 0:D].rearrange("p o (h c) -> p (o h) c", h=HEADS),
                                          rden[0:rows, q].unsqueeze(2).broadcast_to([rows, HEADS, C]), ALU.mult).then_inc(f["gat_ready"], 1)

                    def attention_bias(i, q, rows, it):
                        dve.wait_ge(f["gat_ready"], i + 1)
                        dve.tensor_tensor(gat_b[0:rows, q], gat[0:rows, q], gnn_bias_b[0:rows], ALU.add).then_inc(f["gat_biased"], 1)

                    def first_sum(i, q, rows, it):
                        dve.wait_ge(f["gat_biased"], i + 1)
                        dve.wait_ge(f_in[q], it * 16 + 16)
                        dve.scalar_tensor_tensor(out=x1_of(i, rows), in0=gat_b[0:rows, q], scalar=0.0, in1=mix_slot[0:rows, q],
                                                 op0=ALU.max, op1=ALU.add).then_inc(f["x1_ready"], 1)

                    def moments(k, from_, from_ready):
                        def step(i, q, rows, it):
                            dve.wait_ge(from_ready, i + 1)
                            dve.sem_inc(dve_gate, 1)
                            dve.bn_stats(stats[0:rows, q], from_(i, q, rows)).then_inc(ln_stats[k], 1)
                        return step

                    def mean_variance(k):
                        def step(i, q, rows, it):
                            dve.wait_ge(ln_stats[k], i + 1)
                            dve.sem_inc(dve_gate, 1)
                            dve.bn_aggr(mv[0:rows, q], stats[0:rows, q]).then_inc(ln_mv[k], 1)
                        return step

                    def inverse_deviation(k):
                        def step(i, q, rows, it):
                            dve.wait_ge(ln_std[k], i + 1)
                            dve.reciprocal(rstd[0:rows, q], std[0:rows, q]).then_inc(ln_rstd[k], 1)
                        return step

                    def normalised(k, from_, to, to_ready):
                        def step(i, q, rows, it):
                            dve.wait_ge(ln_rstd[k], i + 1)
                            dve.tensor_scalar(to[0:rows, q], from_(i, q, rows), mv[0:rows, q, 0:1], rstd[0:rows, q],
                                              ALU.subtract, ALU.mult).then_inc(to_ready, 1)
                        return step

                    def gamma_times(i, q, rows, it):
                        dve.wait_ge(f["xb_ready"], i + 1)
                        dve.tensor_tensor(xc[0:rows, q], xb[0:rows, q], gam_b[0:rows], ALU.mult).then_inc(f["xc_ready"], 1)

                    def beta_plus(i, q, rows, it):
                        dve.wait_ge(f["xc_ready"], i + 1)
                        if later(i, 2):
                            dve.wait_ge(f["turned"], i - 1)
                            dve.wait_ge(sent[q], it * 32)
                        dve.tensor_tensor(xd[0:rows, q], xc[0:rows, q], bet_b[0:rows], ALU.add).then_inc(f["xd_ready"], 1)

                    first_from = lambda i, q, rows: x1_of(i, rows)
                    second_from = lambda i, q, rows: xa[0:rows, q]
                    moments_1, mean_1, inverse_1 = moments(0, first_from, f["x1_ready"]), mean_variance(0), inverse_deviation(0)
                    norm_1 = normalised(0, first_from, xa, f["xa_ready"])
                    moments_2, mean_2, inverse_2 = moments(1, second_from, f["xa_ready"]), mean_variance(1), inverse_deviation(1)
                    norm_2 = normalised(1, second_from, xb, f["xb_ready"])

                    def logits_bias(i, q, rows, it):
                        dve.wait_ge(f["logits_done"], i + 1)
                        dve.tensor_tensor(logit[0:rows, q], psD[q][0:rows, 0:NE], br_b[0:rows], ALU.add).then_inc(f["logit_ready"], 1)

                    def largest_two(i, q, rows, it):
                        dve.wait_ge(f["logit_ready"], i + 1)
                        dve.sem_inc(dve_gate, 1)
                        dve.max(top[0:rows, q], logit[0:rows, q]).then_inc(f["top_ready"], 1)

                    def their_experts(i, q, rows, it):
                        dve.wait_ge(f["top_ready"], i + 1)
                        dve.sem_inc(dve_gate, 1)
                        dve.max_index(top_at[0:rows, q], top[0:rows, q], logit[0:rows, q]).then_inc(f["top_at_ready"], 1)
                        dve.tensor_tensor(gaps[0:rows, bass.ds(i, 1)], top[0:rows, q, 1:2], top[0:rows, q, 0:1],
                                          ALU.subtract).then_inc(f["gap_ready"], 1)

                    def as_numbers(i, q, rows, it):
                        dve.wait_ge(f["top_at_ready"], i + 1)
                        dve.tensor_scalar(top_f[0:rows, q], top_at[0:rows, q, 0:2], 0.0, None, ALU.add).then_inc(f["top_f_ready"], 1)

                    def one_hot(i, q, rows, it):
                        dve.wait_ge(f["top_f_ready"], i + 1)
                        dve.tensor_tensor(chosen[0:rows, q], iota8[0:rows].unsqueeze(1).broadcast_to([rows, 2, NE]),
                                          top_f[0:rows, q].unsqueeze(2).broadcast_to([rows, 2, NE]), ALU.is_equal).then_inc(f["chosen_ready"], 1)

                    def both_choices(i, q, rows, it):
                        dve.wait_ge(f["chosen_ready"], i + 1)
                        dve.tensor_tensor(both[0:rows, q], chosen[0:rows, q, 0], chosen[0:rows, q, 1], ALU.add).then_inc(f["both_ready"], 1)

                    def expert_places(i, q, rows, it):
                        dve.wait_ge(f["counted"], i + 1)
                        dve.tensor_tensor(place[0:rows, q], psD[q][0:rows, 16:16 + NE], region[0:rows], ALU.add).then_inc(f["place_ready"], 1)
                        dve.tensor_tensor(seen[0:rows], seen[0:rows], both[0:rows, q], ALU.add).then_inc(f["seen_ready"], 1)

                    def chosen_places(i, q, rows, it):
                        dve.wait_ge(f["place_ready"], i + 1)
                        dve.tensor_tensor(hit[0:rows, q], chosen[0:rows, q], place[0:rows, q].unsqueeze(1).broadcast_to([rows, 2, NE]),
                                          ALU.mult).then_inc(f["hit_ready"], 1)

                    def two_places(i, q, rows, it):
                        dve.wait_ge(f["hit_ready"], i + 1)
                        dve.tensor_reduce(place_f[0:rows, q], hit[0:rows, q], AX_X, ALU.add).then_inc(f["place_f_ready"], 1)

                    def keep_places(i, q, rows, it):
                        dve.wait_ge(f["place_f_ready"], i + 1)
                        if later(i, 2):
                            dve.wait_ge(sent[q], it * 32)
                        dve.tensor_scalar(place_s[0:rows, q], place_f[0:rows, q], 1.0, None, ALU.mult).then_inc(f["place_i_ready"], 1)
                        dve.tensor_scalar(places_f[0:rows, bass.ds(i, 1)], place_f[0:rows, q].unsqueeze(1), 1.0, None, ALU.mult)
                        dve.tensor_scalar(choices[0:rows, bass.ds(i, 1)].rearrange("p o c e -> p o (c e)"),
                                          chosen[0:rows, q].rearrange("p c e -> p (c e)").unsqueeze(1), 1.0, None, ALU.mult)

                    def tile(i, q, rows, it):
                        def front(step):
                            if has_next(i):
                                step(*next_tile(i, q, it))

                        def route(step):
                            step(i, q, rows, it)

                        def last_route(step):
                            if later(i, 1):
                                step(i - 1, 1 - q, P, it - (1 - q))

                        front(denominators)
                        last_route(chosen_places)
                        front(inverses)
                        last_route(two_places)
                        front(attention)
                        last_route(keep_places)
                        front(attention_bias)
                        front(first_sum)
                        front(moments_1)
                        route(logits_bias)
                        front(mean_1)
                        route(largest_two)
                        front(inverse_1)
                        route(their_experts)
                        front(norm_1)
                        route(as_numbers)
                        front(moments_2)
                        route(one_hot)
                        front(mean_2)
                        route(both_choices)
                        front(inverse_2)
                        front(norm_2)
                        front(gamma_times)
                        route(expert_places)
                        front(beta_plus)

                    dve.memset(places_f[:], 0.0)
                    dve.memset(gaps[:], 0.0)
                    dve.memset(choices[:], 0.0)
                    dve.memset(seen[:], 0.0).then_inc(f_set, 1)
                    dve.memset(ones_sq[:], 1.0).then_inc(f_set, 1)
                    dve.memset(zero_rows[:], 0.0).then_inc(f_set, 1)
                    dve.wait_ge(f_tri, 2)
                    dve.tensor_scalar(region[:], iota8[:], float(REGION), None, ALU.mult).then_inc(f_set, 1)
                    dve.wait_ge(f_set, 4)
                    for step in (denominators, inverses, attention, attention_bias, first_sum, moments_1, mean_1, inverse_1, norm_1,
                                 moments_2, mean_2, inverse_2, norm_2, gamma_times, beta_plus):
                        step(0, 0, P, 0)
                    each_tile(dve, tile)
                    for step in (chosen_places, two_places, keep_places):
                        step(FULL, 0, TAIL, FULL // 2)

                    step = [0]

                    def then(ins):
                        step[0] += 1
                        ins.then_inc(blk_chain, 1)
                        dve.wait_ge(blk_chain, step[0])

                    dve.wait_ge(totals_done, 1)
                    then(dve.tensor_tensor(fill_f[:], psA[0][:, 0:NE], region[:], ALU.add))
                    dve.tensor_scalar(fill_at[:], fill_f[:], node_ids[:, 0:1], None, ALU.add).then_inc(fill_ready, 1)
                    then(dve.tensor_scalar(nblk_i[:, 0], psA[0][:, 0:NE], float(P - 1), None, ALU.add))
                    then(dve.tensor_scalar(nblk_i[:, 1], nblk_i[:, 0], P.bit_length() - 1, None, ALU.logical_shift_right))
                    then(dve.tensor_copy(nblk_f[:], nblk_i[:, 1]))
                    then(dve.tensor_tensor_scan(blk_end[:], nblk_f[:], nblk_f[:], 0.0, ALU.add, ALU.bypass))
                    then(dve.tensor_scalar(blk_gone[:, 0], blk_end[:], node_ids[:, 0:1], 0.0, ALU.is_le, ALU.add, accum_out=blk_e[:]))
                    then(dve.tensor_tensor(blk_gone[:, 1], blk_gone[:, 0], nblk_f[:], ALU.mult))
                    then(dve.tensor_reduce(blk_before[:], blk_gone[:, 1], AX_X, ALU.add))
                    then(dve.tensor_tensor(blk_j[:], node_ids[:, 0:1], blk_before[:], ALU.subtract))
                    then(dve.tensor_scalar(blk_e7[:], blk_e[:], float(REGION // P), None, ALU.mult))
                    dve.tensor_tensor(blk_i[:, 0:1], blk_e7[:], blk_j[:], ALU.add).then_inc(blk_ready, 1)
                    dve.tensor_scalar(blk_i[:, 1:2], blk_e[:], float(NE - 1), None, ALU.min).then_inc(blk_ready, 1)
                    then(dve.tensor_tensor(moved[:], blk_end[:], nblk_f[:], ALU.subtract))
                    then(dve.scalar_tensor_tensor(out=moved2[:], in0=moved[:], scalar=float(P), in1=region[:],
                                                  op0=ALU.mult, op1=ALU.subtract))
                    then(dve.tensor_tensor(choices[:].rearrange("p t c e -> p (t c) e"), choices[:].rearrange("p t c e -> p (t c) e"),
                                           moved2[:].unsqueeze(1).broadcast_to([P, 2 * NT, NE]), ALU.mult))
                    then(dve.tensor_reduce(shift[:].rearrange("p t c -> p (t c)"), choices[:].rearrange("p t c e -> p (t c) e"), AX_X, ALU.add))
                    dve.tensor_tensor(places[:], places_f[:], shift[:], ALU.add)
                    dve.wait_ge(ex_ready, 1)
                    then(dve.tensor_scalar(ex1[:], ex[:], 1.0, None, ALU.add))
                    then(dve.reciprocal(share[:, :, 0], ex1[:]))
                    dve.tensor_tensor(share[:, :, 1], ex[:], share[:, :, 0], ALU.mult)

                @block.scalar
                def _(act):
                    def norm_and_turn(i, q, rows, it):
                        for k in range(2):
                            act.wait_ge(ln_mv[k], i + 1)
                            act.activation(std[0:rows, q], mv[0:rows, q, 1:2], ACT.Sqrt, bias=eps_col[0:rows]).then_inc(ln_std[k], 1)
                        act.wait_ge(f["turned"], i + 1)
                        if later(i, 2):
                            act.wait_ge(f["logits_done"], i - 1)
                        act.activation(xnT[:, q, :, 0:rows], psC[q][:, 0:KT * P].rearrange("p (k n) -> p k n", k=KT)[:, :, 0:rows],
                                       ACT.Copy).then_inc(f["xT_ready"], 1)

                    for to, frm in ((W1_s, W1.rearrange("e (k p) n -> p e k n", p=P)), (W2_s, W2.rearrange("e (k p) n -> p e k n", p=P)),
                                    (fb1_b, fb1.partition_broadcast(P)), (fb2_b, fb2.partition_broadcast(P))):
                        act.dma_start(to[:], frm).then_inc(weights_in, 16)

                    each_tile(act, norm_and_turn)
                    act.wait_ge(f["gap_ready"], NT)
                    act.activation(ex[:], gaps[:], ACT.Exp).then_inc(ex_ready, 1)

                @block.gpsimd
                def _(pool):
                    pool.memset(after[:], 1.0).then_inc(f_tri, 1)
                    pool.wait_ge(f_tri, 1)
                    pool.affine_select(out=after[:], in_=after[:], compare_op=ALU.is_gt, fill=0.0, base=0,
                                       pattern=[[1, P]], channel_multiplier=-1).then_inc(f_tri, 1)

                    def tile(i, q, rows, it):
                        pool.wait_ge(f["place_i_ready"], i + 1)
                        pool.sem_inc(pool_gate, 1)
                        for c in range(2):
                            pool.indirect_dma_start(out=sent_dram, out_offset=bass.IndirectOffsetOnAxis(ap=place_s[0:rows, q, c:c + 1], axis=0),
                                                    in_=xd[0:rows, q], in_offset=None).then_inc(sent[q], 16)

                    each_tile(pool, tile)
                    pool.wait_ge(fill_ready, 1)
                    for q in range(2):
                        pool.wait_ge(sent[q], 32 * (NT // 2 + (1 - q)))
                    for e in range(NE):
                        pool.indirect_dma_start(out=sent_dram, out_offset=bass.IndirectOffsetOnAxis(ap=fill_at[:, e:e + 1], axis=0),
                                                in_=zero_rows[:], in_offset=None).then_inc(fills_out, 16)

                @block.tensor
                def _(pe):
                    def logits(i, q, rows, it):
                        pe.wait_ge(f["xd_ready"], i + 1)
                        if later(i, 2):
                            pe.wait_ge(f["xT_ready"], i - 1)
                        for k in range(KT):
                            last = pe.transpose(psC[q][:, k * P:k * P + rows], xd[0:rows, q, k * P:(k + 1) * P],
                                                ident[0:rows, 0:rows])
                        last.then_inc(f["turned"], 1)
                        pe.wait_ge(f["xT_ready"], i + 1)
                        if later(i, 2):
                            pe.wait_ge(f["place_ready"], i - 1)
                        for k in range(KT):
                            last = pe.matmul(psD[q][0:rows, 0:NE], xnT[:, q, k, 0:rows], wr_s[:, k], start=(k == 0), stop=(k == KT - 1))
                        last.then_inc(f["logits_done"], 1)

                    def tile(i, q, rows, it):
                        pe.wait_ge(f["both_ready"], i + 1)
                        if later(i, 1):
                            pe.wait_ge(f["seen_ready"], i)
                        pe.matmul(psD[q][0:rows, 16:16 + NE], after[0:rows, 0:rows], both[0:rows, q], start=True, stop=False)
                        pe.matmul(psD[q][0:rows, 16:16 + NE], ones_sq[:, 0:rows], seen[:], start=False, stop=True).then_inc(f["counted"], 1)
                        if has_next(i):
                            logits(*next_tile(i, q, it))

                    pe.wait_ge(f_set, 3)
                    pe.wait_ge(f_tri, 2)
                    logits(0, 0, P, 0)
                    each_tile(pe, tile)
                    pe.wait_ge(f["seen_ready"], NT)
                    pe.matmul(psA[0][:, 0:NE], ones_sq[:], seen[:], start=True, stop=True).then_inc(totals_done, 1)

        with phase() as (ph, sem):
            xe = sb("xe", [P, 2, D], c=ph)
            xeT = sb("xeT", [P, 2, KT, P], c=ph)
            hb = sb("hb", [P, 2, H], c=ph)
            hg = sb("hg", [P, 2, H], c=ph)
            hT = sb("hT", [P, 2, HK, P], c=ph)
            ys = sb("ys", [P, 2, D], c=ph)
            xe_in, ys_out = [sem("xe_in0"), sem("xe_in1")], [sem("ys_out0"), sem("ys_out1")]
            x_turned, xeT_ready, up_done5, hb_ready, hg_ready, h_turned, hT_ready, down_done5, ys_ready = (
                sem("e_" + n) for n in "x_turned xeT_ready up_done hb_ready hg_ready h_turned hT_ready down_done ys_ready".split())

            def each_block(eng, body):
                for k in range(2):
                    body(k, k, 0)
                with eng.Fori(1, NBLK // 2 - 1) as it:
                    for u in range(2):
                        body(it * 2 + u, u, it)
                for k in range(NBLK - 2, NBLK):
                    body(k, k % 2, k // 2)

            def block_value(eng, w, k, top_v):
                return eng.value_load(blocks_row[0:1, w, bass.ds(k, 1)], min_val=0, max_val=top_v)

            def ahead(k):
                return not (isinstance(k, int) and k == NBLK - 1)

            with nc.Block() as block:
                @block.sync
                def _(sp):
                    LASTB = NE * REGION // P + SPARE - 1

                    def load(k, u):
                        b = block_value(sp, 0, k, LASTB)
                        if later(k, 2):
                            sp.wait_ge(x_turned, k - 1)
                        sp.dma_start(xe[:, u], sent_dram[bass.ds(b * P, P)]).then_inc(xe_in[u], 16)

                    def store(k, u):
                        sp.wait_ge(ys_ready, k + 1)
                        sp.dma_start(done_dram[bass.ds(k * P, P)], ys[:, u]).then_inc(ys_out[u], 16)

                    def one(k, u, it):
                        if not (isinstance(k, int) and k + 2 >= NBLK):
                            load(k + 2, u)
                        if later(k, 1):
                            store(k - 1, 1 - u)

                    load(0, 0)
                    load(1, 1)
                    each_block(sp, one)
                    store(NBLK - 1, (NBLK - 1) % 2)
                    for u in range(2):
                        sp.wait_ge(ys_out[u], 16 * (NBLK // 2))

                @block.scalar
                def _(act):
                    def turn_x(k, u):
                        act.wait_ge(x_turned, k + 1)
                        if later(k, 2):
                            act.wait_ge(up_done5, k - 1)
                        act.activation(xeT[:, u], psD[u][:, 0:KT * P].rearrange("p (k n) -> p k n", k=KT), ACT.Copy).then_inc(xeT_ready, 1)

                    def gelu(k, u):
                        act.wait_ge(hb_ready, k + 1)
                        if later(k, 2):
                            act.wait_ge(h_turned, k - 1)
                        act.activation(hg[:, u], hb[:, u], ACT.Gelu).then_inc(hg_ready, 1)

                    def one(k, u, it):
                        act.wait_ge(h_turned, k + 1)
                        if later(k, 2):
                            act.wait_ge(down_done5, k - 1)
                        act.activation(hT[:, u], psB[u][:, :].rearrange("p (c n) -> p c n", c=HK), ACT.Copy).then_inc(hT_ready, 1)
                        if not (isinstance(k, int) and k + 2 >= NBLK):
                            turn_x(k + 2, u)
                        if ahead(k):
                            gelu(k + 1, 1 - u)

                    turn_x(0, 0)
                    turn_x(1, 1)
                    gelu(0, 0)
                    each_block(act, one)

                @block.vector
                def _(dve):
                    def hidden_bias(k, u, it):
                        e = block_value(dve, 1, k, NE - 1)
                        dve.wait_ge(up_done5, k + 1)
                        if later(k, 2):
                            dve.wait_ge(hg_ready, k - 1)
                        dve.tensor_tensor(hb[:, u].unsqueeze(1), psA[u][:, :].unsqueeze(1), fb1_b[:, bass.ds(e, 1)], ALU.add).then_inc(hb_ready, 1)

                    def result(k, u, it):
                        e = block_value(dve, 1, k, NE - 1)
                        dve.wait_ge(down_done5, k + 1)
                        if later(k, 2):
                            dve.wait_ge(ys_out[u], it * 16)
                        dve.tensor_tensor(ys[:, u].unsqueeze(1), psC[u][:, 0:D].unsqueeze(1), fb2_b[:, bass.ds(e, 1)], ALU.add).then_inc(ys_ready, 1)

                    def one(k, u, it):
                        if ahead(k):
                            hidden_bias(k + 1, 1 - u, it)
                        result(k, u, it)

                    dve.wait_ge(weights_in, 64)
                    hidden_bias(0, 0, 0)
                    each_block(dve, one)

                @block.tensor
                def _(pe):
                    def turn_x(k, u, it):
                        pe.wait_ge(xe_in[u], it * 16 + 16)
                        if later(k, 2):
                            pe.wait_ge(xeT_ready, k - 1)
                        for c in range(KT):
                            last = pe.transpose(psD[u][:, c * P:(c + 1) * P], xe[:, u, c * P:(c + 1) * P], ident[:])
                        last.then_inc(x_turned, 1)

                    def up(k, u, e):
                        pe.wait_ge(xeT_ready, k + 1)
                        if later(k, 2):
                            pe.wait_ge(hb_ready, k - 1)
                        for c in range(KT):
                            last = pe.matmul(psA[u][:, :], xeT[:, u, c], W1_s[:, bass.ds(e, 1), c], start=(c == 0), stop=(c == KT - 1))
                        last.then_inc(up_done5, 1)

                    def turn_h(k, u):
                        pe.wait_ge(hg_ready, k + 1)
                        if later(k, 2):
                            pe.wait_ge(hT_ready, k - 1)
                        for c in range(HK):
                            last = pe.transpose(psB[u][:, c * P:(c + 1) * P], hg[:, u, c * P:(c + 1) * P], ident[:])
                        last.then_inc(h_turned, 1)

                    def down(k, u, e):
                        pe.wait_ge(hT_ready, k + 1)
                        if later(k, 2):
                            pe.wait_ge(ys_ready, k - 1)
                        for c in range(HK):
                            last = pe.matmul(psC[u][:, 0:D], hT[:, u, c], W2_s[:, bass.ds(e, 1), c], start=(c == 0), stop=(c == HK - 1))
                        last.then_inc(down_done5, 1)

                    def one(k, u, it):
                        e = block_value(pe, 1, k, NE - 1)
                        e_next = block_value(pe, 1, k + 1, NE - 1) if ahead(k) else None
                        turn_h(k, u)
                        if not (isinstance(k, int) and k + 2 >= NBLK):
                            turn_x(k + 2, u, it + 1)
                        if ahead(k):
                            up(k + 1, 1 - u, e_next)
                        down(k, u, e)

                    turn_x(0, 0, 0)
                    turn_x(1, 1, 0)
                    pe.wait_ge(weights_in, 64)
                    up(0, 0, block_value(pe, 1, 0, NE - 1))
                    each_block(pe, one)

        with phase() as (ph, sem):
            picked_rows = sb("picked_rows", [P, 4, 2, D], c=ph)
            at_slot = sb("at_slot", [P, 4, 2], I32, c=ph)
            y_first = sb("y_first", [P, 4, D], c=ph)
            y_all = sb("y_all", [P, 4, D], c=ph)
            rows_in, y_out = [sem(f"g_rows_in{r}") for r in range(4)], [sem(f"g_y_out{r}") for r in range(4)]
            at_ready, first_ready, all_ready = sem("g_at_ready"), sem("g_first_ready"), sem("g_all_ready")
            QUADS = FULL // 4

            def each_quad(eng, body):
                for i in range(4):
                    body(i, i, P, 0)
                if QUADS > 2:
                    with eng.Fori(1, QUADS - 1) as it:
                        for r in range(4):
                            body(it * 4 + r, r, P, it)
                for i in range(max(QUADS - 1, 1) * 4, NT):
                    body(i, i % 4, P if i < FULL else TAIL, i // 4)

            with nc.Block() as block:
                @block.gpsimd
                def _(pool):
                    def tile(i, r, rows, it):
                        pool.wait_ge(at_ready, i + 1)
                        if later(i, 4):
                            pool.wait_ge(all_ready, i - 3)
                        pool.sem_inc(pool_gate, 1)
                        for c in range(2):
                            pool.indirect_dma_start(out=picked_rows[0:rows, r, c], out_offset=None, in_=done_dram,
                                                    in_offset=bass.IndirectOffsetOnAxis(ap=at_slot[0:rows, r, c:c + 1], axis=0)
                                                    ).then_inc(rows_in[r], 16)

                    each_quad(pool, tile)

                @block.vector
                def _(dve):
                    def row_numbers(i, r, rows, it):
                        if later(i, 4):
                            dve.wait_ge(rows_in[r], it * 32)
                        dve.tensor_scalar(at_slot[0:rows, r].unsqueeze(1), places[0:rows, bass.ds(i, 1)], 1.0, None, ALU.mult).then_inc(at_ready, 1)

                    def sums(i, r, rows, it):
                        x1 = acc[0:rows, bass.ds(i, 1), 0:D].rearrange("p o c -> p (o c)")
                        w = share[0:rows, bass.ds(i, 1)].rearrange("p o c -> p (o c)")
                        dve.wait_ge(rows_in[r], it * 32 + 32)
                        dve.scalar_tensor_tensor(out=y_first[0:rows, r], in0=picked_rows[0:rows, r, 0], scalar=w[:, 0:1], in1=x1,
                                                 op0=ALU.mult, op1=ALU.add).then_inc(first_ready, 1)
                        dve.wait_ge(first_ready, i + 1)
                        if later(i, 4):
                            dve.wait_ge(y_out[r], it * 16)
                        dve.scalar_tensor_tensor(out=y_all[0:rows, r], in0=picked_rows[0:rows, r, 1], scalar=w[:, 1:2],
                                                 in1=y_first[0:rows, r], op0=ALU.mult, op1=ALU.add).then_inc(all_ready, 1)

                    def tile(i, r, rows, it):
                        if not (isinstance(i, int) and i + 2 > FULL):
                            row_numbers(i + 2, (r + 2) % 4, TAIL if isinstance(i, int) and i + 2 == FULL else P, it + (r + 2) // 4)
                        sums(i, r, rows, it)

                    row_numbers(0, 0, P, 0)
                    row_numbers(1, 1, P, 0)
                    each_quad(dve, tile)

                @block.sync
                def _(sp):
                    def tile(i, r, rows, it):
                        sp.wait_ge(all_ready, i + 1)
                        sp.dma_start(out[node_rows(i, rows)], y_all[0:rows, r]).then_inc(y_out[r], 16)

                    each_quad(sp, tile)
                    for r in range(4):
                        sp.wait_ge(y_out[r], 16 * len(range(r, NT, 4)))


_INS = ['x', 'src', 'dst', 'L0_gnn_W', 'L0_gnn_att_src', 'L0_gnn_att_dst', 'L0_gnn_bias', 'L0_mix_w_qkv', 'L0_mix_b_qkv',
        'L0_mix_kln_g', 'L0_mix_kln_b', 'L0_mix_vln_g', 'L0_mix_vln_b', 'L0_mix_w1', 'L0_mix_b1', 'L0_mix_w2', 'L0_mix_b2',
        'L0_ffn_gamma', 'L0_ffn_beta', 'L0_ffn_Wr', 'L0_ffn_br', 'L0_ffn_W1', 'L0_ffn_b1', 'L0_ffn_W2', 'L0_ffn_b2']


def kernel(**inputs):
    import numpy as _np
    import concourse.bacc as _bacc
    from concourse import mybir as _mybir
    from concourse.bass_utils import run_bass_kernel_spmd as _run

    nc = _bacc.Bacc("TRN2", target_bir_lowering=False, num_devices=1)
    arrays, args = {}, []
    for name in _INS:
        a = _np.ascontiguousarray(inputs[name])
        arrays[f"in_{name}_dram"] = a
        args.append(nc.dram_tensor(f"in_{name}_dram", a.shape, _mybir.dt.from_np(a.dtype), kind="ExternalInput").ap())
    out = nc.dram_tensor("out_0_dram", inputs["x"].shape, F32, kind="ExternalOutput").ap()
    gps_layer(nc, *args, out)
    r = _run(nc, [arrays], core_ids=[0])
    return r.results[0]["out_0_dram"]
```
